# Optimizing a Trainium2 kernel written in Bass

```python
import numpy as np
import jax
import jax.numpy as jnp

def _softmax(x, axis=-1):
    return jax.nn.softmax(x, axis=axis)

def _gelu(x):
    return jax.nn.gelu(x, approximate=True)

def _silu(x):
    return jax.nn.silu(x)

def _sigmoid(x):
    return jax.nn.sigmoid(x)

def _layernorm(x, axis=-1, eps=1e-05):
    m = jnp.mean(x, axis=axis, keepdims=True)
    v = jnp.var(x, axis=axis, keepdims=True)
    return (x - m) / jnp.sqrt(v + eps)

def _scatter_add(tgt, idx, src, axis=0):
    return tgt.at[idx].add(src)

def _segment_sum(src, seg, n):
    return jax.ops.segment_sum(src, seg, n)
kernel_name = 'mk_adj_resnorm_d4_adj_r2_86e9fc'

def setup_inputs(seed: int=0):
    np.random.seed(seed)
    _w = jnp.asarray

    def _rec_inputs():
        import jax
        import jax.numpy as jnp
        _gk = jax.random.key(seed)
        x = 7.22e-05 + 1 * jax.random.normal(jax.random.fold_in(_gk, 1), (128, 64, 256), jnp.float32)
        _a = jax.random.bernoulli(jax.random.fold_in(_gk, 2), 0.0625, (128, 64, 64))
        _a = jnp.logical_or(_a, jnp.swapaxes(_a, -1, -2))
        _a = jnp.logical_or(_a, jnp.eye(64, dtype=bool))
        _af = _a.astype(jnp.float32)
        _af = _af * jax.random.uniform(jax.random.fold_in(_gk, 3), (128, 64, 64), jnp.float32, 0.05, 1)
        adj = _af
        _nm = jnp.ones((128, 64), dtype=bool)
        nodemask = jnp.where(_nm, 1.0, 0.0).astype(jnp.float32)
        return (x, adj, nodemask)
    x, adj, nodemask = _rec_inputs()

    def _L0_gnn_setup():
        import jax, jax.numpy as jnp
        import numpy as np
        EPS_LN = 1e-05

        def hypergraph_conv(x, adj, W, b):
            N, C, _ = adj.shape
            H = (adj != 0).astype(x.dtype)
            w = adj.reshape(N, -1)[:, :C]
            xw = jnp.einsum('ncd,hd->nch', x, W)
            Dn = jnp.einsum('nce,ne->nc', H, w)
            Dn = jnp.where(Dn > 0, 1.0 / Dn, 0.0)
            Be = H.sum(axis=1)
            Be = jnp.where(Be > 0, 1.0 / Be, 0.0)
            m = Be[:, :, None] * jnp.einsum('nce,nch->neh', H, xw)
            out = Dn[:, :, None] * jnp.einsum('nce,neh->nch', H, m)
            return out + b

        def layer_norm(x, g, b):
            mu = jnp.mean(x, axis=-1, keepdims=True)
            var = jnp.var(x, axis=-1, keepdims=True)
            return (x - mu) * jax.lax.rsqrt(var + EPS_LN) * g + b
        key = jax.random.key(seed)
        ks = jax.random.split(key, 4)
        N, C, Din, Dh, Dout = (16, 512, 256, 512, 256)
        x = jax.random.normal(ks[0], (N, C, Din), dtype=jnp.float32)
        adj = jax.random.uniform(ks[1], (N, C, C), dtype=jnp.float32, minval=0.1, maxval=1.0)
        W1 = jax.random.normal(ks[2], (Dh, Din), dtype=jnp.float32) * (1.0 / np.sqrt(Din))
        b1 = jnp.zeros((Dh,), dtype=jnp.float32)
        gamma = jnp.ones((Dh,), dtype=jnp.float32)
        beta = jnp.zeros((Dh,), dtype=jnp.float32)
        W2 = jax.random.normal(ks[3], (Dout, Dh), dtype=jnp.float32) * (1.0 / np.sqrt(Dh))
        b2 = jnp.zeros((Dout,), dtype=jnp.float32)
        return {'x': x, 'adj': adj, 'W1': W1, 'b1': b1, 'gamma': gamma, 'beta': beta, 'W2': W2, 'b2': b2}
    _L0_gnn_all = _L0_gnn_setup()
    _L0_gnn_in = {k: v for k, v in _L0_gnn_all.items() if k in ('W1', 'b1', 'gamma', 'beta', 'W2', 'b2')}
    del _L0_gnn_all

    def _L1_gnn_setup():
        import jax, jax.numpy as jnp
        import numpy as np
        B, N, IN_DIM, ATT_DIM = (2, 4096, 256, 256)
        key = jax.random.key(seed)
        k1, k2, k3, k4 = jax.random.split(key, 4)
        X = jax.random.normal(k1, (B, N, IN_DIM), dtype=jnp.float32)
        adj = jax.random.uniform(k2, (B, N, N), dtype=jnp.float32)
        mask = jnp.ones((B, N), dtype=jnp.float32)
        Wqk = jax.random.normal(k3, (IN_DIM, 2 * ATT_DIM), dtype=jnp.float32) / np.sqrt(IN_DIM)
        Wv = jax.random.normal(k4, (IN_DIM, IN_DIM), dtype=jnp.float32) / np.sqrt(IN_DIM)
        return {'X': X, 'adj': adj, 'mask': mask, 'Wqk': Wqk, 'Wv': Wv}
    _L1_gnn_all = _L1_gnn_setup()
    _L1_gnn_in = {k: v for k, v in _L1_gnn_all.items() if k in ('Wqk', 'Wv')}
    del _L1_gnn_all

    def _L2_gnn_setup():
        import jax, jax.numpy as jnp
        import numpy as np
        EMBED_DIM = 256
        NUM_HEADS = 8
        HEAD_DIM = EMBED_DIM // NUM_HEADS
        SCALE = HEAD_DIM ** (-0.5)
        B, S = (16, 512)
        key = jax.random.key(seed)
        ks = jax.random.split(key, 12)
        init = lambda k, shape: jax.random.normal(k, shape, dtype=jnp.float32) * EMBED_DIM ** (-0.5)
        return {'x': jax.random.normal(ks[0], (B, S, EMBED_DIM), dtype=jnp.float32), 'adj_matrix': jax.random.uniform(ks[1], (B, S, S), dtype=jnp.float32), 'bond_matrix': jax.random.uniform(ks[2], (B, S, S), dtype=jnp.float32), 'Wq': init(ks[3], (EMBED_DIM, EMBED_DIM)), 'bq': jnp.zeros((EMBED_DIM,), jnp.float32), 'Wk': init(ks[4], (EMBED_DIM, EMBED_DIM)), 'bk': jnp.zeros((EMBED_DIM,), jnp.float32), 'Wv': init(ks[5], (EMBED_DIM, EMBED_DIM)), 'bv': jnp.zeros((EMBED_DIM,), jnp.float32), 'Wo': init(ks[6], (EMBED_DIM, EMBED_DIM)), 'bo': jnp.zeros((EMBED_DIM,), jnp.float32), 'seq_len': S}
    _L2_gnn_all = _L2_gnn_setup()
    _L2_gnn_in = {k: v for k, v in _L2_gnn_all.items() if k in ('Wq', 'bq', 'Wk', 'bk', 'Wv', 'bv', 'Wo', 'bo')}
    del _L2_gnn_all

    def _L3_gnn_setup():
        import math
        import jax, jax.numpy as jnp
        import numpy as np
        B, N, D = (8, 1024, 256)
        key = jax.random.key(seed)
        ks = jax.random.split(key, 9)
        s = 1.0 / math.sqrt(D)
        return {'x': jax.random.normal(ks[0], (B, N, D), dtype=jnp.float32), 'adj': jax.random.uniform(ks[1], (B, N, N), dtype=jnp.float32), 'Wqk': jax.random.normal(ks[2], (D, D), dtype=jnp.float32) * s, 'bqk': jax.random.normal(ks[3], (D,), dtype=jnp.float32) * s, 'Wl': jax.random.normal(ks[4], (D, D), dtype=jnp.float32) * s, 'bl': jax.random.normal(ks[5], (D,), dtype=jnp.float32) * s, 'Wr': jax.random.normal(ks[6], (D, D), dtype=jnp.float32) * s, 'Wd': jax.random.normal(ks[7], (D, 1), dtype=jnp.float32), 'bd': jax.random.normal(ks[8], (D,), dtype=jnp.float32)}
    _L3_gnn_all = _L3_gnn_setup()
    _L3_gnn_in = {k: v for k, v in _L3_gnn_all.items() if k in ('Wqk', 'bqk', 'Wl', 'bl', 'Wr', 'Wd', 'bd')}
    del _L3_gnn_all
    return {'x': x, 'adj': adj, 'nodemask': nodemask, 'L0_gnn_W1': _L0_gnn_in['W1'], 'L0_gnn_b1': _L0_gnn_in['b1'], 'L0_gnn_gamma': _L0_gnn_in['gamma'], 'L0_gnn_beta': _L0_gnn_in['beta'], 'L0_gnn_W2': _L0_gnn_in['W2'], 'L0_gnn_b2': _L0_gnn_in['b2'], 'L1_gnn_Wqk': _L1_gnn_in['Wqk'], 'L1_gnn_Wv': _L1_gnn_in['Wv'], 'L2_gnn_Wq': _L2_gnn_in['Wq'], 'L2_gnn_bq': _L2_gnn_in['bq'], 'L2_gnn_Wk': _L2_gnn_in['Wk'], 'L2_gnn_bk': _L2_gnn_in['bk'], 'L2_gnn_Wv': _L2_gnn_in['Wv'], 'L2_gnn_bv': _L2_gnn_in['bv'], 'L2_gnn_Wo': _L2_gnn_in['Wo'], 'L2_gnn_bo': _L2_gnn_in['bo'], 'L3_gnn_Wqk': _L3_gnn_in['Wqk'], 'L3_gnn_bqk': _L3_gnn_in['bqk'], 'L3_gnn_Wl': _L3_gnn_in['Wl'], 'L3_gnn_bl': _L3_gnn_in['bl'], 'L3_gnn_Wr': _L3_gnn_in['Wr'], 'L3_gnn_Wd': _L3_gnn_in['Wd'], 'L3_gnn_bd': _L3_gnn_in['bd']}

def reference(x, adj, nodemask, L0_gnn_W1, L0_gnn_b1, L0_gnn_gamma, L0_gnn_beta, L0_gnn_W2, L0_gnn_b2, L1_gnn_Wqk, L1_gnn_Wv, L2_gnn_Wq, L2_gnn_bq, L2_gnn_Wk, L2_gnn_bk, L2_gnn_Wv, L2_gnn_bv, L2_gnn_Wo, L2_gnn_bo, L3_gnn_Wqk, L3_gnn_bqk, L3_gnn_Wl, L3_gnn_bl, L3_gnn_Wr, L3_gnn_Wd, L3_gnn_bd):
    import jax
    import jax.numpy as jnp

    def _L0_gnn_ref(x, adj, W1, b1, gamma, beta, W2, b2):
        import jax, jax.numpy as jnp
        import numpy as np
        EPS_LN = 1e-05

        def hypergraph_conv(x, adj, W, b):
            N, C, _ = adj.shape
            H = (adj != 0).astype(x.dtype)
            w = adj.reshape(N, -1)[:, :C]
            xw = jnp.einsum('ncd,hd->nch', x, W)
            Dn = jnp.einsum('nce,ne->nc', H, w)
            Dn = jnp.where(Dn > 0, 1.0 / Dn, 0.0)
            Be = H.sum(axis=1)
            Be = jnp.where(Be > 0, 1.0 / Be, 0.0)
            m = Be[:, :, None] * jnp.einsum('nce,nch->neh', H, xw)
            out = Dn[:, :, None] * jnp.einsum('nce,neh->nch', H, m)
            return out + b

        def layer_norm(x, g, b):
            mu = jnp.mean(x, axis=-1, keepdims=True)
            var = jnp.var(x, axis=-1, keepdims=True)
            return (x - mu) * jax.lax.rsqrt(var + EPS_LN) * g + b
        h = jax.nn.relu(hypergraph_conv(x, adj, W1, b1))
        h = layer_norm(h, gamma, beta)
        y = hypergraph_conv(h, adj, W2, b2)
        return y + x

    def _L1_gnn_ref(X, adj, mask, Wqk, Wv):
        import jax, jax.numpy as jnp
        import numpy as np
        B, N, IN_DIM, ATT_DIM = (2, 4096, 256, 256)
        qk = X @ Wqk
        q, k = jnp.split(qk, 2, axis=-1)
        v = X @ Wv
        att_dim = q.shape[-1]
        inv_scale = 1.0 / jnp.sqrt(jnp.float32(att_dim))
        k_m = k * mask[:, :, None]
        agg = jnp.einsum('bij,bjd->bid', adj, k_m)
        w = inv_scale * mask * jnp.einsum('bid,bid->bi', q, agg)
        L = jax.nn.softmax(w, axis=1)[:, :, None] * v
        return L

    def _L2_gnn_ref(x, adj_matrix, bond_matrix, Wq, bq, Wk, bk, Wv, bv, Wo, bo, seq_len):
        import jax, jax.numpy as jnp
        import numpy as np
        EMBED_DIM = 256
        NUM_HEADS = 8
        HEAD_DIM = EMBED_DIM // NUM_HEADS
        SCALE = HEAD_DIM ** (-0.5)
        B, S = (16, 512)
        b = x.shape[0]

        def proj(W, bias):
            y = jnp.einsum('bse,fe->bsf', x, W) + bias
            return y.reshape(b, seq_len, NUM_HEADS, HEAD_DIM).transpose(0, 2, 1, 3)
        q, k, v = (proj(Wq, bq), proj(Wk, bk), proj(Wv, bv))
        scores = jnp.einsum('bhqd,bhkd->bhqk', q, k) * SCALE
        mask = (adj_matrix + bond_matrix)[:, None, :, :]
        scores = scores * mask
        attn = jax.nn.softmax(scores, axis=-1)
        ctx = jnp.einsum('bhqk,bhkd->bhqd', attn, v)
        ctx = ctx.transpose(0, 2, 1, 3).reshape(b, seq_len, EMBED_DIM)
        return jnp.einsum('bse,fe->bsf', ctx, Wo) + bo

    def _L3_gnn_ref(x, adj, Wqk, bqk, Wl, bl, Wr, Wd, bd):
        import math
        import jax, jax.numpy as jnp
        import numpy as np
        B, N, D = (8, 1024, 256)
        deg = jnp.sum(adj, axis=-1, keepdims=True)
        gate = jax.nn.sigmoid(deg * Wd[:, 0] + bd)
        xg = x * gate
        QK = jax.nn.sigmoid(xg @ Wqk.T + bqk)
        scores = jnp.einsum('bnd,bmd->bnm', QK, QK) / math.sqrt(D)
        scores = scores * adj
        attn = scores / (jnp.sum(scores, axis=-1, keepdims=True) + 1e-06)
        out = jnp.einsum('bnm,bmd->bnd', attn, xg)
        out = out @ Wl.T + bl + xg @ Wr.T
        return jax.nn.relu(out)
    x = _layernorm(x + _L0_gnn_ref(x, adj, L0_gnn_W1, L0_gnn_b1, L0_gnn_gamma, L0_gnn_beta, L0_gnn_W2, L0_gnn_b2), axis=-1)
    x = _layernorm(x + _L1_gnn_ref(x, adj, nodemask, L1_gnn_Wqk, L1_gnn_Wv), axis=-1)
    x = _layernorm(x + _L2_gnn_ref(x, adj, adj, L2_gnn_Wq, L2_gnn_bq, L2_gnn_Wk, L2_gnn_bk, L2_gnn_Wv, L2_gnn_bv, L2_gnn_Wo, L2_gnn_bo, 64), axis=-1)
    x = _layernorm(x + _L3_gnn_ref(x, adj, L3_gnn_Wqk, L3_gnn_bqk, L3_gnn_Wl, L3_gnn_bl, L3_gnn_Wr, L3_gnn_Wd, L3_gnn_bd), axis=-1)
    return x

_drawn_inputs = setup_inputs


def setup_inputs(seed=0):
    import zlib

    import numpy as np

    out = dict(_drawn_inputs(seed))
    spreads = {'L0_gnn_b1': (0.0, 0.1),
     'L0_gnn_gamma': (1.0, 0.2),
     'L0_gnn_beta': (0.0, 0.1),
     'L0_gnn_b2': (0.0, 0.1),
     'L2_gnn_bq': (0.0, 0.575),
     'L2_gnn_bk': (0.0, 0.765),
     'L2_gnn_bv': (0.0, 0.1),
     'L2_gnn_bo': (0.0, 0.1)}
    factors = {'L3_gnn_Wqk': 8.0, 'L3_gnn_bqk': 8.0}
    for name, (base, spread) in spreads.items():
        noise = np.random.default_rng([zlib.crc32(name.encode()), seed]).standard_normal(out[name].shape)
        drawn = base * np.exp(spread * noise) if base else spread * noise
        out[name] = jnp.asarray(drawn.astype(out[name].dtype))
    for name, factor in factors.items():
        out[name] = (out[name] * factor).astype(out[name].dtype)
    return out
```

```python
from contextlib import ExitStack

import concourse.bass as bass
from concourse import mybir

F32 = mybir.dt.float32
F16 = mybir.dt.float16
ALU = mybir.AluOpType
ACT = mybir.ActivationFunctionType
AX = mybir.AxisListType

P = 128
GRAPHS, NODES, D = 128, 64, 256
H1 = 512
TILES = 2
TOK = TILES * P
GROUPS = GRAPHS * NODES // TOK
HEADS, HD = 8, D // 8
WS = 64.0
EPS = 1e-5
SOFT1 = 1.0 / 16.0
SOFT2 = 2.0 * HD ** -0.5
QK3 = 0.25 / 16.0
TINY = 1e-37

LAG = {"A": 0, "B": 1, "C": 2, "D": 3, "F": 4, "G": 5}
LAST_LAG = 5
STEPS = GROUPS + LAST_LAG

BIAS = {"b1": (0, 512, WS), "b2": (512, 256, 1.0), "bq": (768, 256, WS), "bk": (1024, 256, WS),
        "bv": (1280, 256, WS), "bo": (1536, 256, WS), "bl": (1792, 256, WS), "bqk": (2048, 256, WS)}
BIAS_W = 2304


def build(nc, x, adj, adj_t, mask, mask_col, w1t, b1, gamma, beta, w2t, b2, wqk1t, wv1, wqt, bq, wkt, bk, wvt, bv,
          wot, bo, wqk3t, bqk, wlt, bl, wrt, wd, bd, out):
    ctx = ExitStack()
    with ctx:
        def sb(name, shape, dt=F32):
            return ctx.enter_context(nc.sbuf_tensor(name, shape, dt))

        sems = {}

        def ev(name):
            if name not in sems:
                sems[name] = ctx.enter_context(nc.semaphore(name))
            return sems[name]

        bank = [ctx.enter_context(nc.psum_tensor(f"bank{i}", [P, 512], F32)) for i in range(8)]
        bA, bB, bC, bD0, bD1, bF0, bF1, bG = bank

        ident = sb("ident", [P, P])
        ones16 = sb("ones16", [P, TOK], F16)
        onesf = sb("onesf", [P, P])
        powm = sb("powm", [P, TILES])

        def weight(name, chunks, n):
            return sb(name, [P, 2, chunks, n], F16)

        W1 = weight("W1", 2, H1)
        W2 = weight("W2", 4, D)
        Gm = weight("Gm", 2, D)
        Wv1 = weight("Wv1", 2, D)
        Wq = weight("Wq", 2, D)
        Wk = weight("Wk", 2, D)
        Wv = weight("Wv", 2, D)
        Wo = weight("Wo", 2, D)
        Wqk3 = weight("Wqk3", 2, D)
        Wl = weight("Wl", 2, D)
        Wr = weight("Wr", 2, D)
        bias = sb("bias", [P, BIAS_W], F16)
        bias_in = sb("bias_in", [2, BIAS_W])
        bias_lo = sb("bias_lo", [2, BIAS_W], F16)
        c2 = sb("c2", [P, D])
        wdb = sb("wdb", [P, D])
        bdb = sb("bdb", [P, D])
        gam = sb("gam", [P, 4])
        bet = sb("bet", [P, 4])
        betb = sb("betb", [P, 4, P])
        stage = [sb(f"stage{i}", [P, 4, 512]) for i in range(2)]

        xin = sb("xin", [P, 2, TILES, D])
        atA = sb("atA", [P, 2, TILES, P])
        xh = sb("xh", [P, TILES, D], F16)
        xl = sb("xl", [P, TILES, D], F16)
        HT = sb("HT", [P, TILES, P], F16)
        cnt = sb("cnt", [P, TILES])
        cnt1 = sb("cnt1", [P, TILES])
        be = sb("be", [P, TILES])
        HBh = sb("HBh", [P, TILES, P], F16)
        HBl = sb("HBl", [P, TILES, P], F16)
        wcf = sb("wcf", [P, TILES])
        wch = sb("wch", [P, TILES], F16)
        wcl = sb("wcl", [P, TILES], F16)
        Dmx = sb("Dmx", [P, TOK])
        Drc = sb("Drc", [P, TOK])
        Dn = sb("Dn", [P, TOK])
        Pf = sb("Pf", [P, TOK])
        Ph = sb("Ph", [P, 2, TILES, P], F16)
        Pl = sb("Pl", [P, 2, TILES, P], F16)
        z1h = sb("z1h", [P, 2, TOK], F16)
        z1l = sb("z1l", [P, 2, TOK], F16)
        r = sb("r", [P, TILES, H1])

        xres = sb("xres", [P, 2, TILES, D])
        rFh = sb("rFh", [P, TILES, 4, P], F16)
        rFl = sb("rFl", [P, TILES, 4, P], F16)
        rst = sb("rst", [P, TILES, 6])
        rmv = sb("rmv", [P, TILES, 2])
        rve = sb("rve", [P, TILES])
        rrs = sb("rrs", [P, TILES])
        rsc = sb("rsc", [P, TILES])
        y0 = sb("y0", [P, TILES, D])
        y0h = sb("y0h", [P, TILES, D], F16)
        y0l = sb("y0l", [P, TILES, D], F16)

        pre, st, mv, ve, rs = {}, {}, {}, {}, {}
        for k in "BCFG":
            pre[k] = sb("pre" + k, [P, TILES, D])
            st[k] = sb("st" + k, [P, TILES, 6])
            mv[k] = sb("mv" + k, [P, TILES, 2])
            ve[k] = sb("ve" + k, [P, TILES])
            rs[k] = sb("rs" + k, [P, TILES])
        x1 = sb("x1", [P, 2, TILES, D])
        x2 = sb("x2", [P, 2, TILES, D])
        x3 = sb("x3", [P, 2, TILES, D])
        x4 = sb("x4", [P, 2, TILES, D])

        aC = sb("aC", [P, 2, TILES, P])
        mrow = sb("mrow", [P, 2, TOK])
        mcol = sb("mcol", [P, 2, TILES])
        am = sb("am", [P, TOK])
        x1Fh = sb("x1Fh", [P, 2, TOK], F16)
        x1Fl = sb("x1Fl", [P, 2, TOK], F16)
        uh = sb("uh", [P, 2, TOK], F16)
        ul = sb("ul", [P, 2, TOK], F16)
        wscr = sb("wscr", [P, TOK])
        wraw = sb("wraw", [P, TILES])
        wpad = sb("wpad", [P, P])
        wrm = sb("wrm", [TILES, 2, NODES])
        wmx = sb("wmx", [TILES, 2])
        wex = sb("wex", [TILES, 2, NODES])
        wsm = sb("wsm", [TILES, 2])
        wrc = sb("wrc", [TILES, 2])
        wpr = sb("wpr", [TILES, 2, NODES])
        pcol = sb("pcol", [P, TILES])

        acD = sb("acD", [P, 2, TILES, NODES])
        x2Fh = sb("x2Fh", [P, 2, TOK], F16)
        x2Fl = sb("x2Fl", [P, 2, TOK], F16)
        qh = sb("qh", [P, 2, TOK], F16)
        ql = sb("ql", [P, 2, TOK], F16)
        kst = sb("kst", [P, 2, 2, TOK], F16)
        Kbd = sb("Kbd", [P, 4, 2, 2, TOK], F16)
        vst = sb("vst", [P, 2, 2, TILES * 4, HD + 1], F16)
        Vbd = sb("Vbd", [P, 2, 2, 2, 2, TILES * 4, HD + 1], F16)
        Sm = sb("Sm", [P, TILES, HEADS, NODES])
        Smx = sb("Smx", [P, TILES, HEADS])
        Ssb = sb("Ssb", [P, TILES, HEADS, NODES])
        E = sb("E", [P, TILES, HEADS, NODES])

        PTh = sb("PTh", [P, TILES, 4, P], F16)
        PTl = sb("PTl", [P, TILES, 4, P], F16)
        rinv = sb("rinv", [P, TILES, HEADS])
        cx = sb("cx", [P, TILES, D])
        cFh = sb("cFh", [P, 2, TOK], F16)
        cFl = sb("cFl", [P, 2, TOK], F16)

        atG = sb("atG", [P, 2, TILES, P])
        acG = sb("acG", [P, 2, TILES, NODES])
        deg = sb("deg", [P, TILES])
        gp = sb("gp", [P, TILES, D])
        gt = sb("gt", [P, TILES, D])
        xg = sb("xg", [P, TILES, D])
        xgFh = sb("xgFh", [P, 2, TOK], F16)
        xgFl = sb("xgFl", [P, 2, TOK], F16)
        qt = sb("qt", [P, 2, TOK])
        Qh = sb("Qh", [P, 2, TOK], F16)
        Ql = sb("Ql", [P, 2, TOK], F16)
        SA = sb("SA", [P, TOK])
        SAh = sb("SAh", [P, TILES, P], F16)
        SAl = sb("SAl", [P, TILES, P], F16)
        ssum = sb("ssum", [P, TILES])
        srec = sb("srec", [P, TILES])
        y3h = sb("y3h", [P, TILES, D], F16)
        y3l = sb("y3l", [P, TILES, D], F16)
        o2 = sb("o2", [P, TILES, D])
        o3 = sb("o3", [P, TILES, D])

        class At:

            def __init__(self, k, j, fixed):
                self.j, self.fixed = j, fixed - LAG[k]
                self.par = self.fixed % 2

            def n(self, d=0):
                return 2 * self.j + (self.fixed + 1 + d) if self.j is not None else self.fixed + 1 + d

            def tile(self, t, d=0):
                k = 2 * (self.fixed + d) + t + 1
                return 4 * self.j + k if self.j is not None else k

            def chain(self, per, i, d=0):
                k = per * (self.fixed + d) + i
                return 2 * per * self.j + k if self.j is not None else k

            def dma(self, per, d=0):
                k = (self.fixed >> 1) + 1 + d
                return self.j * (16 * per) + 16 * per * k if self.j is not None else 16 * per * k

            def before(self):
                return At("A", self.j, self.fixed - 1)

            def group(self):
                return 2 * self.j + self.fixed if self.j is not None else self.fixed

            def earlier(self, d):
                return self.j is not None or self.fixed >= d

        def run(eng, stages, order):
            def step(j, s, lo, hi):
                live = [stages[k](At(k, j, s)) for k in order if lo <= LAG[k] <= hi]
                while live:
                    live = [g for g in live if next(g, None) is not None]

            first = LAST_LAG + 1
            last = first + (GROUPS - first) // 2 * 2
            for s in range(first):
                step(None, s, 0, s)
            with eng.Fori(first // 2, last // 2) as j:
                for par in range(2):
                    step(j, par, 0, LAST_LAG)
            for s in range(last, STEPS):
                step(None, s, max(0, s - GROUPS + 1), LAST_LAG)


        order = ["F", "G", "B", "C", "D", "A"]

        block = ctx.enter_context(nc.Block())

        weights_in = [
            ("W1", w1t, 2, H1), ("W2", w2t, 4, D), ("Wqk1", wqk1t, 4, D), ("Wv1", wv1, 2, D), ("Wq", wqt, 2, D),
            ("Wk", wkt, 2, D), ("Wv", wvt, 2, D), ("Wo", wot, 2, D), ("Wqk3", wqk3t, 2, D), ("Wl", wlt, 2, D),
            ("Wr", wrt, 2, D)]

        @block.sync
        def _(sp):
            def blocks(dst, src, at, name):
                v = src.rearrange("(g t b) i j -> b g i t j", t=TILES, b=2)
                for b in range(2):
                    sp.dma_start(dst[64 * b:64 * b + 64, at.par, :, 64 * b:64 * b + 64],
                                 v[b, bass.ds(at.group(), 1)].rearrange("g i t j -> (g i) t j")
                                 ).then_inc(ev(f"{name}{at.par}"), 16)

            xv = x.rearrange("(g t p) d -> g p t d", t=TILES, p=P)
            ov = out.rearrange("(g t p) d -> g p t d", t=TILES, p=P)
            av = adj.rearrange("(g t b) i j -> g (b i) t j", t=TILES, b=2)
            mr = mask.rearrange("(g o k) -> g o k", o=1, k=TOK)

            def at_group(v, at):
                return v[bass.ds(at.group(), 1)].rearrange("g p t d -> (g p) t d")

            def load_A(at):
                if at.earlier(2):
                    sp.wait_ge(ev("x_lo"), at.n(-2)).then_inc(ev("sp_held"), 1)
                sp.dma_start(xin[:, at.par], at_group(xv, at)).then_inc(ev(f"x_in{at.par}"), 16)
                if at.earlier(2):
                    sp.wait_ge(ev("h_t"), at.n(-2)).then_inc(ev("sp_held"), 1)
                    sp.wait_ge(ev("w_lo"), at.chain(3, 3, -2)).then_inc(ev("sp_held"), 1)
                blocks(atA, adj_t, at, "at_in")

            def load_B(at):
                if at.earlier(2):
                    sp.wait_ge(ev("preB"), at.n(-2)).then_inc(ev("sp_held"), 1)
                sp.dma_start(xres[:, at.par], at_group(xv, at)).then_inc(ev(f"xres_in{at.par}"), 16)

            def load_C(at):
                if at.earlier(2):
                    sp.wait_ge(ev("adj_masked"), at.n(-2)).then_inc(ev("sp_held"), 1)
                    sp.wait_ge(ev("w_masked"), at.n(-2)).then_inc(ev("sp_held"), 1)
                blocks(aC, adj, at, "C_in")
                sp.dma_start(mrow[:, at.par], mr[bass.ds(at.group(), 1)].rearrange("g o k -> (g o) k")
                             .broadcast_to([P, TOK])).then_inc(ev(f"C_in{at.par}"), 16)
                sp.dma_start(mcol[:, at.par], mask_col[bass.ds(at.group(), 1)].rearrange("g p t -> (g p) t")
                             ).then_inc(ev(f"C_in{at.par}"), 16)

            def load_D(at):
                if at.earlier(2):
                    sp.wait_ge(ev("s_masked"), at.tile(1, -2)).then_inc(ev("sp_held"), 1)
                sp.dma_start(acD[:, at.par], at_group(av, at)).then_inc(ev(f"acD_in{at.par}"), 16)

            def load_G(at):
                if at.earlier(2):
                    sp.wait_ge(ev("gate_pre"), at.chain(2, 1, -2)).then_inc(ev("sp_held"), 1)
                    sp.wait_ge(ev("attn"), at.n(-2)).then_inc(ev("sp_held"), 1)
                sp.dma_start(acG[:, at.par], at_group(av, at)).then_inc(ev(f"G_in{at.par}"), 16)
                blocks(atG, adj_t, at, "G_in")

            loads = {"A": load_A, "B": load_B, "C": load_C, "D": load_D, "G": load_G}

            def place_kv(at):
                sp.wait_ge(ev("k_lo"), at.n()).then_inc(ev("sp_held"), 1)
                if at.earlier(1):
                    sp.wait_ge(ev("scores"), at.tile(1, -1)).then_inc(ev("sp_held"), 1)
                for h in range(4):
                    sp.dma_start(Kbd[32 * h:32 * h + 32, h], kst[32 * h:32 * h + 32]
                                 ).then_inc(ev(f"k_bd{at.par}"), 16)
                sp.wait_ge(ev("v_lo"), at.n()).then_inc(ev("sp_held"), 1)
                if at.earlier(2):
                    sp.wait_ge(ev("ctx"), at.tile(1, -2)).then_inc(ev("sp_held"), 1)
                for b in range(2):
                    for h2 in range(2):
                        sp.dma_start(Vbd[64 * h2:64 * h2 + 64, at.par, b, :, h2], vst[64 * b:64 * b + 64, :, h2]
                                     ).then_inc(ev(f"v_bd{at.par}"), 16)

            def store(at):
                sp.wait_ge(ev("xG"), at.n()).then_inc(ev("sp_held"), 1)
                sp.dma_start(at_group(ov, at), x4[:, at.par]).then_inc(ev(f"stored{at.par}"), 16)

            def stage_in(i):
                name, src, chunks, n = weights_in[i]
                if i >= 2:
                    sp.wait_ge(ev("unstaged"), i - 1)
                sp.dma_start(stage[i % 2][:, 0:chunks, 0:n], src.rearrange("(c p) n -> p c n", p=P)
                             ).then_inc(ev(f"staged{i % 2}"), 16)

            sp.wait_ge(ev("cleared"), 1)
            for k in ("A", "B", "C"):
                pass
            small = [(gam[:], gamma), (bet[:], beta),
                     (wdb[:], wd.rearrange("(o d) -> o d", o=1).broadcast_to([P, D])),
                     (bdb[:], bd.rearrange("(o d) -> o d", o=1).broadcast_to([P, D]))]
            for name, src in (("b1", b1), ("b2", b2), ("bq", bq), ("bk", bk), ("bv", bv), ("bo", bo), ("bl", bl),
                              ("bqk", bqk)):
                c, w, _ = BIAS[name]
                small.append((bias_in[:, c:c + w], src.rearrange("(o d) -> o d", o=1).broadcast_to([2, w])))
            stage_in(0)
            for dst, src in small:
                sp.dma_start(dst, src).then_inc(ev("small_in"), 16)
            load_A(At("A", None, 0))
            for i in range(1, len(weights_in)):
                stage_in(i)

            def dmas(j, s, lo, hi):
                for k in "ABCDG":
                    if lo <= LAG[k] + 0 and k in loads:
                        at = At(k, j, s + 1)
                        if j is not None or 0 <= at.fixed < GROUPS:
                            loads[k](at)
                at = At("D", j, s)
                if j is not None or 0 <= at.fixed < GROUPS:
                    place_kv(at)
                at = At("G", j, s)
                if j is not None or 0 <= at.fixed < GROUPS:
                    store(at)

            first = LAST_LAG + 1
            last = first + (GROUPS - first) // 2 * 2
            for s in range(first):
                dmas(None, s, 0, 0)
            with sp.Fori(first // 2, (last - 2) // 2) as j:
                for par in range(2):
                    dmas(j, par, 0, 0)
            for s in range(last - 2, STEPS):
                dmas(None, s, 0, 0)
            for par in range(2):
                sp.wait_ge(ev(f"stored{par}"), 16 * (GROUPS // 2))

        @block.tensor
        def _(pe):
            def mm3(o, sh, sl, mh, ml, start, stop):
                pe.matmul(o, sh, mh, start=start, stop=False, skip_group_check=True)
                pe.matmul(o, sh, ml, start=False, stop=False, skip_group_check=True)
                return pe.matmul(o, sl, mh, start=False, stop=stop, skip_group_check=True)

            def project_fm(o, W, name, ah, al):
                for c in range(2):
                    oc = o[:, c * TOK:(c + 1) * TOK]
                    cols = slice(c * P, (c + 1) * P)
                    if name:
                        b0 = BIAS[name][0] + c * P
                        pe.matmul(oc, bias[:, b0:b0 + P], ones16[:], start=True, stop=False, skip_group_check=True)
                    for k in range(2):
                        m = mm3(oc, W[:, 0, k, cols], W[:, 1, k, cols], ah[:, k], al[:, k],
                                start=(k == 0 and not name), stop=(k == 1))
                return m

            def project_tm(o, ah, al, W, name, t, chunks=2, n=D, n0=0):
                tok = slice(t * P, (t + 1) * P)
                if name:
                    b0 = BIAS[name][0] + n0
                    pe.matmul(o, ones16[:, 0:P], bias[:, b0:b0 + n], start=True, stop=False, skip_group_check=True)
                for k in range(chunks):
                    m = mm3(o, ah[:, k, tok], al[:, k, tok], W[:, 0, k, n0:n0 + n], W[:, 1, k, n0:n0 + n],
                            start=(k == 0 and not name), stop=(k == chunks - 1))
                return m

            def turn(o, src, ident_=ident):
                for c in range(2):
                    for t in range(TILES):
                        m = pe.transpose(o[:, c * TOK + t * P:c * TOK + (t + 1) * P], src[:, t, c * P:(c + 1) * P],
                                         ident_[:])
                return m

            pe.wait_ge(ev("w2_scaled"), 1)
            for k in range(4):
                m = pe.matmul(bA[:, 0:D], onesf[:], stage[1][:, k, 0:D], start=(k == 0), stop=(k == 3))
            m.then_inc(ev("setup_pe"), 1)
            pe.wait_ge(ev("w2_scaled"), 2)
            for k in range(4):
                m = pe.matmul(bB[:, 0:D], betb[:, k], stage[1][:, k, D:2 * D], start=(k == 0), stop=(k == 3))
            m.then_inc(ev("setup_pe"), 1)
            pe.wait_ge(ev("staged0"), 32)
            for c in range(2):
                for k in range(2):
                    m = pe.matmul(bC[:, c * D:(c + 1) * D], stage[0][:, k, c * P:(c + 1) * P], stage[0][:, 2 + k, 0:D],
                                  start=(k == 0), stop=(k == 1))
            m.then_inc(ev("setup_pe"), 1)
            pe.wait_ge(ev("unstaged"), len(weights_in))
            pe.wait_ge(ev("biases"), 1)

            def stage_A(at):
                pe.wait_ge(ev("hb_lo"), at.n())
                if at.earlier(1):
                    pe.wait_ge(ev("relu"), at.tile(1, -1))
                for t in range(TILES):
                    o = bA[:, t * P:(t + 1) * P]
                    pe.matmul(o, HT[:, t], HBh[:, t], start=True, stop=False, skip_group_check=True)
                    pe.matmul(o, HT[:, t], HBl[:, t], start=False, stop=True, skip_group_check=True)
                pe.wait_ge(ev("w_lo"), at.chain(3, 3))
                for t in range(TILES):
                    o = bA[:, TOK + t * P:TOK + (t + 1) * P]
                    pe.matmul(o, wch[:, t:t + 1].broadcast_to([P, P]), HT[:, t], start=True, stop=False,
                              skip_group_check=True)
                    m = pe.matmul(o, wcl[:, t:t + 1].broadcast_to([P, P]), HT[:, t], start=False, stop=True,
                                  skip_group_check=True)
                m.then_inc(ev("m_and_d"), 1)
                yield 1
                pe.wait_ge(ev("p_lo"), at.n())
                pe.wait_ge(ev("x_lo"), at.n())
                for c in range(2):
                    for t in range(TILES):
                        m = mm3(bA[:, c * TOK + t * P:c * TOK + (t + 1) * P], xh[:, t, c * P:(c + 1) * P],
                                xl[:, t, c * P:(c + 1) * P], Ph[:, at.par, t], Pl[:, at.par, t], True, True)
                m.then_inc(ev("z1"), 1)
                yield 1
                pe.wait_ge(ev("z1_lo"), at.n())
                project_tm(bA[:], z1h, z1l, W1, "b1", 0, n=H1).then_inc(ev("z"), 1)
                yield 1
                pe.wait_ge(ev("relu"), at.tile(0))
                project_tm(bA[:], z1h, z1l, W1, "b1", 1, n=H1).then_inc(ev("z"), 1)
                yield 1

            def stage_B(at):
                if at.earlier(1):
                    pe.wait_ge(ev("preB"), at.n(-1))
                for t in range(TILES):
                    pe.wait_ge(ev("relu"), at.tile(t))
                    if t:
                        pe.wait_ge(ev("rF_lo"), at.tile(t - 1))
                    for k in range(4):
                        m = pe.transpose(bB[:, k * P:(k + 1) * P], r[:, t, k * P:(k + 1) * P], ident[:])
                    m.then_inc(ev("r_turned"), 1)
                    yield 1
                pe.wait_ge(ev("rF_lo"), at.tile(1))
                for t in range(TILES):
                    o = bB[:, t * D:(t + 1) * D]
                    for k in range(4):
                        m = mm3(o, rFh[:, t, k], rFl[:, t, k], W2[:, 0, k], W2[:, 1, k], k == 0, k == 3)
                m.then_inc(ev("y0_raw"), 1)
                yield 1
                pe.wait_ge(ev("y0_lo"), at.n())
                b0 = BIAS["b2"][0]
                for t in range(TILES):
                    o = bB[:, t * D:(t + 1) * D]
                    pe.matmul(o, ones16[:, 0:P], bias[:, b0:b0 + D], start=True, stop=False, skip_group_check=True)
                    m = mm3(o, Ph[:, at.par, t], Pl[:, at.par, t], y0h[:, t], y0l[:, t], False, True)
                m.then_inc(ev("conv2"), 1)
                yield 1

            def stage_C(at):
                pe.wait_ge(ev("xB"), at.n())
                if at.earlier(1):
                    pe.wait_ge(ev("preC"), at.n(-1))
                turn(bC, x1[:, at.par]).then_inc(ev("x1_turned"), 1)
                yield 1
                pe.wait_ge(ev("x1F_lo"), at.n())
                project_fm(bC, Gm, None, x1Fh, x1Fl).then_inc(ev("u"), 1)
                yield 1
                pe.wait_ge(ev("u_lo"), at.n())
                for t in range(TILES):
                    tok = slice(t * P, (t + 1) * P)
                    for k in range(2):
                        m = mm3(bC[:, tok], uh[:, k, tok], ul[:, k, tok], x1Fh[:, k, tok], x1Fl[:, k, tok],
                                k == 0, k == 1)
                m.then_inc(ev("uxT"), 1)
                yield 1
                pe.wait_ge(ev("w_masked"), at.n())
                pe.transpose(bC[:, 0:P], wpad[:], ident[:]).then_inc(ev("w_turned"), 1)
                yield 1
                pe.wait_ge(ev("w_probs"), at.n()).then_inc(ev("pe_held"), 1)
                pe.transpose(bC[:, 0:TILES], wpr[:].rearrange("t b k -> t (b k)"), ident[0:TILES, 0:TILES]
                             ).then_inc(ev("p_turned"), 1)
                yield 1
                pe.wait_ge(ev("p_col"), at.n())
                for t in range(TILES):
                    m = project_tm(bC[:, t * D:(t + 1) * D], x1Fh, x1Fl, Wv1, None, t)
                m.then_inc(ev("v1"), 1)
                yield 1

            def stage_D(at):
                pe.wait_ge(ev("xC"), at.n())
                if at.earlier(1):
                    pe.wait_ge(ev("s_masked"), at.tile(1, -1))
                turn(bD0, x2[:, at.par]).then_inc(ev("x2_turned"), 1)
                yield 1
                pe.wait_ge(ev("x2F_lo"), at.n())
                project_fm(bD1, Wq, "bq", x2Fh, x2Fl).then_inc(ev("q"), 1)
                yield 1
                project_fm(bD0, Wk, "bk", x2Fh, x2Fl).then_inc(ev("k"), 1)
                yield 1
                pe.wait_ge(ev("q_lo"), at.n())
                for h2 in range(2):
                    for t in range(TILES):
                        m = project_tm(bD1[:, (h2 * TILES + t) * P:(h2 * TILES + t + 1) * P], x2Fh, x2Fl, Wv, "bv", t,
                                       n=P, n0=h2 * P)
                m.then_inc(ev("v"), 1)
                yield 1
                pe.wait_ge(ev(f"k_bd{at.par}"), at.dma(4))
                for t in range(TILES):
                    if t:
                        pe.wait_ge(ev("v_lo"), at.n())
                    o = (bD0, bD1)[t]
                    for c in range(2):
                        for i, (qq, hl) in enumerate(((qh, 0), (qh, 1), (ql, 0))):
                            for b in range(2):
                                tok = slice(t * P + 64 * b, t * P + 64 * b + 64)
                                m = pe.matmul(o[64 * b:64 * b + 64, c * 256:(c + 1) * 256], qq[:, c, tok],
                                              Kbd[:, :, hl, c, tok], start=(i == 0), stop=(i == 2),
                                              skip_group_check=True)
                    m.then_inc(ev("scores"), 1)
                    yield 1

            def stage_F(at):
                if at.earlier(1):
                    pe.wait_ge(ev("preF"), at.n(-1))
                for t in range(TILES):
                    pe.wait_ge(ev("exp"), at.tile(t))
                    o = (bF0, bF1)[t]
                    for hp in range(4):
                        m = pe.transpose(o[:, hp * P:(hp + 1) * P],
                                         E[:, t, 2 * hp:2 * hp + 2].rearrange("p h k -> p (h k)"), ident[:])
                    m.then_inc(ev("e_turned"), 1)
                    yield 1
                pe.wait_ge(ev(f"v_bd{at.par}"), at.dma(4))
                for t in range(TILES):
                    pe.wait_ge(ev("pt_lo"), at.tile(t))
                    o = (bF0, bF1)[t]
                    for hp in range(4):
                        for i, (pt, hl) in enumerate(((PTh, 0), (PTh, 1), (PTl, 0))):
                            for b in range(2):
                                m = pe.matmul(o[64 * b:64 * b + 64, hp * 66:(hp + 1) * 66],
                                              pt[:, t, hp, 64 * b:64 * b + 64], Vbd[:, at.par, b, hl, :, 4 * t + hp],
                                              start=(i == 0), stop=(i == 2), skip_group_check=True)
                    m.then_inc(ev("ctx"), 1)
                    yield 1
                pe.wait_ge(ev("cx"), at.tile(1))
                turn(bF0, cx).then_inc(ev("cx_turned"), 1)
                yield 1
                pe.wait_ge(ev("cF_lo"), at.n())
                for t in range(TILES):
                    m = project_tm(bF1[:, t * D:(t + 1) * D], cFh, cFl, Wo, "bo", t)
                m.then_inc(ev("attn_out"), 1)
                yield 1

            def stage_G(at):
                yield 1
                pe.wait_ge(ev("xg"), at.n())
                if at.earlier(1):
                    pe.wait_ge(ev("mixed"), at.n(-1))
                turn(bG, xg).then_inc(ev("xg_turned"), 1)
                yield 1
                pe.wait_ge(ev("xgF_lo"), at.n())
                project_fm(bG, Wqk3, "bqk", xgFh, xgFl).then_inc(ev("qk3"), 1)
                yield 1
                pe.wait_ge(ev("Q_split"), at.chain(2, 2))
                for t in range(TILES):
                    tok = slice(t * P, (t + 1) * P)
                    for k in range(2):
                        m = mm3(bG[:, tok], Qh[:, k, tok], Ql[:, k, tok], Qh[:, k, tok], Ql[:, k, tok], k == 0, k == 1)
                m.then_inc(ev("s3"), 1)
                yield 1
                pe.wait_ge(ev("attn_lo"), at.n())
                for t in range(TILES):
                    pe.matmul(bG[:, t:t + 1], SAh[:, t], ones16[:, 0:1], start=True, stop=False, skip_group_check=True)
                    m = pe.matmul(bG[:, t:t + 1], SAl[:, t], ones16[:, 0:1], start=False, stop=True,
                                  skip_group_check=True)
                m.then_inc(ev("row_sum"), 1)
                yield 1
                pe.wait_ge(ev("row_scale"), at.chain(2, 1))
                for t in range(TILES):
                    m = project_tm(bG[:, t * D:(t + 1) * D], xgFh, xgFl, Wl, None, t)
                m.then_inc(ev("y3"), 1)
                yield 1
                pe.wait_ge(ev("y3_lo"), at.n())
                for t in range(TILES):
                    m = project_tm(bG[:, t * D:(t + 1) * D], xgFh, xgFl, Wr, "bl", t)
                m.then_inc(ev("o2_raw"), 1)
                yield 1
                pe.wait_ge(ev("o2"), at.n())
                for t in range(TILES):
                    m = mm3(bG[:, t * D:(t + 1) * D], SAh[:, t], SAl[:, t], y3h[:, t], y3l[:, t], True, True)
                m.then_inc(ev("o1"), 1)
                yield 1

            run(pe, {"A": stage_A, "B": stage_B, "C": stage_C, "D": stage_D, "F": stage_F, "G": stage_G}, order)

        @block.scalar
        def _(act):
            def cast(dst, src, scale=1.0):
                return act.activation(dst, src, ACT.Copy, scale=scale)

            def high(i, W, src, then):
                cast(W, src, WS).then_inc(ev("w_hi"), 1)

            act.wait_ge(ev("staged0"), 16)
            cast(W1[:, 0], stage[0][:, 0:2, 0:H1], WS).then_inc(ev("w_hi"), 1)
            act.wait_ge(ev("w2_centred"), 1)
            cast(W2[:, 0], stage[1][:, :, 0:D], WS).then_inc(ev("w_hi"), 1)
            act.wait_ge(ev("setup_pe"), 3)
            cast(Gm[:, 0], bC[:].rearrange("p (c n) -> p c n", c=2), WS).then_inc(ev("w_hi"), 1)
            for i, W in enumerate((Wv1, Wq, Wk, Wv, Wo, Wqk3, Wl, Wr)):
                i += 3
                act.wait_ge(ev(f"staged{i % 2}"), 16 * (i // 2 + 1))
                cast(W[:, 0], stage[i % 2][:, 0:2, 0:D], WS).then_inc(ev("w_hi"), 1)

            def stage_A(at):
                act.wait_ge(ev(f"x_in{at.par}"), at.dma(1))
                if at.earlier(1):
                    act.wait_ge(ev("z1"), at.n(-1))
                cast(xh[:], xin[:, at.par]).then_inc(ev("x_hi"), 1)
                yield 1
                act.wait_ge(ev("p_f"), at.n())
                cast(Ph[:, at.par].rearrange("p t k -> p (t k)"), Pf[:]).then_inc(ev("p_hi"), 1)
                yield 1
                act.wait_ge(ev("z1"), at.n())
                cast(z1h[:].rearrange("p c k -> p (c k)"), bA[:]).then_inc(ev("z1_hi"), 1)
                yield 1
                for t in range(TILES):
                    act.wait_ge(ev("z"), at.tile(t))
                    if at.earlier(1):
                        act.wait_ge(ev("r_var"), at.chain(2, 1, -1))
                        act.wait_ge(ev("r_turned"), at.tile(1, -1))
                    act.activation(r[:, t], bA[:], ACT.Relu, scale=1.0 / WS).then_inc(ev("relu"), 1)
                    yield 1

            def stage_B(at):
                for t in range(TILES):
                    act.wait_ge(ev("r_turned"), at.tile(t))
                    cast(rFh[:, t].rearrange("p c k -> p (c k)"), bB[:]).then_inc(ev("rF_hi"), 1)
                    yield 1
                act.wait_ge(ev("y0_f"), at.n())
                cast(y0h[:], y0[:]).then_inc(ev("y0_hi"), 1)
                yield 1

            def stage_C(at):
                act.wait_ge(ev("x1_turned"), at.n())
                cast(x1Fh[:].rearrange("p c k -> p (c k)"), bC[:]).then_inc(ev("x1F_hi"), 1)
                yield 1
                act.wait_ge(ev("u"), at.n())
                cast(uh[:].rearrange("p c k -> p (c k)"), bC[:], 1.0 / WS).then_inc(ev("u_hi"), 1)
                yield 1
                yield 1
                act.wait_ge(ev("w_shifted"), at.n())
                act.activation(wex[:], wrm[:], ACT.Exp, scale=SOFT1).then_inc(ev("w_exp"), 1)
                yield 1

            def stage_D(at):
                act.wait_ge(ev("x2_turned"), at.n())
                cast(x2Fh[:].rearrange("p c k -> p (c k)"), bD0[:]).then_inc(ev("x2F_hi"), 1)
                yield 1
                act.wait_ge(ev("q"), at.n())
                cast(qh[:].rearrange("p c k -> p (c k)"), bD1[:], 1.0 / WS).then_inc(ev("q_hi"), 1)
                yield 1
                act.wait_ge(ev("k"), at.n())
                if at.earlier(1):
                    act.wait_ge(ev(f"k_bd{1 - at.par}"), at.before().dma(4))
                cast(kst[:, 0].rearrange("p c k -> p (c k)"), bD0[:], 1.0 / WS).then_inc(ev("k_hi"), 1)
                yield 1
                act.wait_ge(ev("v"), at.n())
                if at.earlier(1):
                    act.wait_ge(ev(f"v_bd{1 - at.par}"), at.before().dma(4))
                cast(vst[:, 0].rearrange("p h e d -> p (h e) d")[:, :, 0:HD],
                     bD1[:].rearrange("p (e d) -> p e d", d=HD), 1.0 / WS).then_inc(ev("v_hi"), 1)
                yield 1
                for t in range(TILES):
                    act.wait_ge(ev("s_shifted"), at.tile(t))
                    if at.earlier(1):
                        act.wait_ge(ev("e_turned"), at.tile(t, -1))
                    act.activation(E[:, t], Ssb[:, t], ACT.Exp, scale=SOFT2).then_inc(ev("exp"), 1)
                    yield 1

            def stage_F(at):
                for t in range(TILES):
                    act.wait_ge(ev("e_turned"), at.tile(t))
                    cast(PTh[:, t].rearrange("p c k -> p (c k)"), (bF0, bF1)[t][:]).then_inc(ev("pt_hi"), 1)
                    yield 1
                yield 1
                yield 1
                act.wait_ge(ev("cx_turned"), at.n())
                cast(cFh[:].rearrange("p c k -> p (c k)"), bF0[:]).then_inc(ev("cF_hi"), 1)
                yield 1

            def stage_G(at):
                act.wait_ge(ev("gate_pre"), at.chain(2, 2))
                act.activation(gt[:], gp[:], ACT.Tanh, scale=0.5).then_inc(ev("gate_tanh"), 1)
                yield 1
                act.wait_ge(ev("xg_turned"), at.n())
                cast(xgFh[:].rearrange("p c k -> p (c k)"), bG[:], 0.5).then_inc(ev("xgF_hi"), 1)
                yield 1
                act.wait_ge(ev("qk3"), at.n())
                act.activation(qt[:].rearrange("p c k -> p (c k)"), bG[:], ACT.Tanh, scale=0.5 / WS
                               ).then_inc(ev("qk_tanh"), 1)
                yield 1
                yield 1
                act.wait_ge(ev("attn"), at.n())
                cast(SAh[:].rearrange("p t k -> p (t k)"), SA[:]).then_inc(ev("attn_hi"), 1)
                yield 1
                act.wait_ge(ev("y3"), at.n())
                cast(y3h[:].rearrange("p t k -> p (t k)"), bG[:], 1.0 / WS).then_inc(ev("y3_hi"), 1)
                yield 1
                act.wait_ge(ev("o2_raw"), at.n())
                if at.earlier(1):
                    act.wait_ge(ev("mixed"), at.n(-1))
                cast(o2[:].rearrange("p t k -> p (t k)"), bG[:], 1.0 / WS).then_inc(ev("o2"), 1)
                yield 1

            run(act, {"A": stage_A, "B": stage_B, "C": stage_C, "D": stage_D, "F": stage_F, "G": stage_G}, order)

        @block.vector
        def _(dve):
            def low(dst, src, hi, scale=1.0):
                return dve.scalar_tensor_tensor(out=dst, in0=src, scalar=scale, in1=hi, op0=ALU.mult,
                                                op1=ALU.subtract)

            dve.memset(ones16[:], 1.0).then_inc(ev("const"), 1)
            dve.memset(onesf[:], 1.0).then_inc(ev("const"), 1)
            for buf in (bias, Kbd, Vbd, atA, aC, atG, wpad):
                dve.memset(buf[:], 0.0).then_inc(ev("const"), 1)
            dve.memset(vst[:, 1], 0.0).then_inc(ev("const"), 1)
            dve.memset(vst[:, 0], 1.0).then_inc(ev("const"), 1)
            dve.wait_ge(ev("const"), 11)
            dve.wait_ge(ev("ident"), 3).then_inc(ev("cleared"), 1)

            dve.wait_ge(ev("w_hi"), 1)
            low(W1[:, 1], stage[0][:, 0:2, 0:H1], W1[:, 0], WS).then_inc(ev("unstaged"), 1)
            dve.wait_ge(ev("staged1"), 16)
            dve.wait_ge(ev("small_in"), 16 * 12)
            dve.tensor_copy(stage[1][:, :, D:2 * D], stage[1][:, :, 0:D]).then_inc(ev("setup"), 1)
            dve.wait_ge(ev("setup"), 1)
            for k in range(4):
                m = dve.tensor_scalar(stage[1][:, k, 0:D], stage[1][:, k, D:2 * D], gam[:, k:k + 1], None, ALU.mult)
            m.then_inc(ev("w2_scaled"), 1)
            for k in range(4):
                m = dve.tensor_scalar(betb[:, k], onesf[:], bet[:, k:k + 1], None, ALU.mult)
            m.then_inc(ev("w2_scaled"), 1)
            dve.wait_ge(ev("setup_pe"), 1)
            dve.wait_ge(ev("w2_scaled"), 1)
            for k in range(4):
                m = dve.scalar_tensor_tensor(out=stage[1][:, k, 0:D], in0=bA[:, 0:D], scalar=-1.0 / H1,
                                             in1=stage[1][:, k, 0:D], op0=ALU.mult, op1=ALU.add)
            m.then_inc(ev("w2_centred"), 1)
            dve.wait_ge(ev("setup_pe"), 2)
            dve.tensor_copy(c2[:], bB[:, 0:D])
            dve.wait_ge(ev("w_hi"), 2)
            low(W2[:, 1], stage[1][:, :, 0:D], W2[:, 0], WS).then_inc(ev("unstaged"), 1)
            dve.wait_ge(ev("w_hi"), 3)
            low(Gm[:, 1], bC[:].rearrange("p (c n) -> p c n", c=2), Gm[:, 0], WS).then_inc(ev("unstaged"), 1)
            for i, W in enumerate((Wv1, Wq, Wk, Wv, Wo, Wqk3, Wl, Wr)):
                dve.wait_ge(ev("w_hi"), i + 4)
                low(W[:, 1], stage[(i + 3) % 2][:, 0:2, 0:D], W[:, 0], WS).then_inc(ev("unstaged"), 1)
            for name, (c, w, scale) in BIAS.items():
                m = dve.tensor_scalar(bias[0:2, c:c + w], bias_in[:, c:c + w], scale, None, ALU.mult)
            m.then_inc(ev("setup"), 1)
            dve.wait_ge(ev("setup"), 2)
            for name, (c, w, scale) in BIAS.items():
                m = low(bias_lo[:, c:c + w], bias_in[:, c:c + w], bias[0:2, c:c + w], scale)
            m.then_inc(ev("setup"), 1)
            dve.wait_ge(ev("setup"), 3)
            dve.tensor_copy(bias[0:2, :], bias_lo[:]).then_inc(ev("setup"), 1)
            dve.wait_ge(ev("setup"), 4)
            for name, (c, w, scale) in BIAS.items():
                m = dve.tensor_scalar(bias[0:1, c:c + w], bias_in[0:1, c:c + w], scale, None, ALU.mult)
            m.then_inc(ev("biases"), 1)

            def norm(k, dst, at):
                dve.wait_ge(ev("pre" + k), at.n())
                for t in range(TILES):
                    m = dve.bn_stats(st[k][:, t], pre[k][:, t])
                m.then_inc(ev("var" + k), 1)
                dve.wait_ge(ev("var" + k), at.chain(2, 1)).then_inc(ev("dve_held"), 1)
                for t in range(TILES):
                    m = dve.bn_aggr(mv[k][:, t], st[k][:, t])
                m.then_inc(ev("var" + k), 1)
                yield 1
                dve.wait_ge(ev("rstd" + k), at.chain(2, 2))
                for t in range(TILES):
                    m = dve.tensor_scalar(dst[:, t], pre[k][:, t], mv[k][:, t, 0:1], rs[k][:, t:t + 1],
                                          ALU.subtract, ALU.mult)
                m.then_inc(ev("x" + k), 1)

            def stage_A(at):
                dve.wait_ge(ev(f"at_in{at.par}"), at.dma(2))
                dve.tensor_scalar(HT[:], atA[:, at.par], 0.0, None, ALU.not_equal).then_inc(ev("h_t"), 1)
                dve.wait_ge(ev("h_t"), at.n())
                dve.tensor_reduce(cnt[:], HT[:], AX.X, ALU.add).then_inc(ev("b_chain"), 1)
                dve.wait_ge(ev("b_chain"), at.chain(4, 1))
                dve.tensor_scalar(cnt1[:], cnt[:], 1.0, None, ALU.max).then_inc(ev("b_chain"), 1)
                dve.wait_ge(ev("b_chain"), at.chain(4, 2))
                dve.reciprocal(be[:], cnt1[:]).then_inc(ev("b_chain"), 1)
                dve.wait_ge(ev("b_chain"), at.chain(4, 3))
                for t in range(TILES):
                    m = dve.tensor_scalar(HBh[:, t], HT[:, t], be[:, t:t + 1], None, ALU.mult)
                m.then_inc(ev("b_chain"), 1)
                dve.wait_ge(ev("b_chain"), at.chain(4, 4))
                for t in range(TILES):
                    m = low(HBl[:, t], HT[:, t], HBh[:, t], be[:, t:t + 1])
                m.then_inc(ev("hb_lo"), 1)
                yield 1
                dve.wait_ge(ev("m_and_d"), at.n())
                dve.tensor_scalar(Dmx[:], bA[:, TOK:2 * TOK], TINY, None, ALU.max).then_inc(ev("d_chain"), 1)
                dve.wait_ge(ev("d_chain"), at.chain(3, 1))
                dve.reciprocal(Drc[:], Dmx[:]).then_inc(ev("d_chain"), 1)
                dve.wait_ge(ev("d_chain"), at.chain(3, 2))
                dve.scalar_tensor_tensor(out=Dn[:], in0=bA[:, TOK:2 * TOK], scalar=0.0, in1=Drc[:], op0=ALU.is_gt,
                                         op1=ALU.mult).then_inc(ev("d_chain"), 1)
                dve.wait_ge(ev("d_chain"), at.chain(3, 3))
                dve.tensor_tensor(Pf[:], bA[:, 0:TOK], Dn[:], ALU.mult).then_inc(ev("p_f"), 1)
                yield 1
                dve.wait_ge(ev("z1_hi"), at.n())
                low(z1l[:].rearrange("p c k -> p (c k)"), bA[:], z1h[:].rearrange("p c k -> p (c k)")
                    ).then_inc(ev("z1_lo"), 1)
                yield 1

            def stage_B(at):
                for t in range(TILES):
                    dve.wait_ge(ev("rF_hi"), at.tile(t))
                    low(rFl[:, t].rearrange("p c k -> p (c k)"), bB[:], rFh[:, t].rearrange("p c k -> p (c k)")
                        ).then_inc(ev("rF_lo"), 1)
                    m = dve.bn_stats(rst[:, t], r[:, t])
                    if t:
                        m.then_inc(ev("r_var"), 1)
                        dve.wait_ge(ev("r_var"), at.chain(2, 1)).then_inc(ev("dve_held"), 1)
                        for u in range(TILES):
                            m = dve.bn_aggr(rmv[:, u], rst[:, u])
                        m.then_inc(ev("r_var"), 1)
                    yield 1
                dve.wait_ge(ev("y0_raw"), at.n())
                dve.wait_ge(ev("r_rstd"), at.chain(3, 3))
                for t in range(TILES):
                    m = dve.scalar_tensor_tensor(out=y0[:, t], in0=bB[:, t * D:(t + 1) * D], scalar=rsc[:, t:t + 1],
                                                 in1=c2[:], op0=ALU.mult, op1=ALU.add)
                m.then_inc(ev("y0_f"), 1)
                yield 1
                dve.wait_ge(ev("conv2"), at.n())
                dve.wait_ge(ev(f"xres_in{at.par}"), at.dma(1))
                dve.scalar_tensor_tensor(out=pre["B"][:].rearrange("p t k -> p (t k)"),
                                         in0=xres[:, at.par].rearrange("p t k -> p (t k)"), scalar=2.0, in1=bB[:],
                                         op0=ALU.mult, op1=ALU.add).then_inc(ev("preB"), 1)
                yield from norm("B", x1[:, at.par], at)
                yield 1

            def stage_C(at):
                dve.wait_ge(ev("x1F_hi"), at.n())
                low(x1Fl[:].rearrange("p c k -> p (c k)"), bC[:], x1Fh[:].rearrange("p c k -> p (c k)")
                    ).then_inc(ev("x1F_lo"), 1)
                yield 1
                dve.wait_ge(ev("u_hi"), at.n())
                low(ul[:].rearrange("p c k -> p (c k)"), bC[:], uh[:].rearrange("p c k -> p (c k)"), 1.0 / WS
                    ).then_inc(ev("u_lo"), 1)
                yield 1
                dve.wait_ge(ev("uxT"), at.n())
                dve.wait_ge(ev("adj_masked"), at.n())
                for t in range(TILES):
                    tok = slice(t * P, (t + 1) * P)
                    m = dve.tensor_tensor_reduce(wscr[:, tok], bC[:, tok], am[:, tok], 1.0, 0.0, ALU.mult, ALU.add,
                                                 wraw[:, t:t + 1])
                m.then_inc(ev("w_raw"), 1)
                dve.wait_ge(ev("w_raw"), at.n())
                dve.wait_ge(ev(f"C_in{at.par}"), at.dma(4))
                dve.tensor_tensor(wpad[:, 0:TILES], wraw[:], mcol[:, at.par], ALU.mult).then_inc(ev("w_masked"), 1)
                yield 1
                wv = bC[0:TILES, 0:P].rearrange("t (b k) -> t b k", b=2)
                dve.wait_ge(ev("w_turned"), at.n())
                dve.tensor_reduce(wmx[:], wv, AX.X, ALU.max).then_inc(ev("c_softmax"), 1)
                dve.wait_ge(ev("c_softmax"), at.chain(3, 1))
                dve.tensor_tensor(wrm[:], wv, wmx[:].rearrange("t (b o) -> t b o", o=1).broadcast_to(
                    [TILES, 2, NODES]), ALU.subtract).then_inc(ev("w_shifted"), 1)
                yield 1
                dve.wait_ge(ev("w_exp"), at.n())
                dve.tensor_reduce(wsm[:], wex[:], AX.X, ALU.add).then_inc(ev("c_softmax"), 1)
                dve.wait_ge(ev("c_softmax"), at.chain(3, 2))
                dve.reciprocal(wrc[:], wsm[:]).then_inc(ev("c_softmax"), 1)
                dve.wait_ge(ev("c_softmax"), at.chain(3, 3))
                dve.tensor_tensor(wpr[:], wex[:], wrc[:].rearrange("t (b o) -> t b o", o=1).broadcast_to(
                    [TILES, 2, NODES]), ALU.mult).then_inc(ev("w_probs"), 1)
                yield 1
                dve.wait_ge(ev("p_turned"), at.n())
                dve.tensor_scalar(pcol[:], bC[:, 0:TILES], 1.0 / WS, None, ALU.mult).then_inc(ev("p_col"), 1)
                yield 1
                dve.wait_ge(ev("v1"), at.n())
                dve.wait_ge(ev("p_col"), at.n())
                for t in range(TILES):
                    m = dve.scalar_tensor_tensor(out=pre["C"][:, t], in0=bC[:, t * D:(t + 1) * D],
                                                 scalar=pcol[:, t:t + 1], in1=x1[:, at.par, t], op0=ALU.mult,
                                                 op1=ALU.add)
                m.then_inc(ev("preC"), 1)
                yield from norm("C", x2[:, at.par], at)
                yield 1

            def stage_D(at):
                dve.wait_ge(ev("x2F_hi"), at.n())
                low(x2Fl[:].rearrange("p c k -> p (c k)"), bD0[:], x2Fh[:].rearrange("p c k -> p (c k)")
                    ).then_inc(ev("x2F_lo"), 1)
                yield 1
                dve.wait_ge(ev("q_hi"), at.n())
                low(ql[:].rearrange("p c k -> p (c k)"), bD1[:], qh[:].rearrange("p c k -> p (c k)"), 1.0 / WS
                    ).then_inc(ev("q_lo"), 1)
                yield 1
                dve.wait_ge(ev("k_hi"), at.n())
                low(kst[:, 1].rearrange("p c k -> p (c k)"), bD0[:], kst[:, 0].rearrange("p c k -> p (c k)"), 1.0 / WS
                    ).then_inc(ev("k_lo"), 1)
                yield 1
                dve.wait_ge(ev("v_hi"), at.n())
                low(vst[:, 1].rearrange("p h e d -> p (h e) d")[:, :, 0:HD],
                    bD1[:].rearrange("p (e d) -> p e d", d=HD),
                    vst[:, 0].rearrange("p h e d -> p (h e) d")[:, :, 0:HD], 1.0 / WS).then_inc(ev("v_lo"), 1)
                yield 1
                dve.wait_ge(ev(f"acD_in{at.par}"), at.dma(1))
                for t in range(TILES):
                    dve.wait_ge(ev("scores"), at.tile(t))
                    dve.tensor_tensor(Sm[:, t], (bD0, bD1)[t][:].rearrange("p (h k) -> p h k", h=HEADS),
                                      acD[:, at.par, t:t + 1].broadcast_to([P, HEADS, NODES]), ALU.mult
                                      ).then_inc(ev("s_masked"), 1)
                    dve.wait_ge(ev("s_masked"), at.tile(t))
                    dve.tensor_reduce(Smx[:, t], Sm[:, t], AX.X, ALU.max).then_inc(ev("s_max"), 1)
                    yield 1

            def stage_F(at):
                for t in range(TILES):
                    dve.wait_ge(ev("pt_hi"), at.tile(t))
                    low(PTl[:, t].rearrange("p c k -> p (c k)"), (bF0, bF1)[t][:],
                        PTh[:, t].rearrange("p c k -> p (c k)")).then_inc(ev("pt_lo"), 1)
                    yield 1
                for t in range(TILES):
                    c = (bF0, bF1)[t][:, 0:HEADS * (HD + 1)].rearrange("p (h d) -> p h d", h=HEADS)
                    dve.wait_ge(ev("ctx"), at.tile(t))
                    dve.reciprocal(rinv[:, t:t + 1].rearrange("p t h -> p h t"), c[:, :, HD:HD + 1]
                                   ).then_inc(ev("rinv"), 1)
                    dve.wait_ge(ev("rinv"), at.tile(t))
                    dve.tensor_tensor(cx[:, t].rearrange("p (h d) -> p h d", h=HEADS), c[:, :, 0:HD],
                                      rinv[:, t:t + 1].rearrange("p t h -> p h t").broadcast_to([P, HEADS, HD]),
                                      ALU.mult).then_inc(ev("cx"), 1)
                    yield 1
                dve.wait_ge(ev("cF_hi"), at.n())
                low(cFl[:].rearrange("p c k -> p (c k)"), bF0[:], cFh[:].rearrange("p c k -> p (c k)")
                    ).then_inc(ev("cF_lo"), 1)
                yield 1
                dve.wait_ge(ev("attn_out"), at.n())
                dve.scalar_tensor_tensor(out=pre["F"][:].rearrange("p t k -> p (t k)"), in0=bF1[:], scalar=1.0 / WS,
                                         in1=x2[:, at.par].rearrange("p t k -> p (t k)"), op0=ALU.mult, op1=ALU.add
                                         ).then_inc(ev("preF"), 1)
                yield from norm("F", x3[:, at.par], at)
                yield 1

            def stage_G(at):
                dve.wait_ge(ev(f"G_in{at.par}"), at.dma(3))
                dve.tensor_reduce(deg[:], acG[:, at.par], AX.X, ALU.add).then_inc(ev("gate_pre"), 1)
                dve.wait_ge(ev("gate_pre"), at.chain(2, 1))
                for t in range(TILES):
                    m = dve.scalar_tensor_tensor(out=gp[:, t], in0=wdb[:], scalar=deg[:, t:t + 1], in1=bdb[:],
                                                 op0=ALU.mult, op1=ALU.add)
                m.then_inc(ev("gate_pre"), 1)
                yield 1
                dve.wait_ge(ev("gate_tanh"), at.n())
                dve.wait_ge(ev("xF"), at.n())
                dve.scalar_tensor_tensor(out=xg[:].rearrange("p t k -> p (t k)"),
                                         in0=gt[:].rearrange("p t k -> p (t k)"), scalar=1.0,
                                         in1=x3[:, at.par].rearrange("p t k -> p (t k)"), op0=ALU.add, op1=ALU.mult
                                         ).then_inc(ev("xg"), 1)
                yield 1
                dve.wait_ge(ev("xgF_hi"), at.n())
                low(xgFl[:].rearrange("p c k -> p (c k)"), bG[:], xgFh[:].rearrange("p c k -> p (c k)"), 0.5
                    ).then_inc(ev("xgF_lo"), 1)
                yield 1
                dve.wait_ge(ev("qk_tanh"), at.n())
                dve.tensor_scalar(Qh[:], qt[:], 1.0, None, ALU.add).then_inc(ev("Q_split"), 1)
                dve.wait_ge(ev("Q_split"), at.chain(2, 1))
                dve.scalar_tensor_tensor(out=Ql[:], in0=qt[:], scalar=1.0, in1=Qh[:], op0=ALU.add, op1=ALU.subtract
                                         ).then_inc(ev("Q_split"), 1)
                yield 1
                dve.wait_ge(ev("s3"), at.n())
                dve.scalar_tensor_tensor(out=SA[:], in0=bG[:, 0:TOK], scalar=QK3,
                                         in1=atG[:, at.par].rearrange("p t k -> p (t k)"), op0=ALU.mult, op1=ALU.mult
                                         ).then_inc(ev("attn"), 1)
                yield 1
                dve.wait_ge(ev("row_sum"), at.n())
                dve.tensor_scalar(ssum[:], bG[:, 0:TILES], 1e-6, None, ALU.add).then_inc(ev("row_scale"), 1)
                dve.wait_ge(ev("row_scale"), at.chain(2, 1))
                dve.reciprocal(srec[:], ssum[:]).then_inc(ev("row_scale"), 1)
                yield 1
                dve.wait_ge(ev("y3_hi"), at.n())
                low(y3l[:].rearrange("p t k -> p (t k)"), bG[:], y3h[:].rearrange("p t k -> p (t k)"), 1.0 / WS
                    ).then_inc(ev("y3_lo"), 1)
                yield 1
                dve.wait_ge(ev("o1"), at.n())
                dve.wait_ge(ev("row_scale"), at.chain(2, 2))
                for t in range(TILES):
                    m = dve.scalar_tensor_tensor(out=o3[:, t], in0=bG[:, t * D:(t + 1) * D], scalar=srec[:, t:t + 1],
                                                 in1=o2[:, t], op0=ALU.mult, op1=ALU.add)
                m.then_inc(ev("mixed"), 1)
                dve.wait_ge(ev("mixed"), at.n())
                dve.scalar_tensor_tensor(out=pre["G"][:].rearrange("p t k -> p (t k)"),
                                         in0=o3[:].rearrange("p t k -> p (t k)"), scalar=0.0,
                                         in1=x3[:, at.par].rearrange("p t k -> p (t k)"), op0=ALU.max, op1=ALU.add
                                         ).then_inc(ev("preG"), 1)
                if at.earlier(2):
                    dve.wait_ge(ev(f"stored{at.par}"), at.dma(1, -1))
                yield from norm("G", x4[:, at.par], at)
                yield 1

            run(dve, {"A": stage_A, "B": stage_B, "C": stage_C, "D": stage_D, "F": stage_F, "G": stage_G}, order)

        @block.gpsimd
        def _(pool):
            pool.memset(powm[:], -0.5).then_inc(ev("ident"), 1)
            pool.memset(ident[:], 0.0).then_inc(ev("ident"), 1)
            pool.wait_ge(ev("ident"), 2)
            pool.affine_select(out=ident[:], in_=ident[:], compare_op=ALU.not_equal, fill=1.0, base=0,
                               pattern=[[-1, P]], channel_multiplier=1).then_inc(ev("ident"), 1)
            pool.wait_ge(ev("ident"), 3)

            def sub(dst, a, b):
                return pool.tensor_tensor(dst, a, b, ALU.subtract)

            def rstd(k, at):
                pool.wait_ge(ev("var" + k), at.chain(2, 2)).then_inc(ev("pool_held"), 1)
                pool.tensor_scalar(ve[k][:], mv[k][:, :, 1], EPS, None, ALU.add).then_inc(ev("rstd" + k), 1)
                pool.wait_ge(ev("rstd" + k), at.chain(2, 1))
                pool.tensor_tensor(rs[k][:], ve[k][:], powm[:], ALU.pow).then_inc(ev("rstd" + k), 1)

            def stage_A(at):
                pool.wait_ge(ev(f"at_in{at.par}"), at.dma(2)).then_inc(ev("pool_held"), 1)
                if at.earlier(1):
                    pool.wait_ge(ev("m_and_d"), at.n(-1)).then_inc(ev("pool_held"), 1)
                pool.tensor_tensor(wcf[:], atA[:, at.par, :, 0], atA[:, at.par, :, 64], ALU.add
                                   ).then_inc(ev("w_lo"), 1)
                pool.wait_ge(ev("w_lo"), at.chain(3, 1)).then_inc(ev("pool_held"), 1)
                pool.tensor_copy(wch[:], wcf[:]).then_inc(ev("w_lo"), 1)
                pool.wait_ge(ev("w_lo"), at.chain(3, 2))
                sub(wcl[:], wcf[:], wch[:]).then_inc(ev("w_lo"), 1)
                pool.wait_ge(ev("x_hi"), at.n())
                sub(xl[:], xin[:, at.par], xh[:]).then_inc(ev("x_lo"), 1)
                yield 1
                pool.wait_ge(ev("p_hi"), at.n())
                sub(Pl[:, at.par].rearrange("p t k -> p (t k)"), Pf[:], Ph[:, at.par].rearrange("p t k -> p (t k)")
                    ).then_inc(ev("p_lo"), 1)
                yield 1

            def stage_B(at):
                yield 1
                pool.wait_ge(ev("r_var"), at.chain(2, 2)).then_inc(ev("pool_held"), 1)
                pool.tensor_scalar(rve[:], rmv[:, :, 1], EPS, None, ALU.add).then_inc(ev("r_rstd"), 1)
                pool.wait_ge(ev("r_rstd"), at.chain(3, 1))
                pool.tensor_tensor(rrs[:], rve[:], powm[:], ALU.pow).then_inc(ev("r_rstd"), 1)
                pool.wait_ge(ev("r_rstd"), at.chain(3, 2)).then_inc(ev("pool_held"), 1)
                pool.tensor_scalar(rsc[:], rrs[:], 1.0 / WS, None, ALU.mult).then_inc(ev("r_rstd"), 1)
                yield 1
                pool.wait_ge(ev("y0_hi"), at.n())
                sub(y0l[:], y0[:], y0h[:]).then_inc(ev("y0_lo"), 1)
                yield 1
                rstd("B", at)
                yield 1

            def stage_C(at):
                pool.wait_ge(ev(f"C_in{at.par}"), at.dma(4))
                if at.earlier(1):
                    pool.wait_ge(ev("w_raw"), at.n(-1))
                pool.tensor_tensor(am[:], aC[:, at.par].rearrange("p t k -> p (t k)"), mrow[:, at.par], ALU.mult
                                   ).then_inc(ev("adj_masked"), 1)
                for _ in range(6):
                    yield 1
                rstd("C", at)
                yield 1

            def stage_D(at):
                for _ in range(4):
                    yield 1
                for t in range(TILES):
                    pool.wait_ge(ev("s_max"), at.tile(t))
                    if at.earlier(1):
                        pool.wait_ge(ev("exp"), at.tile(t, -1))
                    pool.tensor_tensor(Ssb[:, t], Sm[:, t], Smx[:, t:t + 1].rearrange("p t h -> p h t").broadcast_to(
                        [P, HEADS, NODES]), ALU.subtract).then_inc(ev("s_shifted"), 1)
                    yield 1

            def stage_F(at):
                for _ in range(5):
                    yield 1
                rstd("F", at)
                yield 1

            def stage_G(at):
                for _ in range(4):
                    yield 1
                pool.wait_ge(ev("attn_hi"), at.n())
                sub(SAl[:].rearrange("p t k -> p (t k)"), SA[:], SAh[:].rearrange("p t k -> p (t k)")
                    ).then_inc(ev("attn_lo"), 1)
                for _ in range(3):
                    yield 1
                rstd("G", at)
                yield 1

            run(pool, {"A": stage_A, "B": stage_B, "C": stage_C, "D": stage_D, "F": stage_F, "G": stage_G}, order)


def kernel(**inputs):
    import numpy as np
    import concourse.bacc as bacc
    from concourse.bass_utils import run_bass_kernel_spmd

    a = {k: np.ascontiguousarray(v) for k, v in inputs.items()}

    def turned(w):
        return np.ascontiguousarray(w.T)

    even_odd = np.arange(D).reshape(4, 2, HD).transpose(1, 0, 2).reshape(-1)
    arrays = {
        "x": a["x"].reshape(GRAPHS * NODES, D), "adj": a["adj"],
        "adj_t": np.ascontiguousarray(a["adj"].transpose(0, 2, 1)), "mask": a["nodemask"].reshape(-1),
        "mask_col": np.ascontiguousarray(a["nodemask"].reshape(GROUPS, TILES, P).transpose(0, 2, 1)),
        "w1t": turned(a["L0_gnn_W1"]), "b1": a["L0_gnn_b1"], "gamma": turned(a["L0_gnn_gamma"].reshape(4, P)),
        "beta": turned(a["L0_gnn_beta"].reshape(4, P)),
        "w2t": turned(a["L0_gnn_W2"]), "b2": a["L0_gnn_b2"],
        "wqk1t": turned(a["L1_gnn_Wqk"]), "wv1": a["L1_gnn_Wv"],
        "wqt": turned(a["L2_gnn_Wq"]), "bq": a["L2_gnn_bq"], "wkt": turned(a["L2_gnn_Wk"]), "bk": a["L2_gnn_bk"],
        "wvt": np.ascontiguousarray(turned(a["L2_gnn_Wv"])[:, even_odd]),
        "bv": np.ascontiguousarray(a["L2_gnn_bv"][even_odd]),
        "wot": turned(a["L2_gnn_Wo"]), "bo": a["L2_gnn_bo"],
        "wqk3t": turned(a["L3_gnn_Wqk"]), "bqk": a["L3_gnn_bqk"], "wlt": turned(a["L3_gnn_Wl"]), "bl": a["L3_gnn_bl"],
        "wrt": turned(a["L3_gnn_Wr"]), "wd": a["L3_gnn_Wd"].reshape(-1), "bd": a["L3_gnn_bd"],
    }
    nc = bacc.Bacc("TRN2", target_bir_lowering=False, num_devices=1)
    args = [nc.dram_tensor(n, v.shape, mybir.dt.from_np(v.dtype), kind="ExternalInput").ap()
            for n, v in arrays.items()]
    args.append(nc.dram_tensor("out", (GRAPHS * NODES, D), F32, kind="ExternalOutput").ap())
    build(nc, *args)
    res = run_bass_kernel_spmd(nc, [arrays], core_ids=[0])
    return res.results[0]["out"].reshape(GRAPHS, NODES, D)
```

```python
from contextlib import ExitStack

import concourse.bass as bass
from concourse import mybir

F32 = mybir.dt.float32
F16 = mybir.dt.float16
ALU = mybir.AluOpType
ACT = mybir.ActivationFunctionType
AX = mybir.AxisListType

P = 128
GRAPHS, NODES, D = 128, 64, 256
H1 = 512
TILES = 2
TOK = TILES * P
GROUPS = GRAPHS * NODES // TOK
HEADS, HD = 8, D // 8
WS = 64.0
EPS = 1e-5
SOFT1 = 1.0 / 16.0
SOFT2 = 2.0 * HD ** -0.5
QK3 = 0.25 / 16.0
HUGE = 3e38
ORDER = [1, 3, 2, 4, 5, 0]

ROUNDS = 8
LAST_LAG = 5
STEPS = GROUPS + LAST_LAG

BIAS = {"b1": (0, 512, WS), "b2": (512, 256, 1.0), "bq": (768, 256, WS), "bk": (1024, 256, WS),
        "bv": (1280, 256, WS), "bo": (1536, 256, WS), "bl": (1792, 256, WS), "bqk": (2048, 256, WS)}
BIAS_W = 2304


def build(nc, x, adj, adj_t, mask, mask_col, w1t, b1, gamma, beta, w2t, b2, wqk1t, wv1, wqt, bq, wkt, bk, wvt, bv,
          wot, bo, wqk3t, bqk, wlt, bl, wrt, wd, bd, out):
    ctx = ExitStack()
    with ctx:
        def sb(name, shape, dt=F32):
            return ctx.enter_context(nc.sbuf_tensor(name, shape, dt))

        sems = {}

        def ev(name):
            if name not in sems:
                sems[name] = ctx.enter_context(nc.semaphore(name))
            return sems[name]

        bank = [ctx.enter_context(nc.psum_tensor(f"bank{i}", [P, 512], F32)) for i in range(8)]
        bA, bB, bC, bD0, bD1, bF0, bF1, bG = bank

        ident = sb("ident", [P, P])
        ones16 = sb("ones16", [P, TOK], F16)
        onesf = sb("onesf", [P, P])
        powm = sb("powm", [P, TILES])

        def weight(name, chunks, n):
            return sb(name, [P, 2, chunks, n], F16)

        W1 = weight("W1", 2, H1)
        W2 = weight("W2", 4, D)
        Gm = weight("Gm", 2, D)
        Wv1 = weight("Wv1", 2, D)
        Wq = weight("Wq", 2, D)
        Wk = weight("Wk", 2, D)
        Wv = weight("Wv", 2, D)
        Wo = weight("Wo", 2, D)
        Wqk3 = weight("Wqk3", 2, D)
        Wl = weight("Wl", 2, D)
        Wr = weight("Wr", 2, D)
        bias = sb("bias", [P, BIAS_W], F16)
        c2 = sb("c2", [P, D])
        wdb = sb("wdb", [P, D])
        bdb = sb("bdb", [P, D])
        gam = sb("gam", [P, 4])
        bet = sb("bet", [P, 4])
        betb = sb("betb", [P, 4, P])

        late = [sb("late0", [P, 2, 4, 512]), sb("late1", [P, 5, TILES, D])]
        stage = [late[0][:, i] for i in range(2)]
        bias_in = late[1][0:2].rearrange("p a t d -> p (a t d)")[:, 0:BIAS_W]
        bias_lo = sb("bias_lo", [2, BIAS_W], F16)
        x3, x4, Sm, Ssb = [late[0][:, i, 2 * k:2 * k + 2] for i in range(2) for k in range(2)]
        x3, x4 = [v.rearrange("p a (t d) -> p a t d", t=TILES) for v in (x3, x4)]
        cx, gw, xg, o2, o3 = [late[1][:, i] for i in range(5)]
        Sm, Ssb = [v.rearrange("p t (h k) -> p t h k", h=HEADS) for v in (Sm, Ssb)]

        xin = sb("xin", [P, 2, TILES, D])
        atA = sb("atA", [P, 2, TILES, P])
        xh = sb("xh", [P, TILES, D], F16)
        xl = sb("xl", [P, TILES, D], F16)
        HT = sb("HT", [P, TILES, P], F16)
        cnt = sb("cnt", [P, TILES])
        cnt1 = sb("cnt1", [P, TILES])
        be = sb("be", [P, TILES])
        HBh = sb("HBh", [P, TILES, P], F16)
        HBl = sb("HBl", [P, TILES, P], F16)
        wcf = sb("wcf", [P, TILES])
        wch = sb("wch", [P, TILES], F16)
        wcl = sb("wcl", [P, TILES], F16)
        Dbg = sb("Dbg", [P, TILES])
        Dd = sb("Dd", [P, TILES])
        Dinv = sb("Dinv", [P, TILES])
        Pf = sb("Pf", [P, TILES, P])
        Ph = sb("Ph", [P, 2, TILES, P], F16)
        Pl = sb("Pl", [P, 2, TILES, P], F16)
        z1h = sb("z1h", [P, 2, TOK], F16)
        z1l = sb("z1l", [P, 2, TOK], F16)
        r = sb("r", [P, TILES, H1])

        xres = sb("xres", [P, 2, TILES, D])
        rFh = sb("rFh", [P, TILES, 4, P], F16)
        rFl = sb("rFl", [P, TILES, 4, P], F16)
        rst = sb("rst", [P, TILES, 6])
        rmv = sb("rmv", [P, TILES, 2])
        rve = sb("rve", [P, TILES])
        rrs = sb("rrs", [P, TILES])
        rsc = sb("rsc", [P, TILES])
        y0 = sb("y0", [P, TILES, D])
        y0h = sb("y0h", [P, TILES, D], F16)
        y0l = sb("y0l", [P, TILES, D], F16)

        pre, st, mv, ve, rs, nb = {}, {}, {}, {}, {}, {}
        for k in "BCFG":
            pre[k] = sb("pre" + k, [P, TILES, D])
            st[k] = sb("st" + k, [P, TILES, 6])
            mv[k] = sb("mv" + k, [P, TILES, 2])
            ve[k] = sb("ve" + k, [P, TILES])
            rs[k] = sb("rs" + k, [P, TILES])
            nb[k] = sb("nb" + k, [P, TILES])
        x1 = sb("x1", [P, 2, TILES, D])
        x2 = sb("x2", [P, 2, TILES, D])

        aC = sb("aC", [P, 2, TILES, P])
        mrow = sb("mrow", [P, 2, TOK])
        mcol = sb("mcol", [P, 2, TILES])
        am = sb("am", [P, TOK])
        x1Fh = [sb(f"x1Fh{i}", [P, 2, TOK], F16) for i in range(2)]
        x1Fl = [sb(f"x1Fl{i}", [P, 2, TOK], F16) for i in range(2)]
        uh = sb("uh", [P, 2, TOK], F16)
        ul = sb("ul", [P, 2, TOK], F16)
        wscr = sb("wscr", [P, TOK])
        wraw = sb("wraw", [P, TILES])
        wpad = sb("wpad", [P, P])
        wrm = sb("wrm", [TILES, 2, NODES])
        wmx = sb("wmx", [TILES, 2])
        wex = sb("wex", [TILES, 2, NODES])
        wsm = sb("wsm", [TILES, 2])
        wrc = sb("wrc", [TILES, 2])
        wpr = sb("wpr", [TILES, 2, NODES])
        pcol = sb("pcol", [P, TILES])

        acD = sb("acD", [P, 2, TILES, NODES])
        x2Fh = sb("x2Fh", [P, 2, TOK], F16)
        x2Fl = sb("x2Fl", [P, 2, TOK], F16)
        qh = sb("qh", [P, 2, TOK], F16)
        ql = sb("ql", [P, 2, TOK], F16)
        kst = sb("kst", [P, 2, 2, TOK], F16)
        Kbd = sb("Kbd", [P, 4, 2, 2, TOK], F16)
        vst = sb("vst", [P, 2, 2, TILES * 4, HD + 1], F16)
        Vbd = sb("Vbd", [P, 2, 2, 2, 2, TILES * 4, HD + 1], F16)
        Smx = sb("Smx", [P, TILES, HEADS])
        E = sb("E", [P, TILES, HEADS, NODES])

        PTh = sb("PTh", [P, TILES, 4, P], F16)
        PTl = sb("PTl", [P, TILES, 4, P], F16)
        rinv = sb("rinv", [P, TILES, HEADS])
        cFh = sb("cFh", [P, 2, TOK], F16)
        cFl = sb("cFl", [P, 2, TOK], F16)

        atG = sb("atG", [P, 2, TILES, P])
        acG = sb("acG", [P, 2, TILES, NODES])
        deg = sb("deg", [P, TILES])
        gp = sb("gp", [P, TILES, D])
        gt = sb("gt", [P, TILES, D])
        g2 = sb("g2", [P, TILES, D])
        xgFh = sb("xgFh", [P, 2, TOK], F16)
        xgFl = sb("xgFl", [P, 2, TOK], F16)
        qt = sb("qt", [P, 2, TOK])
        Qh = sb("Qh", [P, 2, TOK], F16)
        Ql = sb("Ql", [P, 2, TOK], F16)
        SA = sb("SA", [P, TOK])
        SAh = sb("SAh", [P, TILES, P], F16)
        SAl = sb("SAl", [P, TILES, P], F16)
        ssum = sb("ssum", [P, TILES])
        srec = sb("srec", [P, TILES])
        y3h = sb("y3h", [P, TILES, D], F16)
        y3l = sb("y3l", [P, TILES, D], F16)

        class At:

            def __init__(self, stream, j, fixed):
                self.j, self.fixed = j, fixed - stream
                self.par = self.fixed % 2

            def n(self, d=0):
                return 2 * self.j + (self.fixed + 1 + d) if self.j is not None else self.fixed + 1 + d

            def tile(self, t, d=0):
                k = 2 * (self.fixed + d) + t + 1
                return 4 * self.j + k if self.j is not None else k

            def chain(self, per, i, d=0):
                k = per * (self.fixed + d) + i
                return 2 * per * self.j + k if self.j is not None else k

            def dma(self, per, d=0):
                k = (self.fixed >> 1) + 1 + d
                return self.j * (16 * per) + 16 * per * k if self.j is not None else 16 * per * k

            def before(self):
                return At(0, self.j, self.fixed - 1)

            def group(self):
                return 2 * self.j + self.fixed if self.j is not None else self.fixed

            def earlier(self, d):
                return self.j is not None or self.fixed >= d

        def rest(n):
            for _ in range(n):
                yield 1

        def run(eng, streams):
            def step(j, s, lo, hi):
                live = [streams[k](At(k, j, s)) for k in ORDER if lo <= k <= hi]
                for _ in range(ROUNDS):
                    live = [g for g in live if next(g, None) is not None]
                assert not [g for g in live if next(g, None) is not None]

            first = LAST_LAG + 1
            last = first + (GROUPS - first) // 2 * 2
            for s in range(first):
                step(None, s, 0, s)
            with eng.Fori(first // 2, last // 2) as j:
                for par in range(2):
                    step(j, par, 0, LAST_LAG)
            for s in range(last, STEPS):
                step(None, s, max(0, s - GROUPS + 1), LAST_LAG)



        block = ctx.enter_context(nc.Block())

        weights_in = [
            ("W1", w1t, 2, H1), ("W2", w2t, 4, D), ("Wqk1", wqk1t, 4, D), ("Wv1", wv1, 2, D), ("Wq", wqt, 2, D),
            ("Wk", wkt, 2, D), ("Wv", wvt, 2, D), ("Wo", wot, 2, D), ("Wqk3", wqk3t, 2, D), ("Wl", wlt, 2, D),
            ("Wr", wrt, 2, D)]

        @block.sync
        def _(sp):
            def blocks(dst, src, at, name):
                v = src.rearrange("(g t b) i j -> b g i t j", t=TILES, b=2)
                for b in range(2):
                    sp.dma_start(dst[64 * b:64 * b + 64, at.par, :, 64 * b:64 * b + 64],
                                 v[b, bass.ds(at.group(), 1)].rearrange("g i t j -> (g i) t j")
                                 ).then_inc(ev(f"{name}{at.par}"), 16)

            xv = x.rearrange("(g t p) d -> g p t d", t=TILES, p=P)
            ov = out.rearrange("(g t p) d -> g p t d", t=TILES, p=P)
            av = adj.rearrange("(g t b) i j -> g (b i) t j", t=TILES, b=2)
            mr = mask.rearrange("(g o k) -> g o k", o=1, k=TOK)

            def at_group(v, at):
                return v[bass.ds(at.group(), 1)].rearrange("g p t d -> (g p) t d")

            def load_conv(at):
                if at.earlier(2):
                    sp.wait_ge(ev("x_lo"), at.n(-2)).then_inc(ev("sp_held"), 1)
                sp.dma_start(xin[:, at.par], at_group(xv, at)).then_inc(ev(f"x_in{at.par}"), 16)
                if at.earlier(2):
                    sp.wait_ge(ev("h_t"), at.n(-2)).then_inc(ev("sp_held"), 1)
                    sp.wait_ge(ev("w_lo"), at.chain(3, 3, -2)).then_inc(ev("sp_held"), 1)
                blocks(atA, adj_t, at, "at_in")

            def load_residual(at):
                if at.earlier(2):
                    sp.wait_ge(ev("preB"), at.n(-2)).then_inc(ev("sp_held"), 1)
                sp.dma_start(xres[:, at.par], at_group(xv, at)).then_inc(ev(f"xres_in{at.par}"), 16)

            def load_layer1(at):
                if at.earlier(2):
                    sp.wait_ge(ev("adj_masked"), at.n(-2)).then_inc(ev("sp_held"), 1)
                    sp.wait_ge(ev("w_masked"), at.n(-2)).then_inc(ev("sp_held"), 1)
                blocks(aC, adj, at, "C_in")
                sp.dma_start(mrow[:, at.par], mr[bass.ds(at.group(), 1)].rearrange("g o k -> (g o) k")
                             .broadcast_to([P, TOK])).then_inc(ev(f"C_in{at.par}"), 16)
                sp.dma_start(mcol[:, at.par], mask_col[bass.ds(at.group(), 1)].rearrange("g p t -> (g p) t")
                             ).then_inc(ev(f"C_in{at.par}"), 16)

            def load_layer2(at):
                if at.earlier(2):
                    sp.wait_ge(ev("s_masked"), at.tile(1, -2)).then_inc(ev("sp_held"), 1)
                sp.dma_start(acD[:, at.par], at_group(av, at)).then_inc(ev(f"acD_in{at.par}"), 16)

            def load_gate(at):
                if at.earlier(2):
                    sp.wait_ge(ev("deg"), at.n(-2)).then_inc(ev("sp_held"), 1)
                sp.dma_start(acG[:, at.par], at_group(av, at)).then_inc(ev(f"acG_in{at.par}"), 16)

            def load_layer3(at):
                if at.earlier(2):
                    sp.wait_ge(ev("attn"), at.n(-2)).then_inc(ev("sp_held"), 1)
                blocks(atG, adj_t, at, "atG_in")

            loads = [load_conv, load_residual, None, load_layer2, load_gate, load_layer3]

            def place_k(at):
                sp.wait_ge(ev("k_lo"), at.n()).then_inc(ev("sp_held"), 1)
                if at.earlier(1):
                    sp.wait_ge(ev("scores"), at.tile(1, -1)).then_inc(ev("sp_held"), 1)
                for h in range(4):
                    sp.dma_start(Kbd[32 * h:32 * h + 32, h], kst[32 * h:32 * h + 32]
                                 ).then_inc(ev(f"k_bd{at.par}"), 16)

            def place_v(at):
                sp.wait_ge(ev("v_lo"), at.n()).then_inc(ev("sp_held"), 1)
                if at.earlier(2):
                    sp.wait_ge(ev("ctx"), at.tile(1, -2)).then_inc(ev("sp_held"), 1)
                for b in range(2):
                    for h2 in range(2):
                        sp.dma_start(Vbd[64 * h2:64 * h2 + 64, at.par, b, :, h2], vst[64 * b:64 * b + 64, :, h2]
                                     ).then_inc(ev(f"v_bd{at.par}"), 16)

            def store(at):
                sp.wait_ge(ev("xG"), at.n()).then_inc(ev("sp_held"), 1)
                sp.dma_start(at_group(ov, at), x4[:, at.par]).then_inc(ev(f"stored{at.par}"), 16)

            def stage_in(i):
                name, src, chunks, n = weights_in[i]
                if i >= 2:
                    sp.wait_ge(ev("unstaged"), i - 1)
                sp.dma_start(stage[i % 2][:, 0:chunks, 0:n], src.rearrange("(c p) n -> p c n", p=P)
                             ).then_inc(ev(f"staged{i % 2}"), 16)

            sp.wait_ge(ev("cleared"), 1)
            small = [(gam[:], gamma), (bet[:], beta),
                     (wdb[:], wd.rearrange("(o d) -> o d", o=1).broadcast_to([P, D])),
                     (bdb[:], bd.rearrange("(o d) -> o d", o=1).broadcast_to([P, D]))]
            for name, src in (("b1", b1), ("b2", b2), ("bq", bq), ("bk", bk), ("bv", bv), ("bo", bo), ("bl", bl),
                              ("bqk", bqk)):
                c, w, _ = BIAS[name]
                small.append((bias_in[:, c:c + w], src.rearrange("(o d) -> o d", o=1).broadcast_to([2, w])))
            stage_in(0)
            for dst, src in small:
                sp.dma_start(dst, src).then_inc(ev("small_in"), 16)
            load_conv(At(0, None, 0))
            load_layer1(At(0, None, 0))
            for i in range(1, len(weights_in)):
                stage_in(i)

            def step(j, s):
                def there(at):
                    return j is not None or 0 <= at.fixed < GROUPS

                at = At(3, j, s)
                if there(at):
                    place_k(at)
                for k, load in enumerate(loads):
                    at = At(k, j, s + 1)
                    if load and there(at):
                        load(at)
                at = At(1, j, s + 1)
                if there(at) and (j is not None or at.fixed > 0):
                    load_layer1(at)
                at = At(3, j, s)
                if there(at):
                    place_v(at)
                at = At(5, j, s)
                if there(at):
                    store(at)

            first = LAST_LAG + 1
            last = first + (GROUPS - first) // 2 * 2 - 2
            for s in range(first):
                step(None, s)
            with sp.Fori(first // 2, last // 2) as j:
                for par in range(2):
                    step(j, par)
            for s in range(last, STEPS):
                step(None, s)
            for par in range(2):
                sp.wait_ge(ev(f"stored{par}"), 16 * (GROUPS // 2))

        @block.tensor
        def _(pe):
            def mm3(o, sh, sl, mh, ml, start, stop):
                pe.matmul(o, sh, mh, start=start, stop=False, skip_group_check=True)
                pe.matmul(o, sh, ml, start=False, stop=False, skip_group_check=True)
                return pe.matmul(o, sl, mh, start=False, stop=stop, skip_group_check=True)

            def project_fm(o, W, name, ah, al):
                for c in range(2):
                    oc = o[:, c * TOK:(c + 1) * TOK]
                    cols = slice(c * P, (c + 1) * P)
                    if name:
                        b0 = BIAS[name][0] + c * P
                        pe.matmul(oc, bias[:, b0:b0 + P], ones16[:], start=True, stop=False, skip_group_check=True)
                    for k in range(2):
                        m = mm3(oc, W[:, 0, k, cols], W[:, 1, k, cols], ah[:, k], al[:, k],
                                start=(k == 0 and not name), stop=(k == 1))
                return m

            def project_tm(o, ah, al, W, name, t, chunks=2, n=D, n0=0):
                tok = slice(t * P, (t + 1) * P)
                if name:
                    b0 = BIAS[name][0] + n0
                    pe.matmul(o, ones16[:, 0:P], bias[:, b0:b0 + n], start=True, stop=False, skip_group_check=True)
                for k in range(chunks):
                    m = mm3(o, ah[:, k, tok], al[:, k, tok], W[:, 0, k, n0:n0 + n], W[:, 1, k, n0:n0 + n],
                            start=(k == 0 and not name), stop=(k == chunks - 1))
                return m

            def turn(o, src, ident_=ident):
                for c in range(2):
                    for t in range(TILES):
                        m = pe.transpose(o[:, c * TOK + t * P:c * TOK + (t + 1) * P], src[:, t, c * P:(c + 1) * P],
                                         ident_[:])
                return m

            pe.wait_ge(ev("w2_scaled"), 1)
            for k in range(4):
                m = pe.matmul(bA[:, 0:D], onesf[:], stage[1][:, k, 0:D], start=(k == 0), stop=(k == 3))
            m.then_inc(ev("setup_pe"), 1)
            pe.wait_ge(ev("w2_scaled"), 2)
            for k in range(4):
                m = pe.matmul(bB[:, 0:D], betb[:, k], stage[1][:, k, D:2 * D], start=(k == 0), stop=(k == 3))
            m.then_inc(ev("setup_pe"), 1)
            pe.wait_ge(ev("staged0"), 32)
            for c in range(2):
                for k in range(2):
                    m = pe.matmul(bC[:, c * D:(c + 1) * D], stage[0][:, k, c * P:(c + 1) * P], stage[0][:, 2 + k, 0:D],
                                  start=(k == 0), stop=(k == 1))
            m.then_inc(ev("setup_pe"), 1)
            pe.wait_ge(ev("unstaged"), len(weights_in))
            pe.wait_ge(ev("biases"), 1)

            def stream0(at):
                yield from rest(1)
                pe.wait_ge(ev("hb_lo"), at.n())
                if at.earlier(1):
                    pe.wait_ge(ev("relu"), at.tile(1, -1))
                for t in range(TILES):
                    o = bA[:, t * P:(t + 1) * P]
                    pe.matmul(o, HT[:, t], HBh[:, t], start=True, stop=False, skip_group_check=True)
                    pe.matmul(o, HT[:, t], HBl[:, t], start=False, stop=True, skip_group_check=True)
                pe.wait_ge(ev("w_lo"), at.chain(3, 3))
                for t in range(TILES):
                    o = bA[:, TOK + t:TOK + t + 1]
                    pe.matmul(o, HT[:, t], wch[:, t:t + 1], start=True, stop=False, skip_group_check=True)
                    m = pe.matmul(o, HT[:, t], wcl[:, t:t + 1], start=False, stop=True, skip_group_check=True)
                m.then_inc(ev("m_and_d"), 1)
                yield 1
                pe.wait_ge(ev("p_f"), at.n())
                for t in range(TILES):
                    m = pe.transpose(bA[:, TOK + t * P:TOK + (t + 1) * P], Pf[:, t], ident[:])
                m.then_inc(ev("p_turned0"), 1)
                yield 1
                pe.wait_ge(ev("p_lo"), at.n())
                pe.wait_ge(ev("x_lo"), at.n())
                for c in range(2):
                    for t in range(TILES):
                        m = mm3(bA[:, c * TOK + t * P:c * TOK + (t + 1) * P], xh[:, t, c * P:(c + 1) * P],
                                xl[:, t, c * P:(c + 1) * P], Ph[:, at.par, t], Pl[:, at.par, t], True, True)
                m.then_inc(ev("z1"), 1)
                yield 1
                pe.wait_ge(ev("z1_lo"), at.n())
                project_tm(bA[:], z1h, z1l, W1, "b1", 0, n=H1).then_inc(ev("z"), 1)
                yield 1
                pe.wait_ge(ev("relu"), at.tile(0))
                project_tm(bA[:], z1h, z1l, W1, "b1", 1, n=H1).then_inc(ev("z"), 1)
                yield 1
                if at.earlier(1):
                    pe.wait_ge(ev("preB"), at.n(-1))
                for t in range(TILES):
                    pe.wait_ge(ev("relu"), at.tile(t))
                    if t:
                        pe.wait_ge(ev("rF_lo"), at.tile(t - 1))
                    for k in range(4):
                        m = pe.transpose(bB[:, k * P:(k + 1) * P], r[:, t, k * P:(k + 1) * P], ident[:])
                    m.then_inc(ev("r_turned"), 1)
                    yield 1

            def stream1(at):
                pe.wait_ge(ev("rF_lo"), at.tile(1))
                for t in range(TILES):
                    o = bB[:, t * D:(t + 1) * D]
                    for k in range(4):
                        m = mm3(o, rFh[:, t, k], rFl[:, t, k], W2[:, 0, k], W2[:, 1, k], k == 0, k == 3)
                m.then_inc(ev("y0_raw"), 1)
                yield from rest(2)
                pe.wait_ge(ev("y0_lo"), at.n())
                b0 = BIAS["b2"][0]
                for t in range(TILES):
                    o = bB[:, t * D:(t + 1) * D]
                    pe.matmul(o, ones16[:, 0:P], bias[:, b0:b0 + D], start=True, stop=False, skip_group_check=True)
                    m = mm3(o, Ph[:, at.par, t], Pl[:, at.par, t], y0h[:, t], y0l[:, t], False, True)
                m.then_inc(ev("conv2"), 1)
                yield from rest(3)
                pe.wait_ge(ev("xB"), at.n())
                if at.earlier(1):
                    pe.wait_ge(ev("preC"), at.n(-1))
                turn(bC, x1[:, at.par]).then_inc(ev("x1_turned"), 1)
                yield 1
                pe.wait_ge(ev("x1F_lo"), at.n())
                project_fm(bC, Gm, None, x1Fh[at.par], x1Fl[at.par]).then_inc(ev("u"), 1)
                yield 1
                pe.wait_ge(ev("u_lo"), at.n())
                for t in range(TILES):
                    tok = slice(t * P, (t + 1) * P)
                    for k in range(2):
                        m = mm3(bC[:, tok], uh[:, k, tok], ul[:, k, tok], x1Fh[at.par][:, k, tok],
                                x1Fl[at.par][:, k, tok], k == 0, k == 1)
                m.then_inc(ev("uxT"), 1)
                yield 1

            def stream2(at):
                pe.wait_ge(ev("w_masked"), at.n())
                pe.transpose(bC[:, 0:P], wpad[:], ident[:]).then_inc(ev("w_turned"), 1)
                yield from rest(2)
                pe.wait_ge(ev("w_probs"), at.n()).then_inc(ev("pe_held"), 1)
                pe.transpose(bC[:, 0:TILES], wpr[:].rearrange("t b k -> t (b k)"), ident[0:TILES, 0:TILES]
                             ).then_inc(ev("p_turned"), 1)
                yield 1
                pe.wait_ge(ev("p_col"), at.n())
                for t in range(TILES):
                    m = project_tm(bC[:, t * D:(t + 1) * D], x1Fh[at.par], x1Fl[at.par], Wv1, None, t)
                m.then_inc(ev("v1"), 1)
                yield from rest(3)
                pe.wait_ge(ev("xC"), at.n())
                if at.earlier(1):
                    pe.wait_ge(ev("s_masked"), at.tile(1, -1))
                turn(bD0, x2[:, at.par]).then_inc(ev("x2_turned"), 1)
                yield 1
                pe.wait_ge(ev("x2F_lo"), at.n())
                project_fm(bD1, Wq, "bq", x2Fh, x2Fl).then_inc(ev("q"), 1)
                yield 1

            def stream3(at):
                yield 1
                project_fm(bD0, Wk, "bk", x2Fh, x2Fl).then_inc(ev("k"), 1)
                yield 1
                pe.wait_ge(ev("q_lo"), at.n())
                for h2 in range(2):
                    for t in range(TILES):
                        m = project_tm(bD1[:, (h2 * TILES + t) * P:(h2 * TILES + t + 1) * P], x2Fh, x2Fl, Wv, "bv", t,
                                       n=P, n0=h2 * P)
                m.then_inc(ev("v"), 1)
                yield 1
                pe.wait_ge(ev(f"k_bd{at.par}"), at.dma(4))
                for t in range(TILES):
                    if t:
                        pe.wait_ge(ev("v_lo"), at.n())
                    o = (bD0, bD1)[t]
                    for c in range(2):
                        for i, (qq, hl) in enumerate(((qh, 0), (qh, 1), (ql, 0))):
                            for b in range(2):
                                tok = slice(t * P + 64 * b, t * P + 64 * b + 64)
                                m = pe.matmul(o[64 * b:64 * b + 64, c * 256:(c + 1) * 256], qq[:, c, tok],
                                              Kbd[:, :, hl, c, tok], start=(i == 0), stop=(i == 2),
                                              skip_group_check=True)
                    m.then_inc(ev("scores"), 1)
                    yield 1
                yield 1
                if at.earlier(1):
                    pe.wait_ge(ev("preF"), at.n(-1))
                for t in range(TILES):
                    pe.wait_ge(ev("exp"), at.tile(t))
                    o = (bF0, bF1)[t]
                    for hp in range(4):
                        m = pe.transpose(o[:, hp * P:(hp + 1) * P],
                                         E[:, t, 2 * hp:2 * hp + 2].rearrange("p h k -> p (h k)"), ident[:])
                    m.then_inc(ev("e_turned"), 1)
                    yield 1

            def stream4(at):
                pe.wait_ge(ev(f"v_bd{at.par}"), at.dma(4))
                for t in range(TILES):
                    pe.wait_ge(ev("pt_lo"), at.tile(t))
                    o = (bF0, bF1)[t]
                    for hp in range(4):
                        for i, (pt, hl) in enumerate(((PTh, 0), (PTh, 1), (PTl, 0))):
                            for b in range(2):
                                m = pe.matmul(o[64 * b:64 * b + 64, hp * 66:(hp + 1) * 66],
                                              pt[:, t, hp, 64 * b:64 * b + 64], Vbd[:, at.par, b, hl, :, 4 * t + hp],
                                              start=(i == 0), stop=(i == 2), skip_group_check=True)
                    m.then_inc(ev("ctx"), 1)
                    yield 1
                pe.wait_ge(ev("cx"), at.tile(1))
                turn(bF0, cx).then_inc(ev("cx_turned"), 1)
                yield 1
                pe.wait_ge(ev("cF_lo"), at.n())
                for t in range(TILES):
                    m = project_tm(bF1[:, t * D:(t + 1) * D], cFh, cFl, Wo, "bo", t)
                m.then_inc(ev("attn_out"), 1)
                yield from rest(4)
                pe.wait_ge(ev("xg"), at.n())
                if at.earlier(1):
                    pe.wait_ge(ev("mixed"), at.n(-1))
                turn(bG, xg).then_inc(ev("xg_turned"), 1)
                yield 1

            def stream5(at):
                pe.wait_ge(ev("xgF_lo"), at.n())
                project_fm(bG, Wqk3, "bqk", xgFh, xgFl).then_inc(ev("qk3"), 1)
                yield 1
                pe.wait_ge(ev("qk_tanh"), at.n())
                for t in range(TILES):
                    m = project_tm(bG[:, t * D:(t + 1) * D], xgFh, xgFl, Wl, None, t)
                m.then_inc(ev("y3"), 1)
                yield 1
                pe.wait_ge(ev("y3_lo"), at.n())
                pe.wait_ge(ev("Q_lo"), at.n())
                for t in range(TILES):
                    tok = slice(t * P, (t + 1) * P)
                    for k in range(2):
                        m = mm3(bG[:, tok], Qh[:, k, tok], Ql[:, k, tok], Qh[:, k, tok], Ql[:, k, tok], k == 0, k == 1)
                m.then_inc(ev("s3"), 1)
                yield 1
                pe.wait_ge(ev("attn"), at.n())
                for t in range(TILES):
                    m = project_tm(bG[:, t * D:(t + 1) * D], xgFh, xgFl, Wr, "bl", t)
                m.then_inc(ev("o2_raw"), 1)
                yield 1
                pe.wait_ge(ev("o2"), at.n())
                pe.wait_ge(ev("attn_lo"), at.n())
                for t in range(TILES):
                    pe.matmul(bG[:, t:t + 1], SAh[:, t], ones16[:, 0:1], start=True, stop=False, skip_group_check=True)
                    m = pe.matmul(bG[:, t:t + 1], SAl[:, t], ones16[:, 0:1], start=False, stop=True,
                                  skip_group_check=True)
                m.then_inc(ev("row_sum"), 1)
                yield 1
                pe.wait_ge(ev("row_scale"), at.chain(2, 1))
                for t in range(TILES):
                    m = mm3(bG[:, t * D:(t + 1) * D], SAh[:, t], SAl[:, t], y3h[:, t], y3l[:, t], True, True)
                m.then_inc(ev("o1"), 1)
                yield 1

            run(pe, [stream0, stream1, stream2, stream3, stream4, stream5])

        @block.scalar
        def _(act):
            def cast(dst, src, scale=1.0):
                return act.activation(dst, src, ACT.Copy, scale=scale)

            def high(i, W, src, then):
                cast(W, src, WS).then_inc(ev("w_hi"), 1)

            act.wait_ge(ev("staged0"), 16)
            cast(W1[:, 0], stage[0][:, 0:2, 0:H1], WS).then_inc(ev("w_hi"), 1)
            act.wait_ge(ev("w2_centred"), 1)
            cast(W2[:, 0], stage[1][:, :, 0:D], WS).then_inc(ev("w_hi"), 1)
            act.wait_ge(ev("setup_pe"), 3)
            cast(Gm[:, 0], bC[:].rearrange("p (c n) -> p c n", c=2), WS).then_inc(ev("w_hi"), 1)
            for i, W in enumerate((Wv1, Wq, Wk, Wv, Wo, Wqk3, Wl, Wr)):
                i += 3
                act.wait_ge(ev(f"staged{i % 2}"), 16 * (i // 2 + 1))
                cast(W[:, 0], stage[i % 2][:, 0:2, 0:D], WS).then_inc(ev("w_hi"), 1)

            def norm(k, dst, at):
                act.wait_ge(ev("rstd" + k), at.chain(3, 3))
                for t in range(TILES):
                    m = act.activation(dst[:, t], pre[k][:, t], ACT.Identity, bias=nb[k][:, t:t + 1],
                                       scale=rs[k][:, t:t + 1])
                m.then_inc(ev("x" + k), 1)

            def stream0(at):
                act.wait_ge(ev(f"x_in{at.par}"), at.dma(1))
                if at.earlier(1):
                    act.wait_ge(ev("z1"), at.n(-1))
                cast(xh[:], xin[:, at.par]).then_inc(ev("x_hi"), 1)
                yield 1
                act.wait_ge(ev("d_inv"), at.chain(3, 3))
                for t in range(TILES):
                    m = act.activation(Pf[:, t], bA[:, t * P:(t + 1) * P], ACT.Copy, scale=Dinv[:, t:t + 1])
                m.then_inc(ev("p_f"), 1)
                yield 1
                act.wait_ge(ev("p_turned0"), at.n())
                cast(Ph[:, at.par].rearrange("p t k -> p (t k)"), bA[:, TOK:2 * TOK]).then_inc(ev("p_hi"), 1)
                yield 1
                act.wait_ge(ev("z1"), at.n())
                cast(z1h[:].rearrange("p c k -> p (c k)"), bA[:]).then_inc(ev("z1_hi"), 1)
                yield 1
                if at.earlier(1):
                    act.wait_ge(ev("r_var"), at.chain(2, 1, -1))
                    act.wait_ge(ev("r_turned"), at.tile(1, -1))
                for t in range(TILES):
                    act.wait_ge(ev("z"), at.tile(t))
                    act.activation(r[:, t], bA[:], ACT.Relu, scale=1.0 / WS).then_inc(ev("relu"), 1)
                    yield 1
                for t in range(TILES):
                    act.wait_ge(ev("r_turned"), at.tile(t))
                    cast(rFh[:, t].rearrange("p c k -> p (c k)"), bB[:]).then_inc(ev("rF_hi"), 1)
                    yield 1

            def stream1(at):
                yield 1
                act.wait_ge(ev("y0_f"), at.n())
                cast(y0h[:], y0[:]).then_inc(ev("y0_hi"), 1)
                yield from rest(3)
                norm("B", x1[:, at.par], at)
                yield 1
                act.wait_ge(ev("x1_turned"), at.n())
                cast(x1Fh[at.par][:].rearrange("p c k -> p (c k)"), bC[:]).then_inc(ev("x1F_hi"), 1)
                yield 1
                act.wait_ge(ev("u"), at.n())
                cast(uh[:].rearrange("p c k -> p (c k)"), bC[:], 1.0 / WS).then_inc(ev("u_hi"), 1)
                yield 1

            def stream2(at):
                yield 1
                act.wait_ge(ev("w_shifted"), at.n())
                act.activation(wex[:], wrm[:], ACT.Exp, scale=SOFT1).then_inc(ev("w_exp"), 1)
                yield from rest(4)
                if at.earlier(2):
                    act.wait_ge(ev("preF"), at.n(-2))
                norm("C", x2[:, at.par], at)
                yield 1
                act.wait_ge(ev("x2_turned"), at.n())
                cast(x2Fh[:].rearrange("p c k -> p (c k)"), bD0[:]).then_inc(ev("x2F_hi"), 1)
                yield 1
                act.wait_ge(ev("q"), at.n())
                cast(qh[:].rearrange("p c k -> p (c k)"), bD1[:], 1.0 / WS).then_inc(ev("q_hi"), 1)
                yield 1

            def stream3(at):
                yield 1
                act.wait_ge(ev("k"), at.n())
                if at.earlier(1):
                    act.wait_ge(ev(f"k_bd{1 - at.par}"), at.before().dma(4))
                cast(kst[:, 0].rearrange("p c k -> p (c k)"), bD0[:], 1.0 / WS).then_inc(ev("k_hi"), 1)
                yield 1
                act.wait_ge(ev("v"), at.n())
                if at.earlier(1):
                    act.wait_ge(ev(f"v_bd{1 - at.par}"), at.before().dma(4))
                cast(vst[:, 0].rearrange("p h e d -> p (h e) d")[:, :, 0:HD],
                     bD1[:].rearrange("p (e d) -> p e d", d=HD), 1.0 / WS).then_inc(ev("v_hi"), 1)
                yield from rest(3)
                for t in range(TILES):
                    act.wait_ge(ev("s_shifted"), at.tile(t))
                    if at.earlier(1):
                        act.wait_ge(ev("e_turned"), at.tile(t, -1))
                    act.activation(E[:, t], Ssb[:, t], ACT.Exp, scale=SOFT2).then_inc(ev("exp"), 1)
                    if t == 0:
                        yield 1
                for t in range(TILES):
                    act.wait_ge(ev("e_turned"), at.tile(t))
                    cast(PTh[:, t].rearrange("p c k -> p (c k)"), (bF0, bF1)[t][:]).then_inc(ev("pt_hi"), 1)
                    yield 1

            def stream4(at):
                yield from rest(2)
                act.wait_ge(ev("cx_turned"), at.n())
                cast(cFh[:].rearrange("p c k -> p (c k)"), bF0[:]).then_inc(ev("cF_hi"), 1)
                yield 1
                act.wait_ge(ev("gate_pre"), at.tile(1))
                act.activation(gt[:], gp[:], ACT.Tanh, scale=0.5).then_inc(ev("gate_tanh"), 1)
                yield 1
                act.wait_ge(ev("gate_tanh"), at.n())
                act.activation(g2[:], gt[:], ACT.Copy, bias=1.0).then_inc(ev("gate"), 1)
                yield 1
                norm("F", x3[:, at.par], at)
                yield from rest(2)
                act.wait_ge(ev("xg_turned"), at.n())
                cast(xgFh[:].rearrange("p c k -> p (c k)"), bG[:], 0.5).then_inc(ev("xgF_hi"), 1)
                yield 1

            def stream5(at):
                act.wait_ge(ev("qk3"), at.n())
                act.activation(qt[:].rearrange("p c k -> p (c k)"), bG[:], ACT.Tanh, scale=0.5 / WS
                               ).then_inc(ev("qk_tanh"), 1)
                yield 1
                act.wait_ge(ev("qk_tanh"), at.n())
                act.activation(Qh[:], qt[:], ACT.Copy, bias=1.0).then_inc(ev("Q_hi"), 1)
                act.wait_ge(ev("y3"), at.n())
                cast(y3h[:].rearrange("p t k -> p (t k)"), bG[:], 1.0 / WS).then_inc(ev("y3_hi"), 1)
                yield from rest(2)
                act.wait_ge(ev("attn"), at.n())
                cast(SAh[:].rearrange("p t k -> p (t k)"), SA[:]).then_inc(ev("attn_hi"), 1)
                act.wait_ge(ev("o2_raw"), at.n())
                if at.earlier(1):
                    act.wait_ge(ev("mixed"), at.n(-1))
                cast(o2[:].rearrange("p t k -> p (t k)"), bG[:], 1.0 / WS).then_inc(ev("o2"), 1)
                yield from rest(4)
                if at.earlier(2):
                    act.wait_ge(ev(f"stored{at.par}"), at.dma(1, -1))
                norm("G", x4[:, at.par], at)
                yield 1

            run(act, [stream0, stream1, stream2, stream3, stream4, stream5])

        @block.vector
        def _(dve):
            def low(dst, src, hi, scale=1.0):
                return dve.scalar_tensor_tensor(out=dst, in0=src, scalar=scale, in1=hi, op0=ALU.mult,
                                                op1=ALU.subtract)

            dve.memset(ones16[:], 1.0).then_inc(ev("const"), 1)
            dve.memset(onesf[:], 1.0).then_inc(ev("const"), 1)
            for buf in (bias, Kbd, Vbd, atA, aC, atG, wpad):
                dve.memset(buf[:], 0.0).then_inc(ev("const"), 1)
            dve.memset(vst[:, 1], 0.0).then_inc(ev("const"), 1)
            dve.memset(vst[:, 0], 1.0).then_inc(ev("const"), 1)
            dve.wait_ge(ev("const"), 11)
            dve.wait_ge(ev("ident"), 3).then_inc(ev("cleared"), 1)

            dve.wait_ge(ev("w_hi"), 1)
            low(W1[:, 1], stage[0][:, 0:2, 0:H1], W1[:, 0], WS).then_inc(ev("unstaged"), 1)
            dve.wait_ge(ev("staged1"), 16)
            dve.wait_ge(ev("small_in"), 16 * 12)
            dve.tensor_copy(stage[1][:, :, D:2 * D], stage[1][:, :, 0:D]).then_inc(ev("setup"), 1)
            dve.wait_ge(ev("setup"), 1)
            for k in range(4):
                m = dve.tensor_scalar(stage[1][:, k, 0:D], stage[1][:, k, D:2 * D], gam[:, k:k + 1], None, ALU.mult)
            m.then_inc(ev("w2_scaled"), 1)
            for k in range(4):
                m = dve.tensor_scalar(betb[:, k], onesf[:], bet[:, k:k + 1], None, ALU.mult)
            m.then_inc(ev("w2_scaled"), 1)
            dve.wait_ge(ev("setup_pe"), 1)
            dve.wait_ge(ev("w2_scaled"), 1)
            for k in range(4):
                m = dve.scalar_tensor_tensor(out=stage[1][:, k, 0:D], in0=bA[:, 0:D], scalar=-1.0 / H1,
                                             in1=stage[1][:, k, 0:D], op0=ALU.mult, op1=ALU.add)
            m.then_inc(ev("w2_centred"), 1)
            dve.wait_ge(ev("setup_pe"), 2)
            dve.tensor_copy(c2[:], bB[:, 0:D])
            dve.wait_ge(ev("w_hi"), 2)
            low(W2[:, 1], stage[1][:, :, 0:D], W2[:, 0], WS).then_inc(ev("unstaged"), 1)
            dve.wait_ge(ev("w_hi"), 3)
            low(Gm[:, 1], bC[:].rearrange("p (c n) -> p c n", c=2), Gm[:, 0], WS).then_inc(ev("unstaged"), 1)
            for i, W in enumerate((Wv1, Wq, Wk, Wv, Wo, Wqk3, Wl, Wr)):
                dve.wait_ge(ev("w_hi"), i + 4)
                low(W[:, 1], stage[(i + 3) % 2][:, 0:2, 0:D], W[:, 0], WS).then_inc(ev("unstaged"), 1)
            for name, (c, w, scale) in BIAS.items():
                m = dve.tensor_scalar(bias[0:2, c:c + w], bias_in[:, c:c + w], scale, None, ALU.mult)
            m.then_inc(ev("setup"), 1)
            dve.wait_ge(ev("setup"), 2)
            for name, (c, w, scale) in BIAS.items():
                m = low(bias_lo[:, c:c + w], bias_in[:, c:c + w], bias[0:2, c:c + w], scale)
            m.then_inc(ev("setup"), 1)
            dve.wait_ge(ev("setup"), 3)
            dve.tensor_copy(bias[0:2, :], bias_lo[:]).then_inc(ev("setup"), 1)
            dve.wait_ge(ev("setup"), 4)
            for name, (c, w, scale) in BIAS.items():
                m = dve.tensor_scalar(bias[0:1, c:c + w], bias_in[0:1, c:c + w], scale, None, ALU.mult)
            m.then_inc(ev("biases"), 1)

            def stats(k, at):
                dve.wait_ge(ev("pre" + k), at.n())
                for t in range(TILES):
                    m = dve.bn_stats(st[k][:, t], pre[k][:, t])
                m.then_inc(ev("var" + k), 1)
                dve.wait_ge(ev("var" + k), at.chain(2, 1)).then_inc(ev("dve_held"), 1)
                for t in range(TILES):
                    m = dve.bn_aggr(mv[k][:, t], st[k][:, t])
                m.then_inc(ev("var" + k), 1)

            def stream0(at):
                dve.wait_ge(ev(f"at_in{at.par}"), at.dma(2))
                dve.tensor_scalar(HT[:], atA[:, at.par], 0.0, None, ALU.not_equal).then_inc(ev("h_t"), 1)
                dve.wait_ge(ev("h_t"), at.n())
                dve.tensor_reduce(cnt[:], HT[:], AX.X, ALU.add).then_inc(ev("b_chain"), 1)
                dve.wait_ge(ev("b_chain"), at.chain(4, 1))
                dve.tensor_scalar(cnt1[:], cnt[:], 1.0, None, ALU.max).then_inc(ev("b_chain"), 1)
                dve.wait_ge(ev("b_chain"), at.chain(4, 2))
                dve.reciprocal(be[:], cnt1[:]).then_inc(ev("b_chain"), 1)
                dve.wait_ge(ev("b_chain"), at.chain(4, 3))
                for t in range(TILES):
                    m = dve.tensor_scalar(HBh[:, t], HT[:, t], be[:, t:t + 1], None, ALU.mult)
                m.then_inc(ev("b_chain"), 1)
                dve.wait_ge(ev("b_chain"), at.chain(4, 4))
                for t in range(TILES):
                    m = low(HBl[:, t], HT[:, t], HBh[:, t], be[:, t:t + 1])
                m.then_inc(ev("hb_lo"), 1)
                yield 1
                dcol = bA[:, TOK:TOK + TILES]
                dve.wait_ge(ev("m_and_d"), at.n())
                dve.tensor_scalar(Dbg[:], dcol, 0.0, HUGE, ALU.is_le, ALU.mult).then_inc(ev("d_inv"), 1)
                dve.wait_ge(ev("d_inv"), at.chain(3, 1))
                dve.tensor_tensor(Dd[:], dcol, Dbg[:], ALU.max).then_inc(ev("d_inv"), 1)
                dve.wait_ge(ev("d_inv"), at.chain(3, 2))
                dve.reciprocal(Dinv[:], Dd[:]).then_inc(ev("d_inv"), 1)
                yield 1
                dve.wait_ge(ev("p_hi"), at.n())
                low(Pl[:, at.par].rearrange("p t k -> p (t k)"), bA[:, TOK:2 * TOK],
                    Ph[:, at.par].rearrange("p t k -> p (t k)")).then_inc(ev("p_lo"), 1)
                yield 1
                dve.wait_ge(ev("z1_hi"), at.n())
                low(z1l[:].rearrange("p c k -> p (c k)"), bA[:], z1h[:].rearrange("p c k -> p (c k)")
                    ).then_inc(ev("z1_lo"), 1)
                yield from rest(3)
                for t in range(TILES):
                    dve.wait_ge(ev("rF_hi"), at.tile(t))
                    low(rFl[:, t].rearrange("p c k -> p (c k)"), bB[:], rFh[:, t].rearrange("p c k -> p (c k)")
                        ).then_inc(ev("rF_lo"), 1)
                    m = dve.bn_stats(rst[:, t], r[:, t])
                    if t:
                        m.then_inc(ev("r_var"), 1)
                        dve.wait_ge(ev("r_var"), at.chain(2, 1)).then_inc(ev("dve_held"), 1)
                        for u in range(TILES):
                            m = dve.bn_aggr(rmv[:, u], rst[:, u])
                        m.then_inc(ev("r_var"), 1)
                    yield 1

            def stream1(at):
                dve.wait_ge(ev("y0_raw"), at.n())
                dve.wait_ge(ev("r_rstd"), at.chain(3, 3))
                for t in range(TILES):
                    m = dve.scalar_tensor_tensor(out=y0[:, t], in0=bB[:, t * D:(t + 1) * D], scalar=rsc[:, t:t + 1],
                                                 in1=c2[:], op0=ALU.mult, op1=ALU.add)
                m.then_inc(ev("y0_f"), 1)
                yield from rest(2)
                dve.wait_ge(ev("conv2"), at.n())
                dve.wait_ge(ev(f"xres_in{at.par}"), at.dma(1))
                dve.scalar_tensor_tensor(out=pre["B"][:].rearrange("p t k -> p (t k)"),
                                         in0=xres[:, at.par].rearrange("p t k -> p (t k)"), scalar=2.0, in1=bB[:],
                                         op0=ALU.mult, op1=ALU.add).then_inc(ev("preB"), 1)
                stats("B", at)
                yield from rest(3)
                dve.wait_ge(ev("x1F_hi"), at.n())
                low(x1Fl[at.par][:].rearrange("p c k -> p (c k)"), bC[:],
                    x1Fh[at.par][:].rearrange("p c k -> p (c k)")).then_inc(ev("x1F_lo"), 1)
                yield 1
                dve.wait_ge(ev("u_hi"), at.n())
                low(ul[:].rearrange("p c k -> p (c k)"), bC[:], uh[:].rearrange("p c k -> p (c k)"), 1.0 / WS
                    ).then_inc(ev("u_lo"), 1)
                yield 1
                dve.wait_ge(ev("uxT"), at.n())
                dve.wait_ge(ev("adj_masked"), at.n())
                for t in range(TILES):
                    tok = slice(t * P, (t + 1) * P)
                    m = dve.tensor_tensor_reduce(wscr[:, tok], bC[:, tok], am[:, tok], 1.0, 0.0, ALU.mult, ALU.add,
                                                 wraw[:, t:t + 1])
                m.then_inc(ev("w_raw"), 1)
                dve.wait_ge(ev("w_raw"), at.n())
                dve.wait_ge(ev(f"C_in{at.par}"), at.dma(4))
                dve.tensor_tensor(wpad[:, 0:TILES], wraw[:], mcol[:, at.par], ALU.mult).then_inc(ev("w_masked"), 1)
                yield 1

            def stream2(at):
                wv = bC[0:TILES, 0:P].rearrange("t (b k) -> t b k", b=2)
                dve.wait_ge(ev("w_turned"), at.n())
                dve.tensor_reduce(wmx[:], wv, AX.X, ALU.max).then_inc(ev("c_softmax"), 1)
                dve.wait_ge(ev("c_softmax"), at.chain(3, 1))
                dve.tensor_tensor(wrm[:], wv, wmx[:].rearrange("t (b o) -> t b o", o=1).broadcast_to(
                    [TILES, 2, NODES]), ALU.subtract).then_inc(ev("w_shifted"), 1)
                yield 1
                dve.wait_ge(ev("w_exp"), at.n())
                dve.tensor_reduce(wsm[:], wex[:], AX.X, ALU.add).then_inc(ev("c_softmax"), 1)
                dve.wait_ge(ev("c_softmax"), at.chain(3, 2))
                dve.reciprocal(wrc[:], wsm[:]).then_inc(ev("c_softmax"), 1)
                dve.wait_ge(ev("c_softmax"), at.chain(3, 3))
                dve.tensor_tensor(wpr[:], wex[:], wrc[:].rearrange("t (b o) -> t b o", o=1).broadcast_to(
                    [TILES, 2, NODES]), ALU.mult).then_inc(ev("w_probs"), 1)
                yield 1
                dve.wait_ge(ev("p_turned"), at.n())
                dve.tensor_scalar(pcol[:], bC[:, 0:TILES], 1.0 / WS, None, ALU.mult).then_inc(ev("p_col"), 1)
                yield 1
                dve.wait_ge(ev("v1"), at.n())
                dve.wait_ge(ev("p_col"), at.n())
                for t in range(TILES):
                    m = dve.scalar_tensor_tensor(out=pre["C"][:, t], in0=bC[:, t * D:(t + 1) * D],
                                                 scalar=pcol[:, t:t + 1], in1=x1[:, at.par, t], op0=ALU.mult,
                                                 op1=ALU.add)
                m.then_inc(ev("preC"), 1)
                stats("C", at)
                yield from rest(3)
                dve.wait_ge(ev("x2F_hi"), at.n())
                low(x2Fl[:].rearrange("p c k -> p (c k)"), bD0[:], x2Fh[:].rearrange("p c k -> p (c k)")
                    ).then_inc(ev("x2F_lo"), 1)
                yield 1
                dve.wait_ge(ev("q_hi"), at.n())
                low(ql[:].rearrange("p c k -> p (c k)"), bD1[:], qh[:].rearrange("p c k -> p (c k)"), 1.0 / WS
                    ).then_inc(ev("q_lo"), 1)
                yield 1

            def stream3(at):
                yield 1
                dve.wait_ge(ev("k_hi"), at.n())
                low(kst[:, 1].rearrange("p c k -> p (c k)"), bD0[:], kst[:, 0].rearrange("p c k -> p (c k)"), 1.0 / WS
                    ).then_inc(ev("k_lo"), 1)
                yield 1
                dve.wait_ge(ev("v_hi"), at.n())
                low(vst[:, 1].rearrange("p h e d -> p (h e) d")[:, :, 0:HD],
                    bD1[:].rearrange("p (e d) -> p e d", d=HD),
                    vst[:, 0].rearrange("p h e d -> p (h e) d")[:, :, 0:HD], 1.0 / WS).then_inc(ev("v_lo"), 1)
                yield 1
                dve.wait_ge(ev(f"acD_in{at.par}"), at.dma(1))
                for t in range(TILES):
                    dve.wait_ge(ev("scores"), at.tile(t))
                    dve.tensor_tensor(Sm[:, t], (bD0, bD1)[t][:].rearrange("p (h k) -> p h k", h=HEADS),
                                      acD[:, at.par, t:t + 1].broadcast_to([P, HEADS, NODES]), ALU.mult
                                      ).then_inc(ev("s_masked"), 1)
                    dve.wait_ge(ev("s_masked"), at.tile(t))
                    dve.tensor_reduce(Smx[:, t], Sm[:, t], AX.X, ALU.max).then_inc(ev("s_max"), 1)
                    yield 1
                yield 1
                for t in range(TILES):
                    dve.wait_ge(ev("pt_hi"), at.tile(t))
                    low(PTl[:, t].rearrange("p c k -> p (c k)"), (bF0, bF1)[t][:],
                        PTh[:, t].rearrange("p c k -> p (c k)")).then_inc(ev("pt_lo"), 1)
                    yield 1

            def stream4(at):
                dve.wait_ge(ev(f"acG_in{at.par}"), at.dma(1))
                dve.tensor_reduce(deg[:], acG[:, at.par], AX.X, ALU.add).then_inc(ev("deg"), 1)
                for t in range(TILES):
                    c = (bF0, bF1)[t][:, 0:HEADS * (HD + 1)].rearrange("p (h d) -> p h d", h=HEADS)
                    dve.wait_ge(ev("ctx"), at.tile(t))
                    dve.reciprocal(rinv[:, t:t + 1].rearrange("p t h -> p h t"), c[:, :, HD:HD + 1]
                                   ).then_inc(ev("rinv"), 1)
                    dve.wait_ge(ev("rinv"), at.tile(t))
                    dve.tensor_tensor(cx[:, t].rearrange("p (h d) -> p h d", h=HEADS), c[:, :, 0:HD],
                                      rinv[:, t:t + 1].rearrange("p t h -> p h t").broadcast_to([P, HEADS, HD]),
                                      ALU.mult).then_inc(ev("cx"), 1)
                    yield 1
                dve.wait_ge(ev("cF_hi"), at.n())
                low(cFl[:].rearrange("p c k -> p (c k)"), bF0[:], cFh[:].rearrange("p c k -> p (c k)")
                    ).then_inc(ev("cF_lo"), 1)
                yield 1
                dve.wait_ge(ev("attn_out"), at.n())
                dve.scalar_tensor_tensor(out=pre["F"][:].rearrange("p t k -> p (t k)"), in0=bF1[:], scalar=1.0 / WS,
                                         in1=x2[:, at.par].rearrange("p t k -> p (t k)"), op0=ALU.mult, op1=ALU.add
                                         ).then_inc(ev("preF"), 1)
                stats("F", at)
                yield from rest(4)
                dve.wait_ge(ev("xgF_hi"), at.n())
                low(xgFl[:].rearrange("p c k -> p (c k)"), bG[:], xgFh[:].rearrange("p c k -> p (c k)"), 0.5
                    ).then_inc(ev("xgF_lo"), 1)
                yield 1

            def stream5(at):
                yield 1
                dve.wait_ge(ev("Q_hi"), at.n())
                dve.scalar_tensor_tensor(out=Ql[:], in0=qt[:], scalar=1.0, in1=Qh[:], op0=ALU.add, op1=ALU.subtract
                                         ).then_inc(ev("Q_lo"), 1)
                dve.wait_ge(ev("y3_hi"), at.n())
                low(y3l[:].rearrange("p t k -> p (t k)"), bG[:], y3h[:].rearrange("p t k -> p (t k)"), 1.0 / WS
                    ).then_inc(ev("y3_lo"), 1)
                yield 1
                dve.wait_ge(ev("s3"), at.n())
                dve.wait_ge(ev(f"atG_in{at.par}"), at.dma(2))
                dve.scalar_tensor_tensor(out=SA[:], in0=bG[:, 0:TOK], scalar=QK3,
                                         in1=atG[:, at.par].rearrange("p t k -> p (t k)"), op0=ALU.mult, op1=ALU.mult
                                         ).then_inc(ev("attn"), 1)
                yield from rest(2)
                dve.wait_ge(ev("row_sum"), at.n())
                dve.tensor_scalar(ssum[:], bG[:, 0:TILES], 1e-6, None, ALU.add).then_inc(ev("row_scale"), 1)
                dve.wait_ge(ev("row_scale"), at.chain(2, 1))
                dve.reciprocal(srec[:], ssum[:]).then_inc(ev("row_scale"), 1)
                yield 1
                dve.wait_ge(ev("o1"), at.n())
                dve.wait_ge(ev("row_scale"), at.chain(2, 2))
                for t in range(TILES):
                    m = dve.scalar_tensor_tensor(out=o3[:, t], in0=bG[:, t * D:(t + 1) * D], scalar=srec[:, t:t + 1],
                                                 in1=o2[:, t], op0=ALU.mult, op1=ALU.add)
                m.then_inc(ev("mixed"), 1)
                dve.wait_ge(ev("mixed"), at.n())
                dve.scalar_tensor_tensor(out=pre["G"][:].rearrange("p t k -> p (t k)"),
                                         in0=o3[:].rearrange("p t k -> p (t k)"), scalar=0.0,
                                         in1=x3[:, at.par].rearrange("p t k -> p (t k)"), op0=ALU.max, op1=ALU.add
                                         ).then_inc(ev("preG"), 1)
                stats("G", at)
                yield 1

            run(dve, [stream0, stream1, stream2, stream3, stream4, stream5])

        @block.gpsimd
        def _(pool):
            pool.memset(powm[:], -0.5).then_inc(ev("ident"), 1)
            pool.memset(ident[:], 0.0).then_inc(ev("ident"), 1)
            pool.wait_ge(ev("ident"), 2)
            pool.affine_select(out=ident[:], in_=ident[:], compare_op=ALU.not_equal, fill=1.0, base=0,
                               pattern=[[-1, P]], channel_multiplier=1).then_inc(ev("ident"), 1)
            pool.wait_ge(ev("ident"), 3)

            def sub(dst, a, b):
                return pool.tensor_tensor(dst, a, b, ALU.subtract)

            def rstd(k, at):
                pool.wait_ge(ev("var" + k), at.chain(2, 2)).then_inc(ev("pool_held"), 1)
                pool.tensor_scalar(ve[k][:], mv[k][:, :, 1], EPS, None, ALU.add).then_inc(ev("rstd" + k), 1)
                pool.wait_ge(ev("rstd" + k), at.chain(3, 1))
                pool.tensor_tensor(rs[k][:], ve[k][:], powm[:], ALU.pow).then_inc(ev("rstd" + k), 1)
                pool.wait_ge(ev("rstd" + k), at.chain(3, 2)).then_inc(ev("pool_held"), 1)
                for t in range(TILES):
                    m = pool.tensor_scalar(nb[k][:, t:t + 1], mv[k][:, t, 0:1], rs[k][:, t:t + 1], -1.0, ALU.mult,
                                           ALU.mult)
                m.then_inc(ev("rstd" + k), 1)

            def stream0(at):
                pool.wait_ge(ev(f"at_in{at.par}"), at.dma(2))
                if at.earlier(1):
                    pool.wait_ge(ev("m_and_d"), at.n(-1))
                pool.tensor_tensor(wcf[:], atA[:, at.par, :, 0], atA[:, at.par, :, 64], ALU.add
                                   ).then_inc(ev("w_lo"), 1)
                pool.wait_ge(ev("w_lo"), at.chain(3, 1)).then_inc(ev("pool_held"), 1)
                pool.tensor_copy(wch[:], wcf[:]).then_inc(ev("w_lo"), 1)
                pool.wait_ge(ev("w_lo"), at.chain(3, 2))
                sub(wcl[:], wcf[:], wch[:]).then_inc(ev("w_lo"), 1)
                yield 1
                pool.wait_ge(ev("x_hi"), at.n())
                sub(xl[:], xin[:, at.par], xh[:]).then_inc(ev("x_lo"), 1)
                yield 1

            def stream1(at):
                pool.wait_ge(ev("r_var"), at.chain(2, 2)).then_inc(ev("pool_held"), 1)
                pool.tensor_scalar(rve[:], rmv[:, :, 1], EPS, None, ALU.add).then_inc(ev("r_rstd"), 1)
                pool.wait_ge(ev("r_rstd"), at.chain(3, 1))
                pool.tensor_tensor(rrs[:], rve[:], powm[:], ALU.pow).then_inc(ev("r_rstd"), 1)
                pool.wait_ge(ev("r_rstd"), at.chain(3, 2)).then_inc(ev("pool_held"), 1)
                pool.tensor_scalar(rsc[:], rrs[:], 1.0 / WS, None, ALU.mult).then_inc(ev("r_rstd"), 1)
                yield 1
                pool.wait_ge(ev("y0_hi"), at.n())
                sub(y0l[:], y0[:], y0h[:]).then_inc(ev("y0_lo"), 1)
                yield from rest(2)
                rstd("B", at)
                yield from rest(2)
                pool.wait_ge(ev(f"C_in{at.par}"), at.dma(4))
                if at.earlier(1):
                    pool.wait_ge(ev("w_raw"), at.n(-1))
                pool.tensor_tensor(am[:], aC[:, at.par].rearrange("p t k -> p (t k)"), mrow[:, at.par], ALU.mult
                                   ).then_inc(ev("adj_masked"), 1)
                yield 1

            def stream2(at):
                yield from rest(4)
                rstd("C", at)
                yield 1

            def stream3(at):
                yield from rest(4)
                for t in range(TILES):
                    pool.wait_ge(ev("s_max"), at.tile(t))
                    if at.earlier(1):
                        pool.wait_ge(ev("exp"), at.tile(t, -1))
                    pool.tensor_tensor(Ssb[:, t], Sm[:, t], Smx[:, t:t + 1].rearrange("p t h -> p h t").broadcast_to(
                        [P, HEADS, NODES]), ALU.subtract).then_inc(ev("s_shifted"), 1)
                    yield 1

            def stream4(at):
                yield 1
                pool.wait_ge(ev("deg"), at.n()).then_inc(ev("pool_held"), 1)
                for t in range(TILES):
                    m = pool.tensor_scalar(gw[:, t], wdb[:], deg[:, t:t + 1], None, ALU.mult)
                m.then_inc(ev("gate_pre"), 1)
                yield 1
                pool.wait_ge(ev("gate_pre"), at.tile(0))
                pool.tensor_tensor(gp[:], gw[:], bdb[:].rearrange("p (o d) -> p o d", o=1).broadcast_to(
                    [P, TILES, D]), ALU.add).then_inc(ev("gate_pre"), 1)
                yield from rest(2)
                rstd("F", at)
                yield from rest(2)
                pool.wait_ge(ev("xF"), at.n())
                pool.tensor_tensor(xg[:], g2[:], x3[:, at.par], ALU.mult).then_inc(ev("xg"), 1)
                yield 1

            def stream5(at):
                yield from rest(3)
                pool.wait_ge(ev("attn_hi"), at.n())
                sub(SAl[:].rearrange("p t k -> p (t k)"), SA[:], SAh[:].rearrange("p t k -> p (t k)")
                    ).then_inc(ev("attn_lo"), 1)
                yield from rest(3)
                rstd("G", at)
                yield 1

            run(pool, [stream0, stream1, stream2, stream3, stream4, stream5])


def kernel(**inputs):
    import numpy as np
    import concourse.bacc as bacc
    from concourse.bass_utils import run_bass_kernel_spmd

    a = {k: np.ascontiguousarray(v) for k, v in inputs.items()}

    def turned(w):
        return np.ascontiguousarray(w.T)

    even_odd = np.arange(D).reshape(4, 2, HD).transpose(1, 0, 2).reshape(-1)
    arrays = {
        "x": a["x"].reshape(GRAPHS * NODES, D), "adj": a["adj"],
        "adj_t": np.ascontiguousarray(a["adj"].transpose(0, 2, 1)), "mask": a["nodemask"].reshape(-1),
        "mask_col": np.ascontiguousarray(a["nodemask"].reshape(GROUPS, TILES, P).transpose(0, 2, 1)),
        "w1t": turned(a["L0_gnn_W1"]), "b1": a["L0_gnn_b1"], "gamma": turned(a["L0_gnn_gamma"].reshape(4, P)),
        "beta": turned(a["L0_gnn_beta"].reshape(4, P)),
        "w2t": turned(a["L0_gnn_W2"]), "b2": a["L0_gnn_b2"],
        "wqk1t": turned(a["L1_gnn_Wqk"]), "wv1": a["L1_gnn_Wv"],
        "wqt": turned(a["L2_gnn_Wq"]), "bq": a["L2_gnn_bq"], "wkt": turned(a["L2_gnn_Wk"]), "bk": a["L2_gnn_bk"],
        "wvt": np.ascontiguousarray(turned(a["L2_gnn_Wv"])[:, even_odd]),
        "bv": np.ascontiguousarray(a["L2_gnn_bv"][even_odd]),
        "wot": turned(a["L2_gnn_Wo"]), "bo": a["L2_gnn_bo"],
        "wqk3t": turned(a["L3_gnn_Wqk"]), "bqk": a["L3_gnn_bqk"], "wlt": turned(a["L3_gnn_Wl"]), "bl": a["L3_gnn_bl"],
        "wrt": turned(a["L3_gnn_Wr"]), "wd": a["L3_gnn_Wd"].reshape(-1), "bd": a["L3_gnn_bd"],
    }
    nc = bacc.Bacc("TRN2", target_bir_lowering=False, num_devices=1)
    args = [nc.dram_tensor(n, v.shape, mybir.dt.from_np(v.dtype), kind="ExternalInput").ap()
            for n, v in arrays.items()]
    args.append(nc.dram_tensor("out", (GRAPHS * NODES, D), F32, kind="ExternalOutput").ap())
    build(nc, *args)
    res = run_bass_kernel_spmd(nc, [arrays], core_ids=[0])
    return res.results[0]["out"].reshape(GRAPHS, NODES, D)
```

```python
from contextlib import ExitStack

import concourse.bass as bass
from concourse import mybir

F32 = mybir.dt.float32
F16 = mybir.dt.float16
ALU = mybir.AluOpType
ACT = mybir.ActivationFunctionType
AX = mybir.AxisListType

P = 128
GRAPHS, NODES, D = 128, 64, 256
H1 = 512
TILES = 2
TOK = TILES * P
GROUPS = GRAPHS * NODES // TOK
HEADS, HD = 8, D // 8
WS = 16.0
EPS = 1e-5
SOFT1 = 1.0 / 16.0
SOFT2 = 2.0 * HD ** -0.5 / (WS * WS)
QK3 = 0.25 / 16.0
HUGE = 3e38
ORDER_PE = [4, 2, 5, 4, 1, 3, 0, 5, 4, 3, 2, 0, 1, 5, 0, 2, 4, 0, 0, 5, 3, 1, 5, 3, 5, 2, 1, 3, 2, 1, 0, 3, 4, 0]
ORDER_ACT = [5, 0, 4, 2, 5, 1, 3, 5, 0, 4, 0, 3, 4, 0, 5, 4, 1, 0, 0, 0, 5, 2, 1, 0, 0, 0, 2, 3, 1, 4, 3, 2, 4, 3, 5]
ORDER_DVE = [0, 4, 0, 4, 0, 4, 0, 2, 0, 2, 4, 0, 1, 4, 2, 0, 0, 0, 2, 2, 5, 3, 5, 2, 4, 0, 1, 5, 1, 1, 0, 2, 2, 4, 2, 4, 4, 3, 3, 5, 3, 3, 1, 3, 5, 2, 5, 1, 0, 5, 5, 5, 3, 1, 1, 0, 4, 2, 0, 3, 0]
ORDER_POOL = [0, 0, 0, 1, 4, 1, 0, 3, 1, 1, 5, 1, 2, 2, 4, 2, 4, 0, 5, 3, 4, 0, 3, 0, 4, 1, 5, 5, 5, 0, 0, 0]

LAST_LAG = 5
STEPS = GROUPS + LAST_LAG
SMALL_INPUTS = 12


def build(nc, x, adj, adj_t, mask, mask_col, w1t, b1, gamma, beta, w2t, b2, wqk1t, wv1, wqt, bq, wkt, bk, wvt, bv,
          wot, bo, wqk3t, bqk, wlt, bl, wrt, wd, bd, out):
    ctx = ExitStack()
    with ctx:
        def sb(name, shape, dt=F32):
            return ctx.enter_context(nc.sbuf_tensor(name, shape, dt))

        sems = {}

        def ev(name):
            if name not in sems:
                sems[name] = ctx.enter_context(nc.semaphore(name))
            return sems[name]

        bank = [ctx.enter_context(nc.psum_tensor(f"bank{i}", [P, 512], F32)) for i in range(8)]
        bA, bB, bC, bD0, bD1, bF0, bF1, bG = bank

        ident = sb("ident", [P, P])
        ones16 = sb("ones16", [P, 1], F16)
        onesf = sb("onesf", [P, P])
        powm = sb("powm", [P, TILES])
        b1c = sb("b1c", [P, 4])
        bqc = sb("bqc", [P, 2])
        bkc = sb("bkc", [P, 2])
        bqkc = sb("bqkc", [P, 2])
        bvc = sb("bvc", [P, 2])
        b2b = sb("b2b", [P, D])
        bob = sb("bob", [P, D])
        blb = sb("blb", [P, D])

        def weight(name, chunks, n):
            return sb(name, [P, 2, chunks, n], F16)

        W1 = weight("W1", 2, H1)
        W2 = weight("W2", 4, D)
        Gm = weight("Gm", 2, D)
        Wv1 = weight("Wv1", 2, D)
        Wq = weight("Wq", 2, D)
        Wk = weight("Wk", 2, D)
        Wv = weight("Wv", 2, D)
        Wo = weight("Wo", 2, D)
        Wqk3 = weight("Wqk3", 2, D)
        Wl = weight("Wl", 2, D)
        Wr = weight("Wr", 2, D)
        c2 = sb("c2", [P, D])
        wdb = sb("wdb", [P, D])
        bdb = sb("bdb", [P, D])
        gam = sb("gam", [P, 4])
        bet = sb("bet", [P, 4])
        betb = sb("betb", [P, 4, P])

        late = [sb("late0", [P, 2, 4, 512]), sb("late1", [P, 5, TILES, D])]
        r = sb("r", [P, 4, TOK])
        rsq = sb("rsq", [P, 4, TOK])
        w2_stage = late[0][:, 1]
        stages = {"W1": late[0][:, 0, 0:2], "W2": w2_stage[:, :, 0:D],
                  "Wqk1": late[0][:, 0, 2:4].rearrange("p a (b n) -> p (a b) n", b=2),
                  "Wqk3": r[:, 0:2], "Wl": r[:, 2:4], "Wr": rsq[:, 0:2]}
        for i, name in enumerate(("Wv1", "Wq", "Wk", "Wv", "Wo")):
            stages[name] = late[1][:, i]
        x3, x4, Sm, Ssb = [late[0][:, i, 2 * k:2 * k + 2] for i in range(2) for k in range(2)]
        x3, x4 = [v.rearrange("p a (t d) -> p a t d", t=TILES) for v in (x3, x4)]
        cx, gw, xg, o2, o3 = [late[1][:, i] for i in range(5)]
        Sm, Ssb = [v.rearrange("p t (h k) -> p t h k", h=HEADS) for v in (Sm, Ssb)]

        xin = sb("xin", [P, 2, TILES, D])
        atA = sb("atA", [P, 2, TILES, P])
        xh = sb("xh", [P, TILES, D], F16)
        xl = sb("xl", [P, TILES, D], F16)
        HT = sb("HT", [P, TILES, P], F16)
        cnt = sb("cnt", [P, TILES])
        cnt1 = sb("cnt1", [P, TILES])
        be = sb("be", [P, TILES])
        HBh = sb("HBh", [P, TILES, P], F16)
        HBl = sb("HBl", [P, TILES, P], F16)
        wcf = sb("wcf", [P, TILES])
        wch = sb("wch", [P, TILES], F16)
        wcl = sb("wcl", [P, TILES], F16)
        Dbg = sb("Dbg", [P, TILES])
        Dd = sb("Dd", [P, TILES])
        Dinv = sb("Dinv", [P, TILES])
        Pf = sb("Pf", [P, TILES, P])
        Ph = sb("Ph", [P, 2, TILES, P], F16)
        Pl = sb("Pl", [P, 2, TILES, P], F16)
        z1h = sb("z1h", [P, 2, TOK], F16)
        z1l = sb("z1l", [P, 2, TOK], F16)

        xres = sb("xres", [P, 2, TILES, D])
        rFh = sb("rFh", [P, 4, TOK], F16)
        rFl = sb("rFl", [P, 4, TOK], F16)
        rmean = sb("rmean", [P, TILES])
        rmm = sb("rmm", [P, TILES])
        rvar = sb("rvar", [P, TILES])
        rve = sb("rve", [P, TILES])
        rrs = sb("rrs", [P, TILES])
        rsc = sb("rsc", [P, TILES])
        y0 = sb("y0", [P, TILES, D])
        y0h = sb("y0h", [P, TILES, D], F16)
        y0l = sb("y0l", [P, TILES, D], F16)

        pre, st, mv, ve, rs, nb = {}, {}, {}, {}, {}, {}
        for k in "BCFG":
            pre[k] = sb("pre" + k, [P, TILES, D])
            st[k] = sb("st" + k, [P, TILES, 6])
            mv[k] = sb("mv" + k, [P, TILES, 2])
            ve[k] = sb("ve" + k, [P, TILES])
            rs[k] = sb("rs" + k, [P, TILES])
            nb[k] = sb("nb" + k, [P, TILES])
        x1 = sb("x1", [P, 2, TILES, D])
        x2 = sb("x2", [P, TILES, D])
        x2b = sb("x2b", [P, 2, TILES, D])

        aC = sb("aC", [P, 2, TILES, P])
        mrow = sb("mrow", [P, 2, TOK])
        mcol = sb("mcol", [P, 2, TILES])
        am = sb("am", [P, TOK])
        x1Fh = [sb(f"x1Fh{i}", [P, 2, TOK], F16) for i in range(2)]
        x1Fl = [sb(f"x1Fl{i}", [P, 2, TOK], F16) for i in range(2)]
        uh = sb("uh", [P, 2, TOK], F16)
        ul = sb("ul", [P, 2, TOK], F16)
        wscr = sb("wscr", [P, TOK])
        wraw = sb("wraw", [P, TILES])
        wpad = sb("wpad", [P, P])
        wrm = sb("wrm", [TILES, 2, NODES])
        wmx = sb("wmx", [TILES, 2])
        wex = sb("wex", [TILES, 2, NODES])
        wsm = sb("wsm", [TILES, 2])
        wrc = sb("wrc", [TILES, 2])
        wpr = sb("wpr", [TILES, 2, NODES])
        pcol = sb("pcol", [P, TILES])

        acD = sb("acD", [P, 2, TILES, NODES])
        x2Fh = sb("x2Fh", [P, 2, TOK], F16)
        x2Fl = sb("x2Fl", [P, 2, TOK], F16)
        qh = sb("qh", [P, 2, TOK], F16)
        ql = sb("ql", [P, 2, TOK], F16)
        kst = sb("kst", [P, 2, 2, TOK], F16)
        Kbd = sb("Kbd", [P, 4, 2, 2, TOK], F16)
        vst = sb("vst", [P, 2, 2, TILES * 4, HD + 1], F16)
        Vbd = sb("Vbd", [P, 2, 2, 2, 2, TILES * 4, HD + 1], F16)
        Smx = sb("Smx", [P, TILES, HEADS])
        E = sb("E", [P, TILES, HEADS, NODES])

        PTh = sb("PTh", [P, TILES, 4, P], F16)
        PTl = sb("PTl", [P, TILES, 4, P], F16)
        rinv = sb("rinv", [P, TILES, HEADS])
        cFh = sb("cFh", [P, 2, TOK], F16)
        cFl = sb("cFl", [P, 2, TOK], F16)

        atG = sb("atG", [P, 2, TILES, P])
        acG = sb("acG", [P, 2, TILES, NODES])
        deg = sb("deg", [P, TILES])
        gp = sb("gp", [P, TILES, D])
        gt = sb("gt", [P, TILES, D])
        g2 = sb("g2", [P, TILES, D])
        xgFh = sb("xgFh", [P, 2, TOK], F16)
        xgFl = sb("xgFl", [P, 2, TOK], F16)
        qt = sb("qt", [P, 2, TOK])
        Qh = sb("Qh", [P, 2, TOK], F16)
        Ql = sb("Ql", [P, 2, TOK], F16)
        SA = sb("SA", [P, TOK])
        SAh = sb("SAh", [P, TILES, P], F16)
        SAl = sb("SAl", [P, TILES, P], F16)
        ssum = sb("ssum", [P, TILES])
        srec = sb("srec", [P, TILES])
        y3h = sb("y3h", [P, TILES, D], F16)
        y3l = sb("y3l", [P, TILES, D], F16)

        class At:

            def __init__(self, stream, j, fixed):
                self.j, self.fixed = j, fixed - stream
                self.par = self.fixed % 2

            def n(self, d=0):
                return 2 * self.j + (self.fixed + 1 + d) if self.j is not None else self.fixed + 1 + d

            def tile(self, t, d=0):
                k = 2 * (self.fixed + d) + t + 1
                return 4 * self.j + k if self.j is not None else k

            def chain(self, per, i, d=0):
                k = per * (self.fixed + d) + i
                return 2 * per * self.j + k if self.j is not None else k

            def dma(self, per, d=0):
                k = (self.fixed >> 1) + 1 + d
                return self.j * (16 * per) + 16 * per * k if self.j is not None else 16 * per * k

            def before(self):
                return At(0, self.j, self.fixed - 1)

            def group(self):
                return 2 * self.j + self.fixed if self.j is not None else self.fixed

            def earlier(self, d):
                return self.j is not None or self.fixed >= d

        def run(eng, order, streams):
            def step(j, s, lo, hi):
                live = {k: streams[k](At(k, j, s)) for k in range(lo, hi + 1)}
                for k in order:
                    if k in live:
                        next(live[k], None)
                assert all(next(live[k], "end") == "end" for k in live)

            first = LAST_LAG + 1
            last = first + (GROUPS - first) // 2 * 2
            for s in range(first):
                step(None, s, 0, s)
            with eng.Fori(first // 2, last // 2) as j:
                for par in range(2):
                    step(j, par, 0, LAST_LAG)
            for s in range(last, STEPS):
                step(None, s, max(0, s - GROUPS + 1), LAST_LAG)


        block = ctx.enter_context(nc.Block())

        def arrival(name):
            return ("w2_in", 16) if name == "W2" else ("first_in", 48) if name in ("W1", "Wqk1", "Wv1") else (
                "rest_in", 16 * (len(weights_in) - 4))

        weights_in = [
            ("W1", w1t, 2, H1), ("W2", w2t, 4, D), ("Wqk1", wqk1t, 4, D), ("Wv1", wv1, 2, D), ("Wq", wqt, 2, D),
            ("Wk", wkt, 2, D), ("Wv", wvt, 2, D), ("Wo", wot, 2, D), ("Wqk3", wqk3t, 2, D), ("Wl", wlt, 2, D),
            ("Wr", wrt, 2, D)]

        @block.sync
        def _(sp):
            def blocks(dst, src, at, name):
                v = src.rearrange("(g t b) i j -> b g i t j", t=TILES, b=2)
                for b in range(2):
                    sp.dma_start(dst[64 * b:64 * b + 64, at.par, :, 64 * b:64 * b + 64],
                                 v[b, bass.ds(at.group(), 1)].rearrange("g i t j -> (g i) t j")
                                 ).then_inc(ev(f"{name}{at.par}"), 16)

            xv = x.rearrange("(g t p) d -> g p t d", t=TILES, p=P)
            ov = out.rearrange("(g t p) d -> g p t d", t=TILES, p=P)
            av = adj.rearrange("(g t b) i j -> g (b i) t j", t=TILES, b=2)
            mr = mask.rearrange("(g o k) -> g o k", o=1, k=TOK)

            def at_group(v, at):
                return v[bass.ds(at.group(), 1)].rearrange("g p t d -> (g p) t d")

            def load_conv(at):
                if at.earlier(2):
                    sp.wait_ge(ev("x_lo"), at.n(-2)).then_inc(ev("sp_held"), 1)
                sp.dma_start(xin[:, at.par], at_group(xv, at)).then_inc(ev(f"x_in{at.par}"), 16)
                if at.earlier(2):
                    sp.wait_ge(ev("h_t"), at.n(-2)).then_inc(ev("sp_held"), 1)
                    sp.wait_ge(ev("w_lo"), at.chain(3, 3, -2)).then_inc(ev("sp_held"), 1)
                blocks(atA, adj_t, at, "at_in")

            def load_residual(at):
                if at.earlier(2):
                    sp.wait_ge(ev("preB"), at.n(-2)).then_inc(ev("sp_held"), 1)
                sp.dma_start(xres[:, at.par], at_group(xv, at)).then_inc(ev(f"xres_in{at.par}"), 16)

            def load_layer1(at):
                if at.earlier(2):
                    sp.wait_ge(ev("adj_masked"), at.n(-2)).then_inc(ev("sp_held"), 1)
                    sp.wait_ge(ev("w_masked"), at.n(-2)).then_inc(ev("sp_held"), 1)
                blocks(aC, adj, at, "C_in")
                sp.dma_start(mrow[:, at.par], mr[bass.ds(at.group(), 1)].rearrange("g o k -> (g o) k")
                             .broadcast_to([P, TOK])).then_inc(ev(f"C_in{at.par}"), 16)
                sp.dma_start(mcol[:, at.par], mask_col[bass.ds(at.group(), 1)].rearrange("g p t -> (g p) t")
                             ).then_inc(ev(f"C_in{at.par}"), 16)

            def load_layer2(at):
                if at.earlier(2):
                    sp.wait_ge(ev("s_masked"), at.tile(1, -2)).then_inc(ev("sp_held"), 1)
                sp.dma_start(acD[:, at.par], at_group(av, at)).then_inc(ev(f"acD_in{at.par}"), 16)

            def load_gate(at):
                if at.earlier(2):
                    sp.wait_ge(ev("deg"), at.n(-2)).then_inc(ev("sp_held"), 1)
                sp.dma_start(acG[:, at.par], at_group(av, at)).then_inc(ev(f"acG_in{at.par}"), 16)

            def load_layer3(at):
                if at.earlier(2):
                    sp.wait_ge(ev("attn"), at.n(-2)).then_inc(ev("sp_held"), 1)
                blocks(atG, adj_t, at, "atG_in")

            loads = [load_conv, load_residual, None, load_layer2, load_gate, load_layer3]

            def place_k(at):
                sp.wait_ge(ev("k_lo"), at.n()).then_inc(ev("sp_held"), 1)
                if at.earlier(1):
                    sp.wait_ge(ev("scores"), at.tile(1, -1)).then_inc(ev("sp_held"), 1)
                for h in range(4):
                    sp.dma_start(Kbd[32 * h:32 * h + 32, h], kst[32 * h:32 * h + 32]
                                 ).then_inc(ev(f"k_bd{at.par}"), 16)

            def place_v(at):
                sp.wait_ge(ev("v_lo"), at.n()).then_inc(ev("sp_held"), 1)
                if at.earlier(2):
                    sp.wait_ge(ev("ctx"), at.tile(1, -2)).then_inc(ev("sp_held"), 1)
                for b in range(2):
                    for h2 in range(2):
                        sp.dma_start(Vbd[64 * h2:64 * h2 + 64, at.par, b, :, h2], vst[64 * b:64 * b + 64, :, h2]
                                     ).then_inc(ev(f"v_bd{at.par}"), 16)

            def store(at):
                sp.wait_ge(ev("xG"), at.n()).then_inc(ev("sp_held"), 1)
                sp.dma_start(at_group(ov, at), x4[:, at.par]).then_inc(ev(f"stored{at.par}"), 16)

            def stage_in(i):
                name, src, chunks, n = weights_in[i]
                sp.dma_start(stages[name], src.rearrange("(c p) n -> p c n", p=P)).then_inc(
                    ev(arrival(name)[0]), 16)

            small = [(gam[:], gamma), (bet[:], beta),
                     (wdb[:], wd.rearrange("(o d) -> o d", o=1).broadcast_to([P, D])),
                     (bdb[:], bd.rearrange("(o d) -> o d", o=1).broadcast_to([P, D])),
                     (b2b[:], b2.rearrange("(o d) -> o d", o=1).broadcast_to([P, D])),
                     (bob[:], bo.rearrange("(o d) -> o d", o=1).broadcast_to([P, D])),
                     (blb[:], bl.rearrange("(o d) -> o d", o=1).broadcast_to([P, D])),
                     (b1c[:], b1), (bqc[:], bq), (bkc[:], bk), (bqkc[:], bqk), (bvc[:], bv)]
            assert len(small) == SMALL_INPUTS
            stage_in(1)
            for dst, src in small:
                sp.dma_start(dst, src).then_inc(ev("small_in"), 16)
            stage_in(0)
            for i in range(2, len(weights_in)):
                stage_in(i)
            sp.wait_ge(ev("cleared"), 1)
            load_conv(At(0, None, 0))
            load_layer1(At(0, None, 0))

            def step(j, s):
                def there(at):
                    return j is not None or 0 <= at.fixed < GROUPS

                at = At(3, j, s)
                if there(at):
                    place_k(at)
                for k, load in enumerate(loads):
                    at = At(k, j, s + 1)
                    if load and there(at):
                        load(at)
                at = At(1, j, s + 1)
                if there(at) and (j is not None or at.fixed > 0):
                    load_layer1(at)
                at = At(3, j, s)
                if there(at):
                    place_v(at)
                at = At(5, j, s)
                if there(at):
                    store(at)

            first = LAST_LAG + 1
            last = first + (GROUPS - first) // 2 * 2 - 2
            for s in range(first):
                step(None, s)
            with sp.Fori(first // 2, last // 2) as j:
                for par in range(2):
                    step(j, par)
            for s in range(last, STEPS):
                step(None, s)
            for par in range(2):
                sp.wait_ge(ev(f"stored{par}"), 16 * (GROUPS // 2))

        splits = [("W1", W1), ("Wv1", Wv1), ("Wqk1", Gm), ("W2", W2), ("Wq", Wq), ("Wk", Wk), ("Wv", Wv), ("Wo", Wo),
                  ("Wqk3", Wqk3), ("Wl", Wl), ("Wr", Wr)]
        split_from = dict(stages)
        split_from["Wqk1"] = bC[:].rearrange("p (c n) -> p c n", c=2)

        @block.tensor
        def _(pe):
            def mm3(o, sh, sl, mh, ml, start, stop):
                pe.matmul(o, sh, mh, start=start, stop=False, skip_group_check=True)
                pe.matmul(o, sh, ml, start=False, stop=False, skip_group_check=True)
                return pe.matmul(o, sl, mh, start=False, stop=stop, skip_group_check=True)

            def project_fm(o, W, ah, al, chunks=(0, 1)):
                for i, c in enumerate(chunks):
                    oc = o[:, i * TOK:(i + 1) * TOK]
                    cols = slice(c * P, (c + 1) * P)
                    for k in range(2):
                        m = mm3(oc, W[:, 0, k, cols], W[:, 1, k, cols], ah[:, k], al[:, k], k == 0, k == 1)
                return m

            def project_tm(o, ah, al, W, t, chunks=2, n=D, n0=0):
                tok = slice(t * P, (t + 1) * P)
                for k in range(chunks):
                    m = mm3(o, ah[:, k, tok], al[:, k, tok], W[:, 0, k, n0:n0 + n], W[:, 1, k, n0:n0 + n],
                            k == 0, k == chunks - 1)
                return m

            def turn(o, src, ident_=ident):
                for c in range(2):
                    for t in range(TILES):
                        m = pe.transpose(o[:, c * TOK + t * P:c * TOK + (t + 1) * P], src[:, t, c * P:(c + 1) * P],
                                         ident_[:])
                return m

            pe.wait_ge(ev("w2_scaled"), 1)
            for k in range(4):
                m = pe.matmul(bA[:, 0:D], onesf[:], w2_stage[:, k, 0:D], start=(k == 0), stop=(k == 3))
            m.then_inc(ev("setup_pe"), 1)
            pe.wait_ge(ev("w2_scaled"), 2)
            for k in range(4):
                m = pe.matmul(bB[:, 0:D], betb[:, k], w2_stage[:, k, D:2 * D], start=(k == 0), stop=(k == 3))
            m.then_inc(ev("setup_pe"), 1)
            pe.wait_ge(ev("first_in"), 48)
            for c in range(2):
                for k in range(2):
                    m = pe.matmul(bC[:, c * D:(c + 1) * D], stages["Wqk1"][:, k, c * P:(c + 1) * P],
                                  stages["Wqk1"][:, 2 + k],
                                  start=(k == 0), stop=(k == 1))
            m.then_inc(ev("setup_pe"), 1)
            pe.wait_ge(ev("rest_in"), arrival("Wo")[1])
            pe.wait_ge(ev("small_in"), 16 * SMALL_INPUTS)
            for c in range(2):
                m = pe.matmul(bD0[:, 0:D], bvc[:, c:c + 1].broadcast_to([P, P]), stages["Wo"][:, c],
                              start=(c == 0), stop=(c == 1))
            m.then_inc(ev("setup_pe"), 1)
            pe.wait_ge(ev("unstaged"), len(weights_in))

            def stream0(at):
                pe.wait_ge(ev("hb_lo"), at.n())
                if at.earlier(1):
                    pe.wait_ge(ev("r_mean"), at.chain(3, 3, -1))
                for t in range(TILES):
                    o = bA[:, t * P:(t + 1) * P]
                    pe.matmul(o, HT[:, t], HBh[:, t], start=True, stop=False, skip_group_check=True)
                    pe.matmul(o, HT[:, t], HBl[:, t], start=False, stop=True, skip_group_check=True)
                pe.wait_ge(ev("w_lo"), at.chain(3, 3))
                for t in range(TILES):
                    o = bA[:, TOK + t:TOK + t + 1]
                    pe.matmul(o, HT[:, t], wch[:, t:t + 1], start=True, stop=False, skip_group_check=True)
                    m = pe.matmul(o, HT[:, t], wcl[:, t:t + 1], start=False, stop=True, skip_group_check=True)
                m.then_inc(ev("m_and_d"), 1)
                yield
                pe.wait_ge(ev("p_f"), at.n())
                for t in range(TILES):
                    m = pe.transpose(bA[:, TOK + t * P:TOK + (t + 1) * P], Pf[:, t], ident[:])
                m.then_inc(ev("p_turned0"), 1)
                yield
                pe.wait_ge(ev("p_lo"), at.n())
                pe.wait_ge(ev("x_lo"), at.n())
                for c in range(2):
                    for t in range(TILES):
                        m = mm3(bA[:, c * TOK + t * P:c * TOK + (t + 1) * P], xh[:, t, c * P:(c + 1) * P],
                                xl[:, t, c * P:(c + 1) * P], Ph[:, at.par, t], Pl[:, at.par, t], True, True)
                m.then_inc(ev("z1"), 1)
                yield
                pe.wait_ge(ev("z1_lo"), at.n())
                project_fm(bA, W1, z1h, z1l, (0, 1)).then_inc(ev("z"), 1)
                yield
                if at.earlier(1):
                    pe.wait_ge(ev("preB"), at.n(-1))
                project_fm(bB, W1, z1h, z1l, (2, 3)).then_inc(ev("z"), 1)
                yield
                pe.wait_ge(ev("rF_lo0"), at.n())
                pe.wait_ge(ev("rF_lo1"), at.n())
                pe.wait_ge(ev("sq_sum"), at.tile(1))
                pe.wait_ge(ev("relu"), at.tile(1))
                for t in range(TILES):
                    tok = slice(t * P, (t + 1) * P)
                    for k in range(4):
                        pe.matmul(bA[:, t:t + 1], rFh[:, k, tok], ones16[:], start=(k == 0), stop=False,
                                  skip_group_check=True)
                        pe.matmul(bA[:, t:t + 1], rFl[:, k, tok], ones16[:], start=False, stop=(k == 3),
                                  skip_group_check=True)
                    m = pe.matmul(bA[:, TILES + t:TILES + t + 1], rsq[:, 0, tok], onesf[:, 0:1], start=True,
                                  stop=True, skip_group_check=True)
                m.then_inc(ev("r_sums"), 1)
                yield
                project_tm(bB[:, 0:D], rFh, rFl, W2, 0, chunks=4)
                yield

            def stream1(at):
                project_tm(bB[:, D:2 * D], rFh, rFl, W2, 1, chunks=4).then_inc(ev("y0_raw"), 1)
                yield
                pe.wait_ge(ev("y0_lo"), at.n())
                for t in range(TILES):
                    m = mm3(bB[:, t * D:(t + 1) * D], Ph[:, at.par, t], Pl[:, at.par, t], y0h[:, t], y0l[:, t],
                            True, True)
                m.then_inc(ev("conv2"), 1)
                yield
                pe.wait_ge(ev("xB"), at.n())
                if at.earlier(1):
                    pe.wait_ge(ev("preC"), at.n(-1))
                turn(bC, x1[:, at.par]).then_inc(ev("x1_turned"), 1)
                yield
                pe.wait_ge(ev("x1F_lo"), at.n())
                project_fm(bC, Gm, x1Fh[at.par], x1Fl[at.par]).then_inc(ev("u"), 1)
                yield
                pe.wait_ge(ev("u_lo"), at.n())
                for t in range(TILES):
                    tok = slice(t * P, (t + 1) * P)
                    for k in range(2):
                        m = mm3(bC[:, tok], uh[:, k, tok], ul[:, k, tok], x1Fh[at.par][:, k, tok],
                                x1Fl[at.par][:, k, tok], k == 0, k == 1)
                m.then_inc(ev("uxT"), 1)
                yield

            def stream2(at):
                pe.wait_ge(ev("w_masked"), at.n())
                pe.transpose(bC[:, 0:P], wpad[:], ident[:]).then_inc(ev("w_turned"), 1)
                yield
                pe.wait_ge(ev("w_probs"), at.n()).then_inc(ev("pe_held"), 1)
                pe.transpose(bC[:, 0:TILES], wpr[:].rearrange("t b k -> t (b k)"), ident[0:TILES, 0:TILES]
                             ).then_inc(ev("p_turned"), 1)
                yield
                pe.wait_ge(ev("p_col"), at.n())
                for t in range(TILES):
                    m = project_tm(bC[:, t * D:(t + 1) * D], x1Fh[at.par], x1Fl[at.par], Wv1, t)
                m.then_inc(ev("v1"), 1)
                yield
                pe.wait_ge(ev("xC"), at.n())
                if at.earlier(1):
                    pe.wait_ge(ev("s_masked"), at.tile(1, -1))
                turn(bD0, x2).then_inc(ev("x2_turned"), 1)
                yield
                pe.wait_ge(ev("x2F_lo"), at.n())
                project_fm(bD1, Wq, x2Fh, x2Fl).then_inc(ev("q"), 1)
                yield

            def stream3(at):
                project_fm(bD0, Wk, x2Fh, x2Fl).then_inc(ev("k"), 1)
                yield
                pe.wait_ge(ev("q_lo"), at.n())
                for h2 in range(2):
                    for t in range(TILES):
                        m = project_tm(bD1[:, (h2 * TILES + t) * P:(h2 * TILES + t + 1) * P], x2Fh, x2Fl, Wv, t,
                                       n=P, n0=h2 * P)
                m.then_inc(ev("v"), 1)
                yield
                pe.wait_ge(ev(f"k_bd{at.par}"), at.dma(4))
                for t in range(TILES):
                    if t:
                        pe.wait_ge(ev("v_lo"), at.n())
                    o = (bD0, bD1)[t]
                    for c in range(2):
                        for i, (qq, hl) in enumerate(((qh, 0), (qh, 1), (ql, 0))):
                            for b in range(2):
                                tok = slice(t * P + 64 * b, t * P + 64 * b + 64)
                                m = pe.matmul(o[64 * b:64 * b + 64, c * 256:(c + 1) * 256], qq[:, c, tok],
                                              Kbd[:, :, hl, c, tok], start=(i == 0), stop=(i == 2),
                                              skip_group_check=True)
                    m.then_inc(ev("scores"), 1)
                    yield
                if at.earlier(1):
                    pe.wait_ge(ev("preF"), at.n(-1))
                for t in range(TILES):
                    pe.wait_ge(ev("exp"), at.tile(t))
                    o = (bF0, bF1)[t]
                    for hp in range(4):
                        m = pe.transpose(o[:, hp * P:(hp + 1) * P],
                                         E[:, t, 2 * hp:2 * hp + 2].rearrange("p h k -> p (h k)"), ident[:])
                    m.then_inc(ev("e_turned"), 1)
                    yield

            def stream4(at):
                pe.wait_ge(ev(f"v_bd{at.par}"), at.dma(4))
                for t in range(TILES):
                    pe.wait_ge(ev("pt_lo"), at.tile(t))
                    o = (bF0, bF1)[t]
                    for hp in range(4):
                        for i, (pt, hl) in enumerate(((PTh, 0), (PTh, 1), (PTl, 0))):
                            for b in range(2):
                                m = pe.matmul(o[64 * b:64 * b + 64, hp * 66:(hp + 1) * 66],
                                              pt[:, t, hp, 64 * b:64 * b + 64], Vbd[:, at.par, b, hl, :, 4 * t + hp],
                                              start=(i == 0), stop=(i == 2), skip_group_check=True)
                    m.then_inc(ev("ctx"), 1)
                    yield
                pe.wait_ge(ev("cx"), at.tile(1))
                turn(bF0, cx).then_inc(ev("cx_turned"), 1)
                yield
                pe.wait_ge(ev("cF_lo"), at.n())
                for t in range(TILES):
                    m = project_tm(bF1[:, t * D:(t + 1) * D], cFh, cFl, Wo, t)
                m.then_inc(ev("attn_out"), 1)
                yield
                pe.wait_ge(ev("xg"), at.n())
                if at.earlier(1):
                    pe.wait_ge(ev("mixed"), at.n(-1))
                turn(bG, xg).then_inc(ev("xg_turned"), 1)
                yield

            def stream5(at):
                pe.wait_ge(ev("xgF_lo"), at.n())
                project_fm(bG, Wqk3, xgFh, xgFl).then_inc(ev("qk3"), 1)
                yield
                pe.wait_ge(ev("qk_tanh"), at.n())
                for t in range(TILES):
                    m = project_tm(bG[:, t * D:(t + 1) * D], xgFh, xgFl, Wl, t)
                m.then_inc(ev("y3"), 1)
                yield
                pe.wait_ge(ev("y3_lo"), at.n())
                pe.wait_ge(ev("Q_lo"), at.n())
                for t in range(TILES):
                    tok = slice(t * P, (t + 1) * P)
                    for k in range(2):
                        m = mm3(bG[:, tok], Qh[:, k, tok], Ql[:, k, tok], Qh[:, k, tok], Ql[:, k, tok], k == 0, k == 1)
                m.then_inc(ev("s3"), 1)
                yield
                pe.wait_ge(ev("attn"), at.n())
                for t in range(TILES):
                    m = project_tm(bG[:, t * D:(t + 1) * D], xgFh, xgFl, Wr, t)
                m.then_inc(ev("o2_raw"), 1)
                yield
                pe.wait_ge(ev("o2"), at.n())
                pe.wait_ge(ev("attn_lo"), at.n())
                for t in range(TILES):
                    pe.matmul(bG[:, t:t + 1], SAh[:, t], ones16[:, 0:1], start=True, stop=False, skip_group_check=True)
                    m = pe.matmul(bG[:, t:t + 1], SAl[:, t], ones16[:, 0:1], start=False, stop=True,
                                  skip_group_check=True)
                m.then_inc(ev("row_sum"), 1)
                yield
                pe.wait_ge(ev("row_scale"), at.chain(2, 1))
                for t in range(TILES):
                    m = mm3(bG[:, t * D:(t + 1) * D], SAh[:, t], SAl[:, t], y3h[:, t], y3l[:, t], True, True)
                m.then_inc(ev("o1"), 1)
                yield

            run(pe, ORDER_PE, [stream0, stream1, stream2, stream3, stream4, stream5])

        @block.scalar
        def _(act):
            def cast(dst, src, scale=1.0):
                return act.activation(dst, src, ACT.Copy, scale=scale)

            for name, W in splits:
                if name == "Wqk1":
                    act.wait_ge(ev("setup_pe"), 3)
                elif name == "W2":
                    act.wait_ge(ev("w2_centred"), 1)
                else:
                    act.wait_ge(ev(arrival(name)[0]), arrival(name)[1])
                cast(W[:, 0], split_from[name], WS).then_inc(ev("w_hi"), 1)

            def norm(k, dst, at):
                act.wait_ge(ev("rstd" + k), at.chain(3, 3))
                for t in range(TILES):
                    m = act.activation(dst[:, t], pre[k][:, t], ACT.Identity, bias=nb[k][:, t:t + 1],
                                       scale=rs[k][:, t:t + 1])
                m.then_inc(ev("x" + k), 1)

            def stream0(at):
                act.wait_ge(ev(f"x_in{at.par}"), at.dma(1))
                if at.earlier(1):
                    act.wait_ge(ev("z1"), at.n(-1))
                cast(xh[:], xin[:, at.par]).then_inc(ev("x_hi"), 1)
                yield
                act.wait_ge(ev("d_inv"), at.chain(3, 3))
                for t in range(TILES):
                    m = act.activation(Pf[:, t], bA[:, t * P:(t + 1) * P], ACT.Copy, scale=Dinv[:, t:t + 1])
                m.then_inc(ev("p_f"), 1)
                yield
                act.wait_ge(ev("p_turned0"), at.n())
                cast(Ph[:, at.par].rearrange("p t k -> p (t k)"), bA[:, TOK:2 * TOK]).then_inc(ev("p_hi"), 1)
                yield
                act.wait_ge(ev("z1"), at.n())
                cast(z1h[:].rearrange("p c k -> p (c k)"), bA[:]).then_inc(ev("z1_hi"), 1)
                yield
                if at.earlier(1):
                    act.wait_ge(ev("y0_raw"), at.n(-1))
                def relu(i):
                    act.wait_ge(ev("z"), at.tile(i))
                    for c in range(2):
                        m = act.activation(r[:, 2 * i + c], (bA, bB)[i][:, c * TOK:(c + 1) * TOK], ACT.Relu,
                                           bias=b1c[:, 2 * i + c:2 * i + c + 1], scale=1.0 / WS)
                    m.then_inc(ev("relu"), 1)

                def parts(i):
                    act.wait_ge(ev("relu"), at.tile(i))
                    cast(rFh[:, 2 * i:2 * i + 2], r[:, 2 * i:2 * i + 2]).then_inc(ev("rF_hi"), 1)
                    yield
                    act.activation(rsq[:, 2 * i:2 * i + 2], r[:, 2 * i:2 * i + 2], ACT.Square
                                   ).then_inc(ev("r_squared"), 1)

                relu(0)
                yield
                relu(1)
                yield
                yield from parts(0)
                yield
                yield from parts(1)
                yield

            def stream1(at):
                act.wait_ge(ev("y0_f"), at.n())
                cast(y0h[:], y0[:]).then_inc(ev("y0_hi"), 1)
                yield
                norm("B", x1[:, at.par], at)
                yield
                act.wait_ge(ev("x1_turned"), at.n())
                cast(x1Fh[at.par][:].rearrange("p c k -> p (c k)"), bC[:]).then_inc(ev("x1F_hi"), 1)
                yield
                act.wait_ge(ev("u"), at.n())
                cast(uh[:].rearrange("p c k -> p (c k)"), bC[:], 1.0 / WS).then_inc(ev("u_hi"), 1)
                yield

            def stream2(at):
                act.wait_ge(ev("w_shifted"), at.n())
                act.activation(wex[:], wrm[:], ACT.Exp, scale=SOFT1).then_inc(ev("w_exp"), 1)
                yield
                if at.earlier(1):
                    act.wait_ge(ev("x2_biased"), at.n(-1))
                    act.wait_ge(ev("x2_turned"), at.n(-1))
                norm("C", x2, at)
                yield
                act.wait_ge(ev("x2_turned"), at.n())
                cast(x2Fh[:].rearrange("p c k -> p (c k)"), bD0[:]).then_inc(ev("x2F_hi"), 1)
                yield
                act.wait_ge(ev("q"), at.n())
                for c in range(2):
                    m = act.activation(qh[:, c], bD1[:, c * TOK:(c + 1) * TOK], ACT.Identity, bias=bqc[:, c:c + 1])
                m.then_inc(ev("q_hi"), 1)
                yield

            def stream3(at):
                act.wait_ge(ev("k"), at.n())
                if at.earlier(1):
                    act.wait_ge(ev(f"k_bd{1 - at.par}"), at.before().dma(4))
                for c in range(2):
                    m = act.activation(kst[:, 0, c], bD0[:, c * TOK:(c + 1) * TOK], ACT.Identity, bias=bkc[:, c:c + 1])
                m.then_inc(ev("k_hi"), 1)
                yield
                act.wait_ge(ev("v"), at.n())
                if at.earlier(1):
                    act.wait_ge(ev(f"v_bd{1 - at.par}"), at.before().dma(4))
                cast(vst[:, 0].rearrange("p h e d -> p (h e) d")[:, :, 0:HD],
                     bD1[:].rearrange("p (e d) -> p e d", d=HD), 1.0 / WS).then_inc(ev("v_hi"), 1)
                yield
                for t in range(TILES):
                    act.wait_ge(ev("s_shifted"), at.tile(t))
                    if at.earlier(1):
                        act.wait_ge(ev("e_turned"), at.tile(t, -1))
                    act.activation(E[:, t], Ssb[:, t], ACT.Exp, scale=SOFT2).then_inc(ev("exp"), 1)
                    if t == 0:
                        yield
                for t in range(TILES):
                    act.wait_ge(ev("e_turned"), at.tile(t))
                    cast(PTh[:, t].rearrange("p c k -> p (c k)"), (bF0, bF1)[t][:]).then_inc(ev("pt_hi"), 1)
                    yield

            def stream4(at):
                act.wait_ge(ev("deg"), at.n())
                for t in range(TILES):
                    m = act.activation(gw[:, t], wdb[:], ACT.Copy, scale=deg[:, t:t + 1])
                m.then_inc(ev("gate_scaled"), 1)
                yield
                act.wait_ge(ev("cx_turned"), at.n())
                cast(cFh[:].rearrange("p c k -> p (c k)"), bF0[:]).then_inc(ev("cF_hi"), 1)
                yield
                act.wait_ge(ev("gate_pre"), at.n())
                act.activation(gt[:], gp[:], ACT.Tanh, scale=0.5).then_inc(ev("gate_tanh"), 1)
                yield
                act.wait_ge(ev("gate_tanh"), at.n())
                act.activation(g2[:], gt[:], ACT.Copy, bias=1.0).then_inc(ev("gate"), 1)
                yield
                norm("F", x3[:, at.par], at)
                yield
                act.wait_ge(ev("xg_turned"), at.n())
                cast(xgFh[:].rearrange("p c k -> p (c k)"), bG[:], 0.5).then_inc(ev("xgF_hi"), 1)
                yield

            def stream5(at):
                act.wait_ge(ev("qk3"), at.n())
                for c in range(2):
                    m = act.activation(qt[:, c], bG[:, c * TOK:(c + 1) * TOK], ACT.Tanh, bias=bqkc[:, c:c + 1],
                                       scale=0.5 / WS)
                m.then_inc(ev("qk_tanh"), 1)
                yield
                act.wait_ge(ev("qk_tanh"), at.n())
                act.activation(Qh[:], qt[:], ACT.Copy, bias=1.0).then_inc(ev("Q_hi"), 1)
                yield
                act.wait_ge(ev("y3"), at.n())
                cast(y3h[:].rearrange("p t k -> p (t k)"), bG[:], 1.0 / WS).then_inc(ev("y3_hi"), 1)
                yield
                act.wait_ge(ev("attn"), at.n())
                cast(SAh[:].rearrange("p t k -> p (t k)"), SA[:]).then_inc(ev("attn_hi"), 1)
                yield
                act.wait_ge(ev("o2_raw"), at.n())
                if at.earlier(1):
                    act.wait_ge(ev("mixed"), at.n(-1))
                cast(o2[:].rearrange("p t k -> p (t k)"), bG[:], 1.0 / WS).then_inc(ev("o2"), 1)
                yield
                if at.earlier(2):
                    act.wait_ge(ev(f"stored{at.par}"), at.dma(1, -1))
                norm("G", x4[:, at.par], at)
                yield

            run(act, ORDER_ACT, [stream0, stream1, stream2, stream3, stream4, stream5])

        @block.vector
        def _(dve):
            def low(dst, src, hi, scale=1.0):
                return dve.scalar_tensor_tensor(out=dst, in0=src, scalar=scale, in1=hi, op0=ALU.mult,
                                                op1=ALU.subtract)

            def low_biased(dst, src, b, hi):
                for c in range(2):
                    m = dve.scalar_tensor_tensor(out=dst[:, c], in0=src[:, c * TOK:(c + 1) * TOK],
                                                 scalar=b[:, c:c + 1], in1=hi[:, c], op0=ALU.add, op1=ALU.subtract)
                return m

            dve.memset(ones16[:], 1.0).then_inc(ev("const"), 1)
            dve.memset(onesf[:], 1.0).then_inc(ev("const"), 1)
            for buf in (atA, aC, atG, wpad):
                dve.memset(buf[:], 0.0).then_inc(ev("const"), 1)
            dve.wait_ge(ev("const"), 6)
            dve.wait_ge(ev("ident"), 3).then_inc(ev("cleared"), 1)

            dve.wait_ge(ev("w2_in"), 16)
            dve.wait_ge(ev("small_in"), 16 * SMALL_INPUTS)
            dve.tensor_copy(w2_stage[:, :, D:2 * D], w2_stage[:, :, 0:D]).then_inc(ev("setup"), 1)
            dve.wait_ge(ev("setup"), 1)
            for k in range(4):
                m = dve.tensor_scalar(w2_stage[:, k, 0:D], w2_stage[:, k, D:2 * D], gam[:, k:k + 1], None, ALU.mult)
            m.then_inc(ev("w2_scaled"), 1)
            for k in range(4):
                m = dve.tensor_scalar(betb[:, k], onesf[:], bet[:, k:k + 1], None, ALU.mult)
            m.then_inc(ev("w2_scaled"), 1)
            for b, scale in ((bqc, WS), (bkc, WS), (bqkc, 0.5), (b2b, 0.5)):
                dve.tensor_scalar(b[:], b[:], scale, None, ALU.mult)

            for i, (name, W) in enumerate(splits):
                if name == "Wqk1":
                    dve.wait_ge(ev("setup_pe"), 2)
                    dve.wait_ge(ev("w2_scaled"), 1)
                    for k in range(4):
                        m = dve.scalar_tensor_tensor(out=w2_stage[:, k, 0:D], in0=bA[:, 0:D], scalar=-1.0 / H1,
                                                     in1=w2_stage[:, k, 0:D], op0=ALU.mult, op1=ALU.add)
                    m.then_inc(ev("w2_centred"), 1)
                    dve.tensor_copy(c2[:], bB[:, 0:D])
                if name == "Wo":
                    dve.wait_ge(ev("setup_pe"), 4)
                    dve.tensor_tensor(bob[:], bob[:], bD0[:, 0:D], ALU.add)
                dve.wait_ge(ev("w_hi"), i + 1)
                low(W[:, 1], split_from[name], W[:, 0], WS).then_inc(ev("unstaged"), 1)
            dve.wait_ge(ev("ident"), 7)

            def stats(k, at):
                dve.wait_ge(ev("pre" + k), at.n())
                for t in range(TILES):
                    m = dve.bn_stats(st[k][:, t], pre[k][:, t])
                m.then_inc(ev("var" + k), 1)
                yield
                dve.wait_ge(ev("var" + k), at.chain(2, 1)).then_inc(ev("dve_held"), 1)
                for t in range(TILES):
                    m = dve.bn_aggr(mv[k][:, t], st[k][:, t])
                m.then_inc(ev("var" + k), 1)

            def stream0(at):
                dve.wait_ge(ev(f"at_in{at.par}"), at.dma(2))
                dve.tensor_scalar(HT[:], atA[:, at.par], 0.0, None, ALU.not_equal).then_inc(ev("h_t"), 1)
                yield
                dve.wait_ge(ev("h_t"), at.n())
                dve.tensor_reduce(cnt[:], HT[:], AX.X, ALU.add).then_inc(ev("b_chain"), 1)
                yield
                dve.wait_ge(ev("b_chain"), at.chain(4, 1))
                dve.tensor_scalar(cnt1[:], cnt[:], 1.0, None, ALU.max).then_inc(ev("b_chain"), 1)
                yield
                dve.wait_ge(ev("b_chain"), at.chain(4, 2))
                dve.reciprocal(be[:], cnt1[:]).then_inc(ev("b_chain"), 1)
                yield
                dve.wait_ge(ev("b_chain"), at.chain(4, 3))
                for t in range(TILES):
                    m = dve.tensor_scalar(HBh[:, t], HT[:, t], be[:, t:t + 1], None, ALU.mult)
                m.then_inc(ev("b_chain"), 1)
                yield
                dve.wait_ge(ev("b_chain"), at.chain(4, 4))
                for t in range(TILES):
                    m = low(HBl[:, t], HT[:, t], HBh[:, t], be[:, t:t + 1])
                m.then_inc(ev("hb_lo"), 1)
                yield
                dcol = bA[:, TOK:TOK + TILES]
                dve.wait_ge(ev("m_and_d"), at.n())
                dve.tensor_scalar(Dbg[:], dcol, 0.0, HUGE, ALU.is_le, ALU.mult).then_inc(ev("d_inv"), 1)
                yield
                dve.wait_ge(ev("d_inv"), at.chain(3, 1))
                dve.tensor_tensor(Dd[:], dcol, Dbg[:], ALU.max).then_inc(ev("d_inv"), 1)
                yield
                dve.wait_ge(ev("d_inv"), at.chain(3, 2))
                dve.reciprocal(Dinv[:], Dd[:]).then_inc(ev("d_inv"), 1)
                yield
                dve.wait_ge(ev("p_hi"), at.n())
                low(Pl[:, at.par].rearrange("p t k -> p (t k)"), bA[:, TOK:2 * TOK],
                    Ph[:, at.par].rearrange("p t k -> p (t k)")).then_inc(ev("p_lo"), 1)
                yield
                dve.wait_ge(ev("z1_hi"), at.n())
                low(z1l[:].rearrange("p c k -> p (c k)"), bA[:], z1h[:].rearrange("p c k -> p (c k)")
                    ).then_inc(ev("z1_lo"), 1)
                yield
                dve.wait_ge(ev("rF_hi"), at.tile(1))
                dve.tensor_tensor(rFl[:, 2:4], r[:, 2:4], rFh[:, 2:4], ALU.subtract).then_inc(ev("rF_lo1"), 1)
                yield
                dve.wait_ge(ev("r_sums"), at.n())
                dve.tensor_scalar(rmean[:], bA[:, 0:TILES], 1.0 / H1, None, ALU.mult).then_inc(ev("r_mean"), 1)
                yield
                dve.wait_ge(ev("r_mean"), at.chain(3, 1))
                dve.tensor_tensor(rmm[:], rmean[:], rmean[:], ALU.mult).then_inc(ev("r_mean"), 1)
                yield
                dve.wait_ge(ev("r_mean"), at.chain(3, 2))
                dve.scalar_tensor_tensor(out=rvar[:], in0=bA[:, TILES:2 * TILES], scalar=1.0 / H1, in1=rmm[:],
                                         op0=ALU.mult, op1=ALU.subtract).then_inc(ev("r_mean"), 1)
                yield

            def stream1(at):
                dve.wait_ge(ev("y0_raw"), at.n())
                dve.wait_ge(ev("r_rstd"), at.chain(3, 3))
                for t in range(TILES):
                    m = dve.scalar_tensor_tensor(out=y0[:, t], in0=bB[:, t * D:(t + 1) * D], scalar=rsc[:, t:t + 1],
                                                 in1=c2[:], op0=ALU.mult, op1=ALU.add)
                m.then_inc(ev("y0_f"), 1)
                yield
                dve.wait_ge(ev("conv2"), at.n())
                dve.wait_ge(ev("res_biased"), at.n())
                dve.scalar_tensor_tensor(out=pre["B"][:].rearrange("p t k -> p (t k)"),
                                         in0=xres[:, at.par].rearrange("p t k -> p (t k)"), scalar=2.0, in1=bB[:],
                                         op0=ALU.mult, op1=ALU.add).then_inc(ev("preB"), 1)
                yield
                yield from stats("B", at)
                yield
                dve.wait_ge(ev("x1F_hi"), at.n())
                low(x1Fl[at.par][:].rearrange("p c k -> p (c k)"), bC[:],
                    x1Fh[at.par][:].rearrange("p c k -> p (c k)")).then_inc(ev("x1F_lo"), 1)
                yield
                dve.wait_ge(ev("u_hi"), at.n())
                low(ul[:].rearrange("p c k -> p (c k)"), bC[:], uh[:].rearrange("p c k -> p (c k)"), 1.0 / WS
                    ).then_inc(ev("u_lo"), 1)
                yield
                dve.wait_ge(ev("uxT"), at.n())
                dve.wait_ge(ev("adj_masked"), at.n())
                for t in range(TILES):
                    tok = slice(t * P, (t + 1) * P)
                    m = dve.tensor_tensor_reduce(wscr[:, tok], bC[:, tok], am[:, tok], 1.0, 0.0, ALU.mult, ALU.add,
                                                 wraw[:, t:t + 1])
                m.then_inc(ev("w_raw"), 1)
                yield
                dve.wait_ge(ev("w_raw"), at.n())
                dve.wait_ge(ev(f"C_in{at.par}"), at.dma(4))
                dve.tensor_tensor(wpad[:, 0:TILES], wraw[:], mcol[:, at.par], ALU.mult).then_inc(ev("w_masked"), 1)
                yield

            def stream2(at):
                wv = bC[0:TILES, 0:P].rearrange("t (b k) -> t b k", b=2)
                dve.wait_ge(ev("w_turned"), at.n())
                dve.tensor_reduce(wmx[:], wv, AX.X, ALU.max).then_inc(ev("c_softmax"), 1)
                yield
                dve.wait_ge(ev("c_softmax"), at.chain(3, 1))
                dve.tensor_tensor(wrm[:], wv, wmx[:].rearrange("t (b o) -> t b o", o=1).broadcast_to(
                    [TILES, 2, NODES]), ALU.subtract).then_inc(ev("w_shifted"), 1)
                yield
                dve.wait_ge(ev("w_exp"), at.n())
                dve.tensor_reduce(wsm[:], wex[:], AX.X, ALU.add).then_inc(ev("c_softmax"), 1)
                yield
                dve.wait_ge(ev("c_softmax"), at.chain(3, 2))
                dve.reciprocal(wrc[:], wsm[:]).then_inc(ev("c_softmax"), 1)
                yield
                dve.wait_ge(ev("c_softmax"), at.chain(3, 3))
                dve.tensor_tensor(wpr[:], wex[:], wrc[:].rearrange("t (b o) -> t b o", o=1).broadcast_to(
                    [TILES, 2, NODES]), ALU.mult).then_inc(ev("w_probs"), 1)
                yield
                dve.wait_ge(ev("p_turned"), at.n())
                dve.tensor_scalar(pcol[:], bC[:, 0:TILES], 1.0 / WS, None, ALU.mult).then_inc(ev("p_col"), 1)
                yield
                dve.wait_ge(ev("v1"), at.n())
                dve.wait_ge(ev("p_col"), at.n())
                for t in range(TILES):
                    m = dve.scalar_tensor_tensor(out=pre["C"][:, t], in0=bC[:, t * D:(t + 1) * D],
                                                 scalar=pcol[:, t:t + 1], in1=x1[:, at.par, t], op0=ALU.mult,
                                                 op1=ALU.add)
                m.then_inc(ev("preC"), 1)
                yield
                yield from stats("C", at)
                yield
                dve.wait_ge(ev("x2F_hi"), at.n())
                low(x2Fl[:].rearrange("p c k -> p (c k)"), bD0[:], x2Fh[:].rearrange("p c k -> p (c k)")
                    ).then_inc(ev("x2F_lo"), 1)
                yield
                dve.wait_ge(ev("q_hi"), at.n())
                low_biased(ql, bD1, bqc, qh).then_inc(ev("q_lo"), 1)
                yield

            def stream3(at):
                dve.wait_ge(ev("k_hi"), at.n())
                low_biased(kst[:, 1], bD0, bkc, kst[:, 0]).then_inc(ev("k_lo"), 1)
                yield
                dve.wait_ge(ev("v_hi"), at.n())
                low(vst[:, 1].rearrange("p h e d -> p (h e) d")[:, :, 0:HD],
                    bD1[:].rearrange("p (e d) -> p e d", d=HD),
                    vst[:, 0].rearrange("p h e d -> p (h e) d")[:, :, 0:HD], 1.0 / WS).then_inc(ev("v_lo"), 1)
                yield
                dve.wait_ge(ev(f"acD_in{at.par}"), at.dma(1))
                for t in range(TILES):
                    dve.wait_ge(ev("scores"), at.tile(t))
                    dve.tensor_tensor(Sm[:, t], (bD0, bD1)[t][:].rearrange("p (h k) -> p h k", h=HEADS),
                                      acD[:, at.par, t:t + 1].broadcast_to([P, HEADS, NODES]), ALU.mult
                                      ).then_inc(ev("s_masked"), 1)
                    yield
                    dve.wait_ge(ev("s_masked"), at.tile(t))
                    dve.tensor_reduce(Smx[:, t], Sm[:, t], AX.X, ALU.max).then_inc(ev("s_max"), 1)
                    yield
                for t in range(TILES):
                    dve.wait_ge(ev("pt_hi"), at.tile(t))
                    low(PTl[:, t].rearrange("p c k -> p (c k)"), (bF0, bF1)[t][:],
                        PTh[:, t].rearrange("p c k -> p (c k)")).then_inc(ev("pt_lo"), 1)
                    yield

            def stream4(at):
                dve.wait_ge(ev(f"acG_in{at.par}"), at.dma(1))
                dve.tensor_reduce(deg[:], acG[:, at.par], AX.X, ALU.add).then_inc(ev("deg"), 1)
                yield
                for t in range(TILES):
                    c = (bF0, bF1)[t][:, 0:HEADS * (HD + 1)].rearrange("p (h d) -> p h d", h=HEADS)
                    dve.wait_ge(ev("ctx"), at.tile(t))
                    dve.reciprocal(rinv[:, t:t + 1].rearrange("p t h -> p h t"), c[:, :, HD:HD + 1]
                                   ).then_inc(ev("rinv"), 1)
                    yield
                    dve.wait_ge(ev("rinv"), at.tile(t))
                    dve.tensor_tensor(cx[:, t].rearrange("p (h d) -> p h d", h=HEADS), c[:, :, 0:HD],
                                      rinv[:, t:t + 1].rearrange("p t h -> p h t").broadcast_to([P, HEADS, HD]),
                                      ALU.mult).then_inc(ev("cx"), 1)
                    yield
                dve.wait_ge(ev("cF_hi"), at.n())
                low(cFl[:].rearrange("p c k -> p (c k)"), bF0[:], cFh[:].rearrange("p c k -> p (c k)")
                    ).then_inc(ev("cF_lo"), 1)
                yield
                dve.wait_ge(ev("attn_out"), at.n())
                dve.scalar_tensor_tensor(out=pre["F"][:].rearrange("p t k -> p (t k)"), in0=bF1[:], scalar=1.0 / WS,
                                         in1=x2b[:, at.par].rearrange("p t k -> p (t k)"), op0=ALU.mult, op1=ALU.add
                                         ).then_inc(ev("preF"), 1)
                yield
                yield from stats("F", at)
                yield
                dve.wait_ge(ev("xgF_hi"), at.n())
                low(xgFl[:].rearrange("p c k -> p (c k)"), bG[:], xgFh[:].rearrange("p c k -> p (c k)"), 0.5
                    ).then_inc(ev("xgF_lo"), 1)
                yield

            def stream5(at):
                dve.wait_ge(ev("Q_hi"), at.n())
                dve.scalar_tensor_tensor(out=Ql[:], in0=qt[:], scalar=1.0, in1=Qh[:], op0=ALU.add, op1=ALU.subtract
                                         ).then_inc(ev("Q_lo"), 1)
                yield
                dve.wait_ge(ev("y3_hi"), at.n())
                low(y3l[:].rearrange("p t k -> p (t k)"), bG[:], y3h[:].rearrange("p t k -> p (t k)"), 1.0 / WS
                    ).then_inc(ev("y3_lo"), 1)
                yield
                dve.wait_ge(ev("s3"), at.n())
                dve.wait_ge(ev(f"atG_in{at.par}"), at.dma(2))
                dve.scalar_tensor_tensor(out=SA[:], in0=bG[:, 0:TOK], scalar=QK3,
                                         in1=atG[:, at.par].rearrange("p t k -> p (t k)"), op0=ALU.mult, op1=ALU.mult
                                         ).then_inc(ev("attn"), 1)
                yield
                dve.wait_ge(ev("row_sum"), at.n())
                dve.tensor_scalar(ssum[:], bG[:, 0:TILES], 1e-6, None, ALU.add).then_inc(ev("row_scale"), 1)
                yield
                dve.wait_ge(ev("row_scale"), at.chain(2, 1))
                dve.reciprocal(srec[:], ssum[:]).then_inc(ev("row_scale"), 1)
                yield
                dve.wait_ge(ev("o1"), at.n())
                dve.wait_ge(ev("o2_biased"), at.n())
                dve.wait_ge(ev("row_scale"), at.chain(2, 2))
                for t in range(TILES):
                    m = dve.scalar_tensor_tensor(out=o3[:, t], in0=bG[:, t * D:(t + 1) * D], scalar=srec[:, t:t + 1],
                                                 in1=o2[:, t], op0=ALU.mult, op1=ALU.add)
                m.then_inc(ev("mixed"), 1)
                yield
                dve.wait_ge(ev("mixed"), at.n())
                dve.scalar_tensor_tensor(out=pre["G"][:].rearrange("p t k -> p (t k)"),
                                         in0=o3[:].rearrange("p t k -> p (t k)"), scalar=0.0,
                                         in1=x3[:, at.par].rearrange("p t k -> p (t k)"), op0=ALU.max, op1=ALU.add
                                         ).then_inc(ev("preG"), 1)
                yield
                yield from stats("G", at)
                yield

            run(dve, ORDER_DVE, [stream0, stream1, stream2, stream3, stream4, stream5])

        @block.gpsimd
        def _(pool):
            pool.memset(powm[:], -0.5).then_inc(ev("ident"), 1)
            pool.memset(ident[:], 0.0).then_inc(ev("ident"), 1)
            pool.wait_ge(ev("ident"), 2)
            pool.affine_select(out=ident[:], in_=ident[:], compare_op=ALU.not_equal, fill=1.0, base=0,
                               pattern=[[-1, P]], channel_multiplier=1).then_inc(ev("ident"), 1)
            pool.wait_ge(ev("ident"), 3)
            for part, value in ((Kbd[:], 0.0), (Vbd[:], 0.0), (vst[:, 1], 0.0), (vst[:, 0], 1.0)):
                pool.memset(part, value).then_inc(ev("ident"), 1)
            pool.wait_ge(ev("unstaged"), len(weights_in))

            def sub(dst, a, b):
                return pool.tensor_tensor(dst, a, b, ALU.subtract)

            def rstd(k, at):
                pool.wait_ge(ev("var" + k), at.chain(2, 2)).then_inc(ev("pool_held"), 1)
                pool.tensor_scalar(ve[k][:], mv[k][:, :, 1], EPS, None, ALU.add).then_inc(ev("rstd" + k), 1)
                yield
                pool.wait_ge(ev("rstd" + k), at.chain(3, 1))
                pool.tensor_tensor(rs[k][:], ve[k][:], powm[:], ALU.pow).then_inc(ev("rstd" + k), 1)
                yield
                pool.wait_ge(ev("rstd" + k), at.chain(3, 2)).then_inc(ev("pool_held"), 1)
                for t in range(TILES):
                    m = pool.tensor_scalar(nb[k][:, t:t + 1], mv[k][:, t, 0:1], rs[k][:, t:t + 1], -1.0, ALU.mult,
                                           ALU.mult)
                m.then_inc(ev("rstd" + k), 1)

            def bias_tm(dst, src, b):
                return pool.tensor_tensor(dst, src, b[:].rearrange("p (o d) -> p o d", o=1).broadcast_to(
                    [P, TILES, D]), ALU.add)

            def stream0(at):
                pool.wait_ge(ev(f"at_in{at.par}"), at.dma(2))
                if at.earlier(1):
                    pool.wait_ge(ev("m_and_d"), at.n(-1))
                pool.tensor_tensor(wcf[:], atA[:, at.par, :, 0], atA[:, at.par, :, 64], ALU.add
                                   ).then_inc(ev("w_lo"), 1)
                yield
                pool.wait_ge(ev("w_lo"), at.chain(3, 1)).then_inc(ev("pool_held"), 1)
                pool.tensor_copy(wch[:], wcf[:]).then_inc(ev("w_lo"), 1)
                yield
                pool.wait_ge(ev("w_lo"), at.chain(3, 2))
                sub(wcl[:], wcf[:], wch[:]).then_inc(ev("w_lo"), 1)
                yield
                pool.wait_ge(ev("x_hi"), at.n())
                sub(xl[:], xin[:, at.par], xh[:]).then_inc(ev("x_lo"), 1)
                yield
                pool.wait_ge(ev("rF_hi"), at.tile(0))
                sub(rFl[:, 0:2], r[:, 0:2], rFh[:, 0:2]).then_inc(ev("rF_lo0"), 1)
                yield
                pool.wait_ge(ev("r_squared"), at.tile(1))
                pool.tensor_tensor(rsq[:, 0:2], rsq[:, 0:2], rsq[:, 2:4], ALU.add).then_inc(ev("sq_sum"), 1)
                yield
                pool.wait_ge(ev("sq_sum"), at.tile(0))
                pool.tensor_tensor(rsq[:, 0], rsq[:, 0], rsq[:, 1], ALU.add).then_inc(ev("sq_sum"), 1)
                yield
                pool.wait_ge(ev("r_mean"), at.chain(3, 3)).then_inc(ev("pool_held"), 1)
                pool.tensor_scalar(rve[:], rvar[:], EPS, None, ALU.add).then_inc(ev("r_rstd"), 1)
                yield
                pool.wait_ge(ev("r_rstd"), at.chain(3, 1))
                pool.tensor_tensor(rrs[:], rve[:], powm[:], ALU.pow).then_inc(ev("r_rstd"), 1)
                yield
                pool.wait_ge(ev("r_rstd"), at.chain(3, 2)).then_inc(ev("pool_held"), 1)
                pool.tensor_scalar(rsc[:], rrs[:], 1.0 / WS, None, ALU.mult).then_inc(ev("r_rstd"), 1)
                yield

            def stream1(at):
                pool.wait_ge(ev(f"xres_in{at.par}"), at.dma(1))
                bias_tm(xres[:, at.par], xres[:, at.par], b2b).then_inc(ev("res_biased"), 1)
                yield
                pool.wait_ge(ev("y0_hi"), at.n())
                sub(y0l[:], y0[:], y0h[:]).then_inc(ev("y0_lo"), 1)
                yield
                yield from rstd("B", at)
                yield
                pool.wait_ge(ev(f"C_in{at.par}"), at.dma(4))
                if at.earlier(1):
                    pool.wait_ge(ev("w_raw"), at.n(-1))
                pool.tensor_tensor(am[:], aC[:, at.par].rearrange("p t k -> p (t k)"), mrow[:, at.par], ALU.mult
                                   ).then_inc(ev("adj_masked"), 1)
                yield

            def stream2(at):
                yield from rstd("C", at)
                yield

            def stream3(at):
                if at.earlier(2):
                    pool.wait_ge(ev("preF"), at.n(-2))
                pool.wait_ge(ev("xC"), at.n())
                bias_tm(x2b[:, at.par], x2[:], bob).then_inc(ev("x2_biased"), 1)
                yield
                for t in range(TILES):
                    pool.wait_ge(ev("s_max"), at.tile(t))
                    if at.earlier(1):
                        pool.wait_ge(ev("exp"), at.tile(t, -1))
                    pool.tensor_tensor(Ssb[:, t], Sm[:, t], Smx[:, t:t + 1].rearrange("p t h -> p h t").broadcast_to(
                        [P, HEADS, NODES]), ALU.subtract).then_inc(ev("s_shifted"), 1)
                    yield

            def stream4(at):
                pool.wait_ge(ev("gate_scaled"), at.n())
                bias_tm(gp[:], gw[:], bdb).then_inc(ev("gate_pre"), 1)
                yield
                yield from rstd("F", at)
                yield
                pool.wait_ge(ev("xF"), at.n())
                pool.tensor_tensor(xg[:], g2[:], x3[:, at.par], ALU.mult).then_inc(ev("xg"), 1)
                yield

            def stream5(at):
                pool.wait_ge(ev("attn_hi"), at.n())
                sub(SAl[:].rearrange("p t k -> p (t k)"), SA[:], SAh[:].rearrange("p t k -> p (t k)")
                    ).then_inc(ev("attn_lo"), 1)
                yield
                pool.wait_ge(ev("o2"), at.n())
                bias_tm(o2[:], o2[:], blb).then_inc(ev("o2_biased"), 1)
                yield
                yield from rstd("G", at)
                yield

            run(pool, ORDER_POOL, [stream0, stream1, stream2, stream3, stream4, stream5])


def kernel(**inputs):
    import numpy as np
    import concourse.bacc as bacc
    from concourse.bass_utils import run_bass_kernel_spmd

    a = {k: np.ascontiguousarray(v) for k, v in inputs.items()}

    def turned(w):
        return np.ascontiguousarray(w.T)

    def column(b):
        return turned(b.reshape(-1, P))

    even_odd = np.arange(D).reshape(4, 2, HD).transpose(1, 0, 2).reshape(-1)
    arrays = {
        "x": a["x"].reshape(GRAPHS * NODES, D), "adj": a["adj"],
        "adj_t": np.ascontiguousarray(a["adj"].transpose(0, 2, 1)), "mask": a["nodemask"].reshape(-1),
        "mask_col": np.ascontiguousarray(a["nodemask"].reshape(GROUPS, TILES, P).transpose(0, 2, 1)),
        "w1t": turned(a["L0_gnn_W1"]), "b1": column(a["L0_gnn_b1"]), "gamma": column(a["L0_gnn_gamma"]),
        "beta": column(a["L0_gnn_beta"]),
        "w2t": turned(a["L0_gnn_W2"]), "b2": a["L0_gnn_b2"],
        "wqk1t": turned(a["L1_gnn_Wqk"]), "wv1": a["L1_gnn_Wv"],
        "wqt": turned(a["L2_gnn_Wq"]), "bq": column(a["L2_gnn_bq"]), "wkt": turned(a["L2_gnn_Wk"]), "bk": column(a["L2_gnn_bk"]),
        "wvt": np.ascontiguousarray(turned(a["L2_gnn_Wv"])[:, even_odd]),
        "bv": column(a["L2_gnn_bv"]),
        "wot": turned(a["L2_gnn_Wo"]), "bo": a["L2_gnn_bo"],
        "wqk3t": turned(a["L3_gnn_Wqk"]), "bqk": column(a["L3_gnn_bqk"]), "wlt": turned(a["L3_gnn_Wl"]), "bl": a["L3_gnn_bl"],
        "wrt": turned(a["L3_gnn_Wr"]), "wd": a["L3_gnn_Wd"].reshape(-1), "bd": a["L3_gnn_bd"],
    }
    nc = bacc.Bacc("TRN2", target_bir_lowering=False, num_devices=1)
    args = [nc.dram_tensor(n, v.shape, mybir.dt.from_np(v.dtype), kind="ExternalInput").ap()
            for n, v in arrays.items()]
    args.append(nc.dram_tensor("out", (GRAPHS * NODES, D), F32, kind="ExternalOutput").ap())
    build(nc, *args)
    res = run_bass_kernel_spmd(nc, [arrays], core_ids=[0])
    return res.results[0]["out"].reshape(GRAPHS, NODES, D)
```
